# Optimizing a Trainium2 kernel written in Bass

```python
import numpy as np
import jax
import jax.numpy as jnp

def _softmax(x, axis=-1):
    return jax.nn.softmax(x, axis=axis)

def _gelu(x):
    return jax.nn.gelu(x, approximate=True)

def _silu(x):
    return jax.nn.silu(x)

def _sigmoid(x):
    return jax.nn.sigmoid(x)

def _layernorm(x, axis=-1, eps=1e-05):
    m = jnp.mean(x, axis=axis, keepdims=True)
    v = jnp.var(x, axis=axis, keepdims=True)
    return (x - m) / jnp.sqrt(v + eps)

def _scatter_add(tgt, idx, src, axis=0):
    return tgt.at[idx].add(src)

def _segment_sum(src, seg, n):
    return jax.ops.segment_sum(src, seg, n)
kernel_name = 'mk_macaron_d1_jaxref_r8_c119d0'

def setup_inputs(seed: int=0):
    np.random.seed(seed)
    _w = jnp.asarray

    def _L0_attn_setup():
        import jax, jax.numpy as jnp
        import numpy as np
        import math
        B, S, HID = (2, 256, 256)
        NH = 16
        QK_NOPE, QK_ROPE, KV_RANK, Q_RANK, V_DIM = (64, 64, 64, 64, 64)
        Q_HEAD = QK_NOPE + QK_ROPE
        ROPE_BASE = 10000.0
        FACTOR = 40.0
        BETA_FAST, BETA_SLOW = (32.0, 1.0)
        ORIG_MAX = 512
        MSCALE = 0.707
        SOFTMAX_SCALE = Q_HEAD ** (-0.5)

        def yarn_get_mscale(scale, mscale=1.0):
            if scale <= 1:
                return 1.0
            return 0.1 * mscale * math.log(scale) + 1.0

        def yarn_cos_sin(seq_len, dim):
            exponents = np.arange(0, dim, 2, dtype=np.float64) / dim
            freq_extra = 1.0 / ROPE_BASE ** exponents
            freq_inter = 1.0 / (FACTOR * ROPE_BASE ** exponents)

            def corr_dim(num_rot):
                return dim * math.log(ORIG_MAX / (num_rot * 2 * math.pi)) / (2 * math.log(ROPE_BASE))
            low = max(math.floor(corr_dim(BETA_FAST)), 0)
            high = min(math.ceil(corr_dim(BETA_SLOW)), dim - 1)
            if low == high:
                high = high + 0.001
            ramp = np.clip((np.arange(dim // 2, dtype=np.float64) - low) / (high - low), 0.0, 1.0)
            inv_freq_mask = 1.0 - ramp
            inv_freq = freq_inter * (1.0 - inv_freq_mask) + freq_extra * inv_freq_mask
            t = np.arange(seq_len, dtype=np.float64)
            freqs = np.outer(t, inv_freq)
            msc = yarn_get_mscale(FACTOR, MSCALE) / yarn_get_mscale(FACTOR, 0.0)
            emb = np.concatenate([freqs, freqs], axis=-1)
            return (jnp.asarray(np.cos(emb) * msc, jnp.float32), jnp.asarray(np.sin(emb) * msc, jnp.float32))

        def rms_norm(x, w, eps=1e-06):
            xf = x.astype(jnp.float32)
            var = jnp.mean(xf * xf, axis=-1, keepdims=True)
            return (xf * jax.lax.rsqrt(var + eps)).astype(x.dtype) * w

        def rotate_half(x):
            x1, x2 = jnp.split(x, 2, axis=-1)
            return jnp.concatenate([-x2, x1], axis=-1)

        def apply_rope(x, cos, sin):
            b, h, s, d = x.shape
            x = x.reshape(b, h, s, d // 2, 2).transpose(0, 1, 2, 4, 3).reshape(b, h, s, d)
            return x * cos + rotate_half(x) * sin
        key = jax.random.key(seed)
        ks = jax.random.split(key, 8)
        sc = 0.02
        return {'hidden_states': jax.random.normal(ks[0], (B, S, HID), jnp.float32), 'wq_a': jax.random.normal(ks[1], (HID, Q_RANK), jnp.float32) * sc, 'q_a_norm_w': jnp.ones((Q_RANK,), jnp.float32), 'wq_b': jax.random.normal(ks[2], (Q_RANK, NH * Q_HEAD), jnp.float32) * sc, 'wkv_a': jax.random.normal(ks[3], (HID, KV_RANK + QK_ROPE), jnp.float32) * sc, 'kv_a_norm_w': jnp.ones((KV_RANK,), jnp.float32), 'wkv_b': jax.random.normal(ks[4], (KV_RANK, NH * (QK_NOPE + V_DIM)), jnp.float32) * sc, 'wo': jax.random.normal(ks[5], (NH * V_DIM, HID), jnp.float32) * sc}
    _L0_attn_in = _L0_attn_setup()

    def _L0_ffn_setup():
        import jax, jax.numpy as jnp
        import numpy as np
        NUM_EXPERTS = 8
        TOP_K = 2
        EMB = 256
        MLP = 512
        B, S = (4, 128)
        key = jax.random.key(seed)
        ks = jax.random.split(key, 5)
        scale_x = 1.0
        return {'x': jax.random.normal(ks[0], (B, S, EMB), dtype=jnp.float32), 'gate_kernel': jax.random.normal(ks[1], (EMB, NUM_EXPERTS), dtype=jnp.float32) / np.sqrt(EMB), 'w0_kernel': jax.random.normal(ks[2], (NUM_EXPERTS, EMB, MLP), dtype=jnp.float32) / np.sqrt(EMB), 'w1_kernel': jax.random.normal(ks[3], (NUM_EXPERTS, EMB, MLP), dtype=jnp.float32) / np.sqrt(EMB), 'wo_kernel': jax.random.normal(ks[4], (NUM_EXPERTS, MLP, EMB), dtype=jnp.float32) / np.sqrt(MLP)}
    _L0_ffn_in = _L0_ffn_setup()
    _d = {'L0_attn_hidden_states': _L0_attn_in['hidden_states'], 'L0_attn_wq_a': _L0_attn_in['wq_a'], 'L0_attn_q_a_norm_w': _L0_attn_in['q_a_norm_w'], 'L0_attn_wq_b': _L0_attn_in['wq_b'], 'L0_attn_wkv_a': _L0_attn_in['wkv_a'], 'L0_attn_kv_a_norm_w': _L0_attn_in['kv_a_norm_w'], 'L0_attn_wkv_b': _L0_attn_in['wkv_b'], 'L0_attn_wo': _L0_attn_in['wo'], 'L0_ffn_gate_kernel': _L0_ffn_in['gate_kernel'], 'L0_ffn_w0_kernel': _L0_ffn_in['w0_kernel'], 'L0_ffn_w1_kernel': _L0_ffn_in['w1_kernel'], 'L0_ffn_wo_kernel': _L0_ffn_in['wo_kernel']}
    _x0 = _d['L0_attn_hidden_states']
    _d['L0_attn_hidden_states'] = jax.random.normal(jax.random.fold_in(jax.random.key(seed), 1), (4, 512, 256), dtype=_x0.dtype)
    del _x0
    return _d

def reference(L0_attn_hidden_states, L0_attn_wq_a, L0_attn_q_a_norm_w, L0_attn_wq_b, L0_attn_wkv_a, L0_attn_kv_a_norm_w, L0_attn_wkv_b, L0_attn_wo, L0_ffn_gate_kernel, L0_ffn_w0_kernel, L0_ffn_w1_kernel, L0_ffn_wo_kernel):

    def _L0_attn_ref(hidden_states, wq_a, q_a_norm_w, wq_b, wkv_a, kv_a_norm_w, wkv_b, wo):
        import jax, jax.numpy as jnp
        import numpy as np
        import math
        B, S, HID = (2, 256, 256)
        NH = 16
        QK_NOPE, QK_ROPE, KV_RANK, Q_RANK, V_DIM = (64, 64, 64, 64, 64)
        Q_HEAD = QK_NOPE + QK_ROPE
        ROPE_BASE = 10000.0
        FACTOR = 40.0
        BETA_FAST, BETA_SLOW = (32.0, 1.0)
        ORIG_MAX = 512
        MSCALE = 0.707
        SOFTMAX_SCALE = Q_HEAD ** (-0.5)

        def yarn_get_mscale(scale, mscale=1.0):
            if scale <= 1:
                return 1.0
            return 0.1 * mscale * math.log(scale) + 1.0

        def yarn_cos_sin(seq_len, dim):
            exponents = np.arange(0, dim, 2, dtype=np.float64) / dim
            freq_extra = 1.0 / ROPE_BASE ** exponents
            freq_inter = 1.0 / (FACTOR * ROPE_BASE ** exponents)

            def corr_dim(num_rot):
                return dim * math.log(ORIG_MAX / (num_rot * 2 * math.pi)) / (2 * math.log(ROPE_BASE))
            low = max(math.floor(corr_dim(BETA_FAST)), 0)
            high = min(math.ceil(corr_dim(BETA_SLOW)), dim - 1)
            if low == high:
                high = high + 0.001
            ramp = np.clip((np.arange(dim // 2, dtype=np.float64) - low) / (high - low), 0.0, 1.0)
            inv_freq_mask = 1.0 - ramp
            inv_freq = freq_inter * (1.0 - inv_freq_mask) + freq_extra * inv_freq_mask
            t = np.arange(seq_len, dtype=np.float64)
            freqs = np.outer(t, inv_freq)
            msc = yarn_get_mscale(FACTOR, MSCALE) / yarn_get_mscale(FACTOR, 0.0)
            emb = np.concatenate([freqs, freqs], axis=-1)
            return (jnp.asarray(np.cos(emb) * msc, jnp.float32), jnp.asarray(np.sin(emb) * msc, jnp.float32))

        def rms_norm(x, w, eps=1e-06):
            xf = x.astype(jnp.float32)
            var = jnp.mean(xf * xf, axis=-1, keepdims=True)
            return (xf * jax.lax.rsqrt(var + eps)).astype(x.dtype) * w

        def rotate_half(x):
            x1, x2 = jnp.split(x, 2, axis=-1)
            return jnp.concatenate([-x2, x1], axis=-1)

        def apply_rope(x, cos, sin):
            b, h, s, d = x.shape
            x = x.reshape(b, h, s, d // 2, 2).transpose(0, 1, 2, 4, 3).reshape(b, h, s, d)
            return x * cos + rotate_half(x) * sin
        b, s, _ = hidden_states.shape
        q = rms_norm(hidden_states @ wq_a, q_a_norm_w) @ wq_b
        q = q.reshape(b, s, NH, Q_HEAD).transpose(0, 2, 1, 3)
        q_nope, q_pe = (q[..., :QK_NOPE], q[..., QK_NOPE:])
        ckv = hidden_states @ wkv_a
        compressed_kv, k_pe = (ckv[..., :KV_RANK], ckv[..., KV_RANK:])
        k_pe = k_pe.reshape(b, s, 1, QK_ROPE).transpose(0, 2, 1, 3)
        kv = rms_norm(compressed_kv, kv_a_norm_w) @ wkv_b
        kv = kv.reshape(b, s, NH, QK_NOPE + V_DIM).transpose(0, 2, 1, 3)
        k_nope, value_states = (kv[..., :QK_NOPE], kv[..., QK_NOPE:])
        cos, sin = yarn_cos_sin(s, QK_ROPE)
        cos, sin = (cos[None, None], sin[None, None])
        k_pe = jnp.broadcast_to(k_pe, (b, NH, s, QK_ROPE))
        q_pe = apply_rope(q_pe, cos, sin)
        k_pe = apply_rope(k_pe, cos, sin)
        query_states = jnp.concatenate([q_nope, q_pe], axis=-1)
        key_states = jnp.concatenate([k_nope, k_pe], axis=-1)
        attn = jnp.einsum('bhqd,bhkd->bhqk', query_states, key_states) * SOFTMAX_SCALE
        attn = jax.nn.softmax(attn.astype(jnp.float32), axis=-1).astype(query_states.dtype)
        out = jnp.einsum('bhqk,bhkd->bhqd', attn, value_states)
        out = out.transpose(0, 2, 1, 3).reshape(b, s, NH * V_DIM)
        return out @ wo

    def _L0_ffn_ref(x, gate_kernel, w0_kernel, w1_kernel, wo_kernel):
        import jax, jax.numpy as jnp
        import numpy as np
        NUM_EXPERTS = 8
        TOP_K = 2
        EMB = 256
        MLP = 512
        B, S = (4, 128)
        gate_logits = jnp.einsum('bsd,de->bse', x, gate_kernel)
        top_k_weights, top_k_indices = jax.lax.top_k(gate_logits, TOP_K)
        top_k_weights = jax.nn.softmax(top_k_weights.astype(jnp.float32), axis=-1).astype(x.dtype)
        one_hot = jax.nn.one_hot(top_k_indices, NUM_EXPERTS, dtype=x.dtype)
        combine = jnp.einsum('bsk,bske->bse', top_k_weights, one_hot)
        h0 = jnp.einsum('bsd,edm->bsem', x, w0_kernel)
        h1 = jnp.einsum('bsd,edm->bsem', x, w1_kernel)
        inter = jax.nn.silu(h0) * h1
        out = jnp.einsum('bse,bsem,emd->bsd', combine, inter, wo_kernel)
        return out
    x = L0_attn_hidden_states
    x = x + 0.5 * _L0_ffn_ref(_layernorm(x, axis=-1), L0_ffn_gate_kernel, L0_ffn_w0_kernel, L0_ffn_w1_kernel, L0_ffn_wo_kernel)
    x = x + _L0_attn_ref(_layernorm(x, axis=-1), L0_attn_wq_a, L0_attn_q_a_norm_w, L0_attn_wq_b, L0_attn_wkv_a, L0_attn_kv_a_norm_w, L0_attn_wkv_b, L0_attn_wo)
    x = x + 0.5 * _L0_ffn_ref(_layernorm(x, axis=-1), L0_ffn_gate_kernel, L0_ffn_w0_kernel, L0_ffn_w1_kernel, L0_ffn_wo_kernel)
    return x

_drawn_inputs = setup_inputs


def setup_inputs(seed=0):
    import zlib

    import numpy as np

    out = dict(_drawn_inputs(seed))
    spreads = {'L0_attn_q_a_norm_w': (1.0, 0.6), 'L0_attn_kv_a_norm_w': (1.0, 0.6)}
    factors = {'L0_attn_wq_a': 8.0,
     'L0_attn_wq_b': 8.0,
     'L0_attn_wkv_a': 4.701,
     'L0_attn_wkv_b': 5.221,
     'L0_attn_wo': 5.548}
    for name, (base, spread) in spreads.items():
        noise = np.random.default_rng([zlib.crc32(name.encode()), seed]).standard_normal(out[name].shape)
        drawn = base * np.exp(spread * noise) if base else spread * noise
        out[name] = jnp.asarray(drawn.astype(out[name].dtype))
    for name, factor in factors.items():
        out[name] = (out[name] * factor).astype(out[name].dtype)
    return out
```

```python
import math
from contextlib import ExitStack, contextmanager

import numpy as np
import concourse.bass as bass
from concourse import mybir

F32 = mybir.dt.float32
I32 = mybir.dt.int32
U32 = mybir.dt.uint32
ALU = mybir.AluOpType
ACT = mybir.ActivationFunctionType
AX = mybir.AxisListType

P = 128
B, S, D = 4, 512, 256
T = B * S
NT = T // P
GT = S // P
NG = NT // GT
KC = D // P

E, TOPK, MLP = 8, 2, 512
MC = MLP // P
REGION = T + P
TILES = (T * TOPK + E * (P - 1)) // P
SPARE = TILES - T * TOPK // P
ROW = D + 2
SKIP = 1 << 20
WEXP = 2 * KC * MLP + MC * D

NH, HD, ROPE = 16, 64, 64
HALF = ROPE // 2
PAIRS = NH // 2
SCALE = (HD + ROPE) ** -0.5
VW = HD + 1
NPAIR = B * PAIRS
LN_EPS, RMS_EPS = 1e-5, 1e-6


def rope_tables():
    base, factor, fast, slow, orig, mscale = 10000.0, 40.0, 32.0, 1.0, 512, 0.707
    ex = np.arange(0, ROPE, 2, dtype=np.float64) / ROPE
    extra, inter = 1.0 / base ** ex, 1.0 / (factor * base ** ex)
    corr = lambda rot: ROPE * math.log(orig / (rot * 2 * math.pi)) / (2 * math.log(base))
    low, high = max(math.floor(corr(fast)), 0), min(math.ceil(corr(slow)), ROPE - 1)
    if low == high:
        high = high + 0.001
    ramp = np.clip((np.arange(HALF, dtype=np.float64) - low) / (high - low), 0.0, 1.0)
    freq = inter * ramp + extra * (1.0 - ramp)
    ang = np.outer(np.arange(S, dtype=np.float64), freq)
    m = (0.1 * mscale * math.log(factor) + 1.0) / 1.0
    return (np.cos(ang) * m).astype(np.float32), (np.sin(ang) * m).astype(np.float32)


C_ID, C_UP, C_ONE = 0, P, 2 * P
C_IOTA = 3 * P
C_BASE = C_IOTA + E
C_J = C_BASE + E
C_STEP = C_J + TILES
C_HALF = C_STEP + NT
C_KCOS = C_HALF + NT
C_KSIN = C_KCOS + GT * HALF
C_COS = C_KSIN + GT * HALF
C_SIN = C_COS + S
C_ALL = C_SIN + S


def constants():
    c = np.zeros((P, C_ALL), np.float32)
    c[:, C_ID:C_ID + P] = np.eye(P)
    c[:, C_UP:C_UP + P] = np.triu(np.ones((P, P)), 1)
    c[:, C_ONE:C_ONE + P] = 1.0
    c[:, C_IOTA:C_IOTA + E] = np.arange(E)
    c[:, C_BASE:C_BASE + E] = np.arange(E) * REGION
    c[:, C_J:C_J + TILES] = np.arange(TILES)
    c[:, C_STEP:C_STEP + NT] = np.arange(NT) * P
    c[:, C_HALF:C_HALF + NT] = -0.5
    cos, sin = rope_tables()
    c[:, C_KCOS:C_KSIN] = cos.reshape(GT, P, HALF).transpose(1, 0, 2).reshape(P, -1)
    c[:, C_KSIN:C_COS] = sin.reshape(GT, P, HALF).transpose(1, 0, 2).reshape(P, -1)
    c[:, C_COS:C_SIN] = np.tile(cos.T, (4, 1))
    c[:, C_SIN:C_ALL] = np.tile(sin.T, (4, 1))
    ids = (np.arange(NT)[None, :] * P + np.arange(P)[:, None]).astype(np.int32)
    return c, ids


class Steps:

    def __init__(self, eng, sem):
        self.eng, self.sem, self.done, self.it = eng, sem, 0, 0
        self.per = 0

    @contextmanager
    def loop(self, i, times, per):
        start = self.done
        self.it, self.per = i, per
        yield
        assert self.done - start == per, (self.done - start, per)
        self.it, self.per, self.done = 0, 0, start + times * per

    def step(self, ins):
        ins.then_inc(self.sem, 1)
        self.done += 1

    def settle(self):
        self.eng.wait_ge(self.sem, self.it * self.per + self.done)


def build(nc, x_in, wq_a, qn_w, wq_b, wkv_a, kvn_w, wkv_b, wo, gate, w0, w1, wout, const, ids_in, out):
    xs = nc.dram_tensor("rows_by_expert", [E * REGION + SPARE * P, ROW], F32, kind="Internal").ap()
    xd = nc.dram_tensor("x_after_moe", [T, D], F32, kind="Internal").ap()
    atd = nc.dram_tensor("attended", [T, NH * HD], F32, kind="Internal").ap()

    ctx = ExitStack()
    with ctx:
        def sb(name, shape, dt=F32):
            return ctx.enter_context(nc.sbuf_tensor(name, shape, dt))

        def sem(name):
            return ctx.enter_context(nc.semaphore(name))

        def sems(name, n):
            return [sem(f"{name}{k}") for k in range(n)]

        bank = [ctx.enter_context(nc.psum_tensor(f"bank{k}", [P, 512], F32)) for k in range(8)]

        wall = sb("expert_weights", [P, E * WEXP])
        cst = sb("constants", [P, C_ALL])
        ids = sb("token_ids", [P, NT], I32)
        gate_sb = sb("gate_weights", [P, KC, E])
        wproj = sb("attention_in_weights", [P, KC, 3 * HD])
        norm_w = sb("latent_norm_weights", [HD, 2])
        rows = [sb(f"rows{u}", [P, GT, TOPK, ROW]) for u in range(2)]
        wpair = sb("query_weights", [HD, PAIRS, 3, P])
        wvo = sb("value_out_weights", [P, PAIRS, D])
        zrow = sb("empty_rows", [P, ROW])
        small = sb("small", [P, 1024])
        shared = sb("shared", [P, 8 * 256 + 13328])

        used = [0]

        def tiny(shape, dt=F32):
            n = int(np.prod(shape))
            v = small[:, used[0]:used[0] + n]
            used[0] += n
            assert used[0] <= 1024
            if dt != F32:
                v = v.bitcast(dt)
            names = "abcd"[:len(shape)]
            return v.rearrange(f"p ({' '.join(names)}) -> p {' '.join(names)}", **dict(zip(names, shape)))

        def area(at, shape, parts=P):
            n = int(np.prod(shape))
            v = shared[0:parts, at:at + n]
            names = "abcd"[:len(shape)]
            return v.rearrange(f"p ({' '.join(names)}) -> p {' '.join(names)}", **dict(zip(names, shape)))

        ident, upper, ones = (cst[:, c:c + P] for c in (C_ID, C_UP, C_ONE))
        iota_e = cst[:, C_IOTA:C_IOTA + E]
        region_at = cst[:, C_BASE:C_BASE + E]
        minus_half = cst[:, C_HALF:C_HALF + NT]
        kcos = cst[:, C_KCOS:C_KSIN].rearrange("p (t c) -> p t c", t=GT)
        ksin = cst[:, C_KSIN:C_COS].rearrange("p (t c) -> p t c", t=GT)
        qcos, qsin = cst[:, C_COS:C_SIN], cst[:, C_SIN:C_ALL]

        stats = tiny([GT, 6])
        mv = tiny([NT, 2])
        veps = tiny([NT])
        rstd = tiny([NT])
        logit = tiny([GT, E])
        top = tiny([GT, 8])
        topi = tiny([GT, 8], U32)
        topf = tiny([GT, TOPK])
        diff = tiny([GT])
        e2 = tiny([GT])
        den = tiny([GT])
        rden = tiny([GT])
        hot1, hot2 = tiny([GT, E]), tiny([GT, E])
        mask = tiny([GT, E])
        msum = tiny([E])
        carry = tiny([E])
        place = tiny([GT, E])
        pl1, pl2 = tiny([GT, E]), tiny([GT, E])
        slotf = tiny([TOPK, GT])
        slot = [tiny([TOPK, GT], U32) for _ in range(2)]
        cnt = tiny([E])
        over = tiny([E, NT])
        ntile = tiny([E])
        tend = tiny([E])
        zero8 = tiny([E])
        cnt_i = tiny([E], I32)
        texp = tiny([TILES])
        tfirst = tiny([TILES])
        trow = tiny([TILES])
        row_tab = tiny([TILES], I32)
        wcol_tab = tiny([TILES], I32)
        tag = [tiny([2]) for _ in range(3)]
        ssq = tiny([GT, 3])
        rvar = tiny([GT, 3])
        rrms = tiny([GT, 3])
        negmax = tiny([8])
        rsum = tiny([GT])

        xgroup = [area(u * GT * D, [GT, D]) for u in range(2)]
        xall = area(0, [NT, D])
        o = NT * D
        stage_q = area(o, [NH * 2 * HD], HD)
        stage_kv = area(o + 2048, [NH * 2 * HD], HD)
        stage_o = area(o + 4096, [NH, D], HD)
        qnT = area(o + 8192, [NH, HD], HD)
        knT = area(o + 9216, [NH, HD], HD)
        vT = area(o + 10240, [NH, HD], HD)
        o = 2 * GT * D
        ge_tab = area(o, [TILES, E])
        o = 2 * GT * D
        xslot = [area(o + k * ROW, [ROW]) for k in range(3)]
        o += 3 * ROW + 2
        xT = [area(o + k * D, [KC, P]) for k in range(3)]
        o += 3 * D
        gated = area(o, [MLP])
        inter = area(o + MLP, [MLP])
        interT = area(o + 2 * MLP, [MC, P])
        ysb = [area(o + 3 * MLP + k * D, [D]) for k in range(3)]
        o = 2 * GT * D
        kE = area(o, [B, S])
        kO = area(o + 2048, [B, S])
        vals = area(o + 4096, [B, GT, VW])
        o += 4096 + B * GT * VW
        cqT = area(o, [B, S])
        o += 2048
        m = o
        xnT = area(m, [KC, S])
        proj = area(m + 1024, [GT, 3 * HD])
        psq = area(m + 1792, [GT, 3 * HD])
        keys = area(m + 2560, [GT, 3 * HD])
        cqn = area(m + 3328, [GT, HD])
        rt = [area(m + 3584 + k * GT * HALF, [GT, HALF]) for k in range(4)]
        qs = [[area(m + (2 * par + hh) * S, [S]) for hh in range(2)] for par in range(2)]
        prob = [area(m + 2048 + k * S, [S]) for k in range(2)]
        probT = [area(m + 3072 + k * S, [S]) for k in range(2)]
        ropeA, ropeB = area(m + 4096, [S]), area(m + 4608, [S])
        att = [area(m + 5120 + k * S, [GT, P]) for k in range(2)]
        wcur = wproj[:, :, :].rearrange("p c n -> p (c n)").rearrange("p (a n) -> p a n", a=3)
        o = 2 * GT * D
        xTr = [wvo[:, 0:KC * S // D, :].rearrange("p a n -> p (a n)").rearrange("p (c n) -> p c n", c=KC),
               area(o, [KC, S])]
        attl = [area(o + 1024 + k * 1024, [8, P]) for k in range(2)]
        attT = [area(o + 3072 + k * 1024, [8, P]) for k in range(2)]

        const_in, x_in_sem = sem("const_in"), sems("x_group_in", NG)
        attw_in, moew_in, xd_copied, spare_zeroed = sem("attw_in"), sem("moew_in"), sem("xd_copied"), sem("spare_zeroed")
        zrow_ready = sem("zrow_ready")
        own_v, own_a, own_p = sem("own_v"), sem("own_a"), sem("own_p")
        veps_ready, rstd_ready = sems("veps_ready", 3), sems("rstd_ready", 3)
        xn_ready, xn_psum = sems("xn_ready", 3), sems("xn_psum", 3)
        xn_sb0, xn_sb1 = sems("xn_sb_a", 3), sems("xn_sb_b", 3)
        xn_copied = sems("xn_copied", 2)
        logits_psum, diff_ready, e2_ready = sems("logits_psum", 2), sems("diff_ready", 2), sems("e2_ready", 2)
        mask_ready, ranks_psum = sems("mask_ready", 2), sems("ranks_psum", 2)
        slots_ready = sems("slots_ready", 2)
        scattered = [sems(f"scattered{f}_", 2) for f in range(2)]
        carry_ready, counts_psum, tables_ready, tails_zeroed = sems("carry_ready", 2), sems("counts_psum", 2), sems("tables_ready", 2), sems("tails_zeroed", 2)
        slots_in = [sems(f"slots_in{f}_", 3) for f in range(2)]
        xt_psum, xt_sb = sems("xt_psum", 2), sems("xt_sb", 2)
        h0_psum, h1_psum = sems("h0_psum", 2), sems("h1_psum", 2)
        silu_ready, inter_ready = sems("silu_ready", 2), sems("inter_ready", 2)
        it_psum, it_sb = sems("it_psum", 2), sems("it_sb", 2)
        y_psum, y_sb = sems("y_psum", 2), sems("y_sb", 2)
        tag_sb = sems("tag_sb", 2)
        add_due = sems("add_due", 2)
        added = [sems(f"added{f}_", 3) for f in range(2)]
        scaled_w, wt_psum, wt_sb, zw_psum, vo_psum = sem("scaled_w"), sem("wt_psum"), sem("wt_sb"), sem("zw_psum"), sem("vo_psum")
        folded_w, wa_ready = sem("folded_w"), sem("wa_ready")
        xattn_in = sems("xattn_in", 2)
        proj_psum, proj_sb, var2_ready, rms_ready = sem("proj_psum"), sem("proj_sb"), sem("var2_ready"), sem("rms_ready")
        keys_ready, kT_psum, kE_sb, kO_sb = sem("keys_ready"), sem("kT_psum"), sem("kE_sb"), sem("kO_sb")
        wcur_ready, qa_psum, qb_psum, qz_psum = sem("wcur_ready"), sem("qa_psum"), sem("qb_psum"), sem("qz_psum")
        ropeA_sb, ropeB_sb, qz_sb, q_rope = sem("ropeA_sb"), sem("ropeB_sb"), sem("qz_sb"), sem("q_rope")
        s_psum, max_ready, exp_ready = sem("s_psum"), sem("max_ready"), sem("exp_ready")
        pT_psum, pT_even, pT_odd = sem("pT_psum"), sem("pT_even"), sem("pT_odd")
        o_psum, att_ready, att_stored = sem("o_psum"), sem("att_ready"), sems("att_stored", 2)
        x2in, attl_in = sems("x2in", 2), sems("attl_in", 2)
        aT_psum, aT_sb0, aT_sb1 = sem("aT_psum"), sem("aT_sb_a"), sem("aT_sb_b")
        wo_psum, x2_ready, out_stored = sem("wo_psum"), sem("x2_ready"), sems("out_stored", 2)

        block = ctx.enter_context(nc.Block())

        def in_turn(i, k):
            return i + k // 3 + 1

        @block.sync
        def _(sp):
            sp.dma_start(cst[:, :], const).then_inc(const_in, 16)
            sp.dma_start(ids[:, :], ids_in).then_inc(const_in, 16)
            sp.dma_start(gate_sb[:, :, :], gate.rearrange("(c p) e -> p c e", p=P)).then_inc(const_in, 16)
            for g in range(NG):
                sp.dma_start(xall[:, g * GT:(g + 1) * GT, :],
                             x_in[g].rearrange("(t p) d -> p t d", p=P)).then_inc(x_in_sem[g], 16)
            sp.dma_start(wproj[:, :, 0:2 * HD], wkv_a.rearrange("(c p) n -> p c n", p=P)).then_inc(attw_in, 16)
            sp.dma_start(wproj[:, :, 2 * HD:3 * HD], wq_a.rearrange("(c p) n -> p c n", p=P)).then_inc(attw_in, 16)
            sp.dma_start(norm_w[:, 0:1], qn_w.rearrange("(p a) -> p a", a=1)).then_inc(attw_in, 16)
            sp.dma_start(norm_w[:, 1:2], kvn_w.rearrange("(p a) -> p a", a=1)).then_inc(attw_in, 16)
            sp.dma_start(stage_q, wq_b).then_inc(attw_in, 16)
            sp.dma_start(stage_kv, wkv_b).then_inc(attw_in, 16)
            sp.dma_start(stage_o, wo.rearrange("(h v) n -> v h n", v=HD)).then_inc(attw_in, 16)
            for e in range(E):
                we = wall[:, e * WEXP:(e + 1) * WEXP]
                sp.dma_start(we[:, 0:KC * MLP].rearrange("p (c n) -> p c n", c=KC),
                             w0[e].rearrange("(c p) n -> p c n", p=P)).then_inc(moew_in, 16)
                sp.dma_start(we[:, KC * MLP:2 * KC * MLP].rearrange("p (c n) -> p c n", c=KC),
                             w1[e].rearrange("(c p) n -> p c n", p=P)).then_inc(moew_in, 16)
                sp.dma_start(we[:, 2 * KC * MLP:WEXP].rearrange("p (c n) -> p c n", c=MC),
                             wout[e].rearrange("(c p) n -> p c n", p=P)).then_inc(moew_in, 16)
            sp.dma_start(xd, x_in.rearrange("b s d -> (b s) d")).then_inc(xd_copied, 16)
            sp.wait_ge(zrow_ready, 2)
            for k in range(SPARE):
                at = E * REGION + k * P
                sp.dma_start(xs[at:at + P, :], zrow[:, :]).then_inc(spare_zeroed, 16)

            def moe(f):
                sp.wait_ge(tables_ready[f], 1)
                for e in range(E):
                    n = sp.value_load(cnt_i[0:1, e:e + 1], min_val=0, max_val=T)
                    sp.dma_start(xs[bass.ds(n + e * REGION, P), :], zrow[:, :]).then_inc(tails_zeroed[f], 16)
                if f == 0:
                    sp.wait_ge(spare_zeroed, 16 * SPARE)
                sp.wait_ge(tails_zeroed[f], 16 * E)
                for u in range(2):
                    sp.wait_ge(scattered[f][u], 16 * GT * TOPK * NG // 2)

                def turn(i):
                    for v in range(3):
                        at = sp.value_load(row_tab[0:1, bass.ds(i * 3 + v, 1)], min_val=0,
                                           max_val=E * REGION + (SPARE - 1) * P)
                        if not isinstance(i, int):
                            sp.wait_ge(tag_sb[f], i * 3 + v - 2)
                        sp.dma_start(xslot[v], xs[bass.ds(at, P), :]).then_inc(slots_in[f][v], 16)

                turn(0)
                with sp.Fori(1, TILES // 3) as i:
                    turn(i)
                for v in range(3):
                    sp.wait_ge(added[f][v], 16 * TILES // 3)

            moe(0)
            for i in range(NG // 2):
                for u in range(2):
                    sp.wait_ge(xn_ready[1], i * 2)
                    sp.dma_start(xgroup[u], xd[bass.ds((i * 2 + u) * S, S), :]
                                 .rearrange("(t p) d -> p t d", p=P)).then_inc(xattn_in[u], 16)
            with sp.Fori(0, NPAIR // 2) as i:
                for v in range(2):
                    p = i * 2 + v
                    row, col = sp.snap((p // PAIRS) * S), sp.snap((p % PAIRS) * P)
                    dst = atd[bass.ds(row, S), bass.ds(col, P)]
                    sp.wait_ge(att_ready, p * 2 + 2)
                    sp.dma_start(dst.rearrange("(t p) n -> p t n", p=P), att[v]).then_inc(att_stored[v], 16)
            for v in range(2):
                sp.wait_ge(att_stored[v], 16 * NPAIR // 2)
            for i in range(NG // 2):
                for u in range(2):
                    g = i * 2 + u
                    sp.wait_ge(out_stored[u], i * 16)
                    sp.wait_ge(xn_ready[2], i * 2)
                    sp.dma_start(xgroup[u], xd[bass.ds(g * S, S), :]
                                 .rearrange("(t p) d -> p t d", p=P)).then_inc(x2in[u], 16)
                    for j in range(GT):
                        k = g * GT + j
                        sp.wait_ge(aT_psum, g * GT * 2 + max(j - 1, 0) * 2)
                        sp.dma_start(attl[j % 2], atd[bass.ds(k * P, P), :]
                                     .rearrange("p (c n) -> p c n", n=P)).then_inc(attl_in[j % 2], 16)
                    sp.wait_ge(x2_ready, g * GT + GT)
                    sp.dma_start(out.rearrange("b s d -> (b s) d")[bass.ds(g * S, S), :]
                                 .rearrange("(t p) d -> p t d", p=P), xgroup[u]).then_inc(out_stored[u], 16)
            moe(1)

        @block.gpsimd
        def _(pool):
            own = Steps(pool, own_p)
            nc.gpsimd.memset(zrow[:, 0:D + 1], 0.0).then_inc(zrow_ready, 1)
            nc.gpsimd.memset(zrow[:, D + 1:ROW].bitcast(I32), SKIP).then_inc(zrow_ready, 1)

            def root(n, at, count):
                nc.gpsimd.tensor_tensor(rstd[:, bass.ds(at, count)], veps[:, bass.ds(at, count)],
                                        minus_half[:, 0:count], ALU.pow).then_inc(rstd_ready[n], 1)

            def scatter(f, i, u):
                pool.wait_ge(slots_ready[f], i * 2 + u + 1)
                pool.wait_ge(xn_copied[f], i * 2 + u + 1)
                for k in range(TOPK):
                    for j in range(GT):
                        nc.gpsimd.indirect_dma_start(
                            out=xs, out_offset=bass.IndirectOffsetOnAxis(ap=slot[u][:, k, j:j + 1], axis=0),
                            in_=rows[u][:, j, k, :], in_offset=None).then_inc(scattered[f][u], 16)

            def add_results(f, dst):

                def turn(i):
                    for v in range(3):
                        pool.wait_ge(y_sb[f], i * 3 + v + 1)
                        prev = (v - 1) % 3
                        pool.wait_ge(added[f][prev], (i + (v > 0)) * 16)
                        pool.sem_inc(add_due[f], 1)
                        nc.gpsimd.indirect_dma_start(
                            out=dst, out_offset=bass.IndirectOffsetOnAxis(
                                ap=tag[v][:, 1:2].bitcast(U32), axis=0),
                            in_=ysb[v], in_offset=None, bounds_check=T - 1, oob_is_err=False,
                            compute_op=ALU.add).then_inc(added[f][v], 16)

                turn(0)
                with pool.Fori(1, TILES // 3) as i:
                    turn(i)

            pool.wait_ge(const_in, 48)
            pool.wait_ge(veps_ready[0], 1)
            root(0, 0, NT)
            for i in range(NG // 2):
                for u in range(2):
                    scatter(0, i, u)
            pool.wait_ge(xd_copied, 16)
            add_results(0, xd)

            for i in range(NG // 2):
                for u in range(2):
                    g = i * 2 + u
                    pool.wait_ge(veps_ready[1], g + 1)
                    root(1, 0, GT)
                    pool.wait_ge(var2_ready, g + 1)
                    nc.gpsimd.tensor_tensor(rrms, rvar, minus_half[:, 0:GT * 3].rearrange("p (a b) -> p a b", a=GT),
                                            ALU.pow).then_inc(rms_ready, 1)

            def load_pair(p, used):
                a = p % PAIRS if isinstance(p, int) else pool.snap(p % PAIRS)
                if used is not None:
                    pool.wait_ge(qz_psum, used)
                nc.gpsimd.tensor_copy(wcur[0:HD], wpair[:, bass.ds(a, 1), :, :]
                                      .rearrange("p a s n -> p (a s) n")).then_inc(wcur_ready, 1)

            def rope_sum(p, par):
                pool.wait_ge(ropeB_sb, p + 1)
                nc.gpsimd.tensor_tensor(qs[par][0][0:HD, :], ropeA[0:HD, :], ropeB[0:HD, :], ALU.add)
                nc.gpsimd.tensor_tensor(qs[par][1][HD:P, :], ropeA[HD:P, :], ropeB[HD:P, :],
                                        ALU.add).then_inc(q_rope, 1)

            pool.wait_ge(folded_w, 2)
            pool.wait_ge(wa_ready, 1)
            pool.wait_ge(kE_sb, 2 * B)
            own.step(nc.gpsimd.memset(wcur, 0.0))
            own.settle()
            load_pair(0, None)
            load_pair(1, 1)
            rope_sum(0, 0)

            def pair(p, par):
                load_pair(p + 2, p + 2)
                rope_sum(p + 1, 1 - par)

            pair(0, 0)
            with pool.Fori(0, NPAIR // 2 - 1) as i:
                for v in range(2):
                    pair(i * 2 + 1 + v, 1 - v)

            for i in range(NG // 2):
                for u in range(2):
                    g = i * 2 + u
                    pool.wait_ge(veps_ready[2], g + 1)
                    root(2, 0, GT)
                    scatter(1, i, u)
            for u in range(2):
                pool.wait_ge(out_stored[u], 16 * NG // 2)
            add_results(1, out.rearrange("b s d -> (b s) d"))
            for v in range(3):
                pool.wait_ge(added[1][v], 16 * TILES // 3)

        @block.scalar
        def _(act):
            own = Steps(act, own_a)

            def xn_out(n, g, u, dst, freed, copies):
                if copies:
                    act.wait_ge(xn_ready[n], g + 1)
                    nc.scalar.copy(rows[u][:, :, 1, 0:D], rows[u][:, :, 0, 0:D]).then_inc(xn_copied[n // 2], 1)
                act.wait_ge(xn_psum[n], g * 2 + 1)
                act.wait_ge(freed, g)
                nc.scalar.copy(dst[:, 0, :], bank[0][:, :]).then_inc(xn_sb0[n], 1)

            def route(f, i, u):
                g = i * 2 + u
                xn_out(2 * f, g, u, xTr[f], logits_psum[f], True)
                act.wait_ge(diff_ready[f], g + 1)
                nc.scalar.activation(e2, diff, ACT.Exp).then_inc(e2_ready[f], 1)

            for i in range(NG // 2):
                for u in range(2):
                    route(0, i, u)

            act.wait_ge(attw_in, 16 * 7)
            own.step(nc.scalar.activation(stage_q, stage_q, ACT.Copy, scale=norm_w[:, 0:1]))
            own.step(nc.scalar.activation(stage_kv, stage_kv, ACT.Copy, scale=norm_w[:, 1:2]))
            own.settle()
            nc.scalar.mul(stage_q, stage_q, SCALE).then_inc(scaled_w, 1)
            for k, dst in enumerate((qnT, qnT, knT, knT, vT, vT)):
                act.wait_ge(wt_psum, k + 1)
                nc.scalar.copy(dst[:, (k % 2) * 8:(k % 2) * 8 + 8, :].rearrange("p h n -> p (h n)"),
                               bank[k][0:HD, :]).then_inc(wt_sb, 1)
            for k in range(2):
                act.wait_ge(zw_psum, k + 1)
                src = bank[6 + k][0:HD, :].rearrange("p (a h n) -> p a h n", a=4, h=2)
                for hh in range(2):
                    last = nc.scalar.copy(wpair[:, 4 * k:4 * k + 4, 2, (1 - hh) * HD:(2 - hh) * HD], src[:, :, hh, :])
                last.then_inc(folded_w, 1)
            for k in range(4):
                act.wait_ge(vo_psum, k + 1)
                nc.scalar.copy(wvo[:, 2 * k:2 * k + 2, :].rearrange("p a n -> p (a n)"), bank[k][:, :]).then_inc(folded_w, 1)

            def moe(f):
                with act.Fori(0, TILES // 3) as i:
                    for v in range(3):
                        t = i * 3 + v
                        act.wait_ge(h0_psum[f], t + 1)
                        nc.scalar.activation(gated, bank[4][:, :], ACT.Silu).then_inc(silu_ready[f], 1)
                        act.wait_ge(it_psum[f], t + 1)
                        nc.scalar.copy(interT.rearrange("p c n -> p (c n)"), bank[6][:, :]).then_inc(it_sb[f], 1)

            moe(0)

            for i in range(NG // 2):
                for u in range(2):
                    g = i * 2 + u
                    xn_out(1, g, u, xnT, proj_psum, False)
                    act.wait_ge(proj_psum, g + 1)
                    act.wait_ge(keys_ready, g)
                    nc.scalar.copy(proj[:, 0:2, :].rearrange("p t n -> p (t n)"), bank[2][:, 0:6 * HD]).then_inc(proj_sb, 1)
                    act.wait_ge(kT_psum, g + 1)
                    nc.scalar.copy(kE[:, bass.ds(g, 1), :].rearrange("p a n -> p (a n)"), bank[4][:, :]).then_inc(kE_sb, 1)
                    nc.scalar.copy(cqT[0:HD, bass.ds(g, 1), :].rearrange("p a n -> p (a n)"), bank[6][0:HD, :]).then_inc(kE_sb, 1)

            def exp(s, k):
                act.wait_ge(max_ready, s + 1)
                if k > 0:
                    act.wait_ge(pT_psum, s - 1)
                nc.scalar.activation(prob[k % 2], bank[k % 4][:, :], ACT.Exp,
                                     bias=negmax[:, k % 8:k % 8 + 1]).then_inc(exp_ready, 1)

            def queries_latent(p, par):
                act.wait_ge(qz_psum, p + 1)
                nc.scalar.copy(qs[par][0][HD:P, :], bank[7][HD:P, :])
                nc.scalar.copy(qs[par][1][0:HD, :], bank[7][0:HD, :]).then_inc(qz_sb, 1)

            def pair(p, par, last):
                for k in range(8):
                    s = p * 8 + k
                    if not (last and k == 7):
                        exp(s + 1, k + 1)
                    if k % 2:
                        act.wait_ge(pT_psum, s + 1)
                        nc.scalar.copy(probT[1], bank[5][:, :]).then_inc(pT_odd, 1)
                    if k == 4 and not last:
                        queries_latent(p + 1, 1 - par)

            queries_latent(0, 0)
            exp(0, 0)
            pair(0, 0, False)
            with act.Fori(0, NPAIR // 2 - 1) as i:
                for v in range(2):
                    pair(i * 2 + 1 + v, 1 - v, False)
            pair(NPAIR - 1, 1, True)

            for i in range(NG // 2):
                for u in range(2):
                    g = i * 2 + u
                    for j in range(GT):
                        t = g * GT + j
                        act.wait_ge(aT_psum, t * 2 + 1)
                        nc.scalar.copy(attT[j % 2][:, 0:4, :].rearrange("p c n -> p (c n)"), bank[4][:, :]).then_inc(aT_sb0, 1)
                    route(1, i, u)
            moe(1)

        @block.vector
        def _(dve):
            own = Steps(dve, own_v)
            V = nc.vector

            def ln_stats(x, at, tiles, signal):
                for j in range(tiles):
                    own.step(V.bn_stats(stats[:, j, :], x[:, j, :]))
                own.settle()
                for j in range(tiles):
                    own.step(V.bn_aggr(mv[:, bass.ds(at + j, 1), :].rearrange("p a b -> p (a b)"), stats[:, j, :]))
                own.settle()
                ins = V.tensor_scalar(veps[:, bass.ds(at, tiles)],
                                      mv[:, bass.ds(at, tiles), 1:2].rearrange("p a b -> p (a b)"),
                                      LN_EPS, None, ALU.add)
                if signal is None:
                    own.step(ins)
                else:
                    ins.then_inc(signal, 1)

            def ln_rows(n, x, at, g, u):
                for j in range(GT):
                    ins = V.tensor_scalar(rows[u][:, j, 0, 0:D], x[:, j, :],
                                          mv[:, bass.ds(at + j, 1), 0:1].rearrange("p a b -> p (a b)"),
                                          rstd[:, bass.ds(at + j, 1)], ALU.subtract, ALU.mult)
                ins.then_inc(xn_ready[n], 1)

            def route(f, x, i, u):
                g = i * 2 + u
                dve.wait_ge(slots_ready[f], g)
                dve.wait_ge(scattered[f][u], i * (16 * GT * TOPK))
                ln_rows(2 * f, x, g * GT if f == 0 else 0, g, u)
                dve.wait_ge(xn_psum[2 * f], g * 2 + 2)
                V.tensor_copy(xTr[f][:, 1, :], bank[1][:, :]).then_inc(xn_sb1[2 * f], 1)
                dve.wait_ge(logits_psum[f], g + 1)
                own.step(V.tensor_copy(logit.rearrange("p t e -> p (t e)"), bank[2][:, 0:GT * E]))
                own.settle()
                for j in range(GT):
                    own.step(V.max(top[:, j, :], logit[:, j, :]))
                own.settle()
                for j in range(GT):
                    own.step(V.max_index(topi[:, j, :], top[:, j, :], logit[:, j, :]))
                own.settle()
                own.step(V.tensor_copy(topf, topi[:, :, 0:TOPK]))
                V.tensor_tensor(diff.unsqueeze(2), top[:, :, 1:2], top[:, :, 0:1], ALU.subtract).then_inc(diff_ready[f], 1)
                own.settle()
                iota_b = iota_e.unsqueeze(1).to_broadcast([P, GT, E])
                own.step(V.tensor_tensor(hot1, iota_b, topf[:, :, 0:1].to_broadcast([P, GT, E]), ALU.is_equal))
                own.step(V.tensor_tensor(hot2, iota_b, topf[:, :, 1:2].to_broadcast([P, GT, E]), ALU.is_equal))
                own.settle()
                V.tensor_tensor(mask, hot1, hot2, ALU.add).then_inc(mask_ready[f], 1)
                dve.wait_ge(e2_ready[f], g + 1)
                own.step(V.tensor_scalar(den, e2, 1.0, None, ALU.add))
                own.settle()
                own.step(V.reciprocal(rden, den))
                own.settle()
                V.tensor_scalar(rows[u][:, :, 0, D:D + 1], rden.unsqueeze(2), 0.5, None, ALU.mult)
                V.scalar_tensor_tensor(rows[u][:, :, 1, D:D + 1], e2.unsqueeze(2), 0.5, rden.unsqueeze(2),
                                       ALU.mult, ALU.mult)
                for k in range(TOPK):
                    own.step(V.tensor_copy(rows[u][:, :, k, D + 1:ROW].bitcast(I32),
                                           ids[:, bass.ds(g * GT, GT)].unsqueeze(2)))
                dve.wait_ge(ranks_psum[f], g + 1)
                own.step(V.tensor_reduce(msum, mask.rearrange("p t e -> p e t"), AX.X, ALU.add))
                own.step(V.tensor_tensor(place, bank[3][:, 0:GT * E].rearrange("p (t e) -> p t e", e=E),
                                         region_at.unsqueeze(1).to_broadcast([P, GT, E]), ALU.add))
                own.settle()
                V.tensor_tensor(carry, carry, msum, ALU.add).then_inc(carry_ready[f], 1)
                own.step(V.tensor_tensor(pl1, place, hot1, ALU.mult))
                own.step(V.tensor_tensor(pl2, place, hot2, ALU.mult))
                own.settle()
                own.step(V.tensor_reduce(slotf[:, 0, :], pl1, AX.X, ALU.add))
                own.step(V.tensor_reduce(slotf[:, 1, :], pl2, AX.X, ALU.add))
                own.settle()
                V.tensor_copy(slot[u], slotf).then_inc(slots_ready[f], 1)

            def tables(f):
                dve.wait_ge(counts_psum[f], 1)
                own.step(V.tensor_copy(cnt, bank[3][:, 0:E]))
                own.settle()
                own.step(V.tensor_copy(cnt_i, cnt))
                own.step(V.tensor_tensor(over, cnt.unsqueeze(2).to_broadcast([P, E, NT]),
                                         cst[:, C_STEP:C_STEP + NT].unsqueeze(1).to_broadcast([P, E, NT]), ALU.is_gt))
                own.settle()
                own.step(V.tensor_reduce(ntile, over, AX.X, ALU.add))
                own.settle()
                own.step(V.tensor_tensor_scan(tend, ntile, zero8, 0.0, ALU.add, ALU.add))
                own.settle()
                own.step(V.tensor_tensor(ge_tab, cst[:, C_J:C_J + TILES].unsqueeze(2).to_broadcast([P, TILES, E]),
                                         tend.unsqueeze(1).to_broadcast([P, TILES, E]), ALU.is_ge))
                own.settle()
                own.step(V.tensor_reduce(texp, ge_tab, AX.X, ALU.add))
                own.settle()
                own.step(V.tensor_tensor(ge_tab, ge_tab, ntile.unsqueeze(1).to_broadcast([P, TILES, E]), ALU.mult))
                own.settle()
                own.step(V.tensor_reduce(tfirst, ge_tab, AX.X, ALU.add))
                own.settle()
                own.step(V.tensor_tensor(tfirst, cst[:, C_J:C_J + TILES], tfirst, ALU.subtract))
                own.step(V.tensor_scalar(trow, texp, float(REGION), None, ALU.mult))
                own.settle()
                own.step(V.scalar_tensor_tensor(trow, tfirst, float(P), trow, ALU.mult, ALU.add))
                own.step(V.tensor_scalar(texp, texp, float(E - 1), float(WEXP), ALU.min, ALU.mult))
                own.settle()
                own.step(V.tensor_copy(row_tab, trow))
                V.tensor_copy(wcol_tab, texp).then_inc(tables_ready[f], 1)

            def moe(f):
                def xt(t, c, v):
                    dve.wait_ge(xt_psum[f], t + 1)
                    V.tensor_copy(xT[v].rearrange("p c n -> p (c n)"), bank[0][:, 0:D]).then_inc(xt_sb[f], 1)

                def multiply(t):
                    dve.wait_ge(h1_psum[f], t + 1)
                    dve.wait_ge(silu_ready[f], t + 1)
                    V.tensor_tensor(inter, gated, bank[5][:, :], ALU.mult).then_inc(inter_ready[f], 1)

                def keep_tag(t, i, v):
                    dve.wait_ge(added[f][v], i * 16)
                    V.tensor_copy(tag[v].bitcast(I32), xslot[v][:, D:ROW].bitcast(I32)).then_inc(tag_sb[f], 1)

                def scale(t, i, v):
                    dve.wait_ge(y_psum[f], t + 1)
                    dve.wait_ge(tag_sb[f], t + 1)
                    V.tensor_scalar(ysb[v], bank[7][:, 0:D], tag[v][:, 0:1], None, ALU.mult).then_inc(y_sb[f], 1)

                xt(0, 0, 0)
                xt(1, 0, 1)
                multiply(0)
                keep_tag(0, 0, 0)

                def turn(i):
                    for v in range(3):
                        t = i * 3 + 1 + v
                        xt(t + 1, 0, (2 + v) % 3)
                        multiply(t)
                        keep_tag(t, i + (1 + v) // 3, (1 + v) % 3)
                        scale(t - 1, i, v)

                turn(0)
                with dve.Fori(1, TILES // 3 - 1) as i:
                    turn(i)
                n = TILES // 3 - 1
                xt(3 * n + 2, 0, 2)
                multiply(3 * n + 1)
                keep_tag(3 * n + 1, n, 1)
                scale(3 * n, n, 0)
                multiply(3 * n + 2)
                keep_tag(3 * n + 2, n, 2)
                scale(3 * n + 1, n, 1)
                scale(3 * n + 2, n, 2)

            own.step(V.memset(carry, 0.0))
            own.step(V.memset(zero8, 0.0))
            dve.wait_ge(const_in, 48)
            for g in range(NG):
                dve.wait_ge(x_in_sem[g], 16)
                ln_stats(xall[:, g * GT:(g + 1) * GT, :], g * GT, GT, veps_ready[0] if g == NG - 1 else None)
            dve.wait_ge(rstd_ready[0], 1)
            for i in range(NG // 2):
                for u in range(2):
                    route(0, xall[:, (i * 2 + u) * GT:(i * 2 + u + 1) * GT, :], i, u)
            tables(0)
            dve.wait_ge(scaled_w, 1)
            q_rope_w = stage_q.rearrange("p (a h n) -> p a h n", a=PAIRS, h=2)
            for two in range(2):
                src = q_rope_w[:, :, :, HD + two:2 * HD:2]
                for hh in range(2):
                    at = hh * HD
                    V.tensor_copy(wpair[:, :, 0, at + two * HALF:at + (two + 1) * HALF], src[:, :, hh, :])
                    last = V.tensor_scalar(wpair[:, :, 1, at + (1 - two) * HALF:at + (2 - two) * HALF], src[:, :, hh, :],
                                           -1.0 if two else 1.0, None, ALU.mult)
            last.then_inc(wa_ready, 1)
            moe(0)

            own.step(V.memset(vals[:, :, :, HD:VW], 1.0))
            own.step(V.memset(cqT[HD:P, :, :], 0.0))
            for i in range(NG // 2):
                if True:
                    for u in range(2):
                        g = i * 2 + u
                        dve.wait_ge(xattn_in[u], i * 16 + 16)
                        ln_stats(xgroup[u], 0, GT, veps_ready[1])
                        dve.wait_ge(rstd_ready[1], g + 1)
                        ln_rows(1, xgroup[u], 0, g, u)
                        dve.wait_ge(xn_psum[1], g * 2 + 2)
                        V.tensor_copy(xnT[:, 1, :], bank[1][:, :]).then_inc(xn_sb1[1], 1)
                        dve.wait_ge(proj_psum, g + 1)
                        own.step(V.tensor_copy(proj[:, 2:4, :].rearrange("p t n -> p (t n)"), bank[3][:, 0:6 * HD]))
                        own.settle()
                        dve.wait_ge(proj_sb, g + 1)
                        own.step(V.tensor_tensor(psq, proj, proj, ALU.mult))
                        own.settle()
                        own.step(V.tensor_reduce(ssq, psq.rearrange("p t (a n) -> p t a n", a=3), AX.X, ALU.add))
                        own.settle()
                        V.tensor_scalar(rvar, ssq, 1.0 / HD, RMS_EPS, ALU.mult, ALU.add).then_inc(var2_ready, 1)
                        x1, x2 = proj[:, :, HD:2 * HD:2], proj[:, :, HD + 1:2 * HD:2]
                        own.step(V.tensor_tensor(rt[0], x1, kcos, ALU.mult))
                        own.step(V.tensor_tensor(rt[1], x2, ksin, ALU.mult))
                        own.step(V.tensor_tensor(rt[2], x2, kcos, ALU.mult))
                        own.step(V.tensor_tensor(rt[3], x1, ksin, ALU.mult))
                        own.settle()
                        for at in (0, 2 * HD):
                            own.step(V.tensor_tensor(keys[:, :, at:at + HALF], rt[0], rt[1], ALU.subtract))
                            own.step(V.tensor_tensor(keys[:, :, at + HALF:at + HD], rt[2], rt[3], ALU.add))
                        dve.wait_ge(rms_ready, g + 1)
                        r_kv = rrms[:, :, 0:1].to_broadcast([P, GT, HD])
                        own.step(V.tensor_tensor(cqn, proj[:, :, 2 * HD:3 * HD], rrms[:, :, 2:3].to_broadcast([P, GT, HD]), ALU.mult))
                        V.tensor_tensor(vals[:, bass.ds(g, 1), :, 0:HD].rearrange("p a t n -> p (a t) n"),
                                        proj[:, :, 0:HD], r_kv, ALU.mult)
                        V.tensor_tensor(keys[:, :, HD:2 * HD], proj[:, :, 0:HD], r_kv, ALU.mult).then_inc(keys_ready, 1)
                        dve.wait_ge(kT_psum, g + 1)
                        V.tensor_copy(kO[:, bass.ds(g, 1), :].rearrange("p a n -> p (a n)"), bank[5][:, :]).then_inc(kO_sb, 1)

            def row_max(s, k):
                dve.wait_ge(s_psum, s + 1)
                V.tensor_reduce(negmax[:, k % 8:k % 8 + 1], bank[k % 4][:, :], AX.X, ALU.max, negate=True).then_inc(max_ready, 1)

            def ropes(p, which):
                if which == 0:
                    dve.wait_ge(qa_psum, p + 1)
                    dve.wait_ge(q_rope, p)
                    V.tensor_tensor(ropeA, bank[7][:, :], qcos, ALU.mult).then_inc(ropeA_sb, 1)
                else:
                    dve.wait_ge(qb_psum, p + 1)
                    V.tensor_tensor(ropeB, bank[7][:, :], qsin, ALU.mult).then_inc(ropeB_sb, 1)

            def divide(p, par, hh, stored):
                dve.wait_ge(o_psum, p * 8 + 4 * hh + 4)
                if hh == 0:
                    dve.wait_ge(att_stored[par], stored)
                dve.wait_ge(att_ready, p * 2 + hh)
                o_v = bank[6][:, 0:GT * VW].rearrange("p (t n) -> p t n", n=VW)
                own.step(V.reciprocal(rsum.unsqueeze(2), o_v[:, :, HD:VW]))
                own.settle()
                V.tensor_tensor(att[par][:, :, hh * HD:(hh + 1) * HD], o_v[:, :, 0:HD],
                                rsum.unsqueeze(2).to_broadcast([P, GT, HD]), ALU.mult).then_inc(att_ready, 1)

            def pair(p, par, first, last, stored):
                for k in range(8):
                    s = p * 8 + k
                    if k % 2 == 0:
                        dve.wait_ge(pT_psum, s + 1)
                        V.tensor_copy(probT[0], bank[4][:, :]).then_inc(pT_even, 1)
                    if not (last and k >= 6):
                        row_max(s + 2, k + 2)
                    if k == 0 and not first:
                        divide(p - 1, 1 - par, 1, None)
                    if k == 4:
                        divide(p, par, 0, stored)
                    if k == 1 and not last:
                        ropes(p + 1, 0)
                    if k == 2 and not last:
                        ropes(p + 1, 1)

            ropes(0, 0)
            ropes(0, 1)
            row_max(0, 0)
            row_max(1, 1)
            pair(0, 0, True, False, 0)
            pair(1, 1, False, False, 0)
            pair(2, 0, False, False, 16)
            with dve.Fori(0, NPAIR // 2 - 2) as i:
                with own.loop(i, NPAIR // 2 - 2, 4):
                    for v in range(2):
                        pair(i * 2 + 3 + v, 1 - v, False, False, (i + v + 1) * 16)
            pair(NPAIR - 1, 1, False, True, (NPAIR // 2 - 1) * 16)
            divide(NPAIR - 1, 1, 1, None)

            own.step(V.memset(carry, 0.0))
            own.settle()
            for i in range(NG // 2):
                if True:
                    for u in range(2):
                        g = i * 2 + u
                        dve.wait_ge(x2in[u], i * 16 + 16)
                        for j in range(GT):
                            t = g * GT + j
                            dve.wait_ge(aT_psum, t * 2 + 2)
                            V.tensor_copy(attT[j % 2][:, 4:8, :].rearrange("p c n -> p (c n)"), bank[5][:, :]).then_inc(aT_sb1, 1)
                            dve.wait_ge(wo_psum, t + 1)
                            V.tensor_tensor(xgroup[u][:, j, :], xgroup[u][:, j, :], bank[6][:, 0:D], ALU.add).then_inc(x2_ready, 1)
                        dve.wait_ge(x2_ready, g * GT + GT)
                        ln_stats(xgroup[u], 0, GT, veps_ready[2])
                        dve.wait_ge(rstd_ready[2], g + 1)
                        route(1, xgroup[u], i, u)
            tables(1)
            moe(1)

        @block.tensor
        def _(pe):
            mm, tr = nc.tensor.matmul, nc.tensor.transpose

            def xn_transpose(n, g, u):
                pe.wait_ge(xn_ready[n], g + 1)
                for c, freed in ((0, xn_sb0[n]), (1, xn_sb1[n])):
                    pe.wait_ge(freed, g)
                    for j in range(GT):
                        last = tr(bank[c][:, j * P:(j + 1) * P], rows[u][:, j, 0, c * P:(c + 1) * P], ident)
                    last.then_inc(xn_psum[n], 1)
                pe.wait_ge(xn_sb0[n], g + 1)
                pe.wait_ge(xn_sb1[n], g + 1)

            def route(f, i, u):
                g = i * 2 + u
                xn_transpose(2 * f, g, u)
                for j in range(GT):
                    for c in range(KC):
                        last = mm(bank[2][:, j * E:(j + 1) * E], xTr[f][:, c, j * P:(j + 1) * P], gate_sb[:, c, :],
                                  start=(c == 0), stop=(c == KC - 1))
                last.then_inc(logits_psum[f], 1)
                pe.wait_ge(mask_ready[f], g + 1)
                pe.wait_ge(carry_ready[f], g)
                mask2 = mask.rearrange("p t e -> p (t e)")
                mm(bank[3][:, 0:GT * E], upper, mask2, start=True, stop=False)
                for j in range(GT - 1):
                    mm(bank[3][:, (j + 1) * E:GT * E].rearrange("p (t e) -> p t e", e=E), ones,
                       mask[:, j:j + 1, :].to_broadcast([P, GT - 1 - j, E]), start=False, stop=False)
                mm(bank[3][:, 0:GT * E].rearrange("p (t e) -> p t e", e=E), ones,
                   carry.unsqueeze(1).to_broadcast([P, GT, E]), start=False, stop=True).then_inc(ranks_psum[f], 1)

            def counts(f):
                pe.wait_ge(carry_ready[f], NG)
                mm(bank[3][:, 0:E], ones, carry, start=True, stop=True).then_inc(counts_psum[f], 1)

            def moe(f):
                def xt(t, i, v):
                    pe.wait_ge(slots_in[f][v], i * 16)
                    pe.wait_ge(xt_sb[f], t)
                    for c in range(KC):
                        last = tr(bank[0][:, c * P:(c + 1) * P], xslot[v][:, c * P:(c + 1) * P], ident)
                    last.then_inc(xt_psum[f], 1)

                def weights_of(t):
                    return pe.value_load(wcol_tab[0:1, bass.ds(t, 1)], min_val=0, max_val=(E - 1) * WEXP)

                def hidden(t, v, at, part):
                    b, signal = ((bank[4], h0_psum), (bank[5], h1_psum))[part]
                    if part == 0:
                        pe.wait_ge(xt_sb[f], t + 1)
                        pe.wait_ge(silu_ready[f], t)
                    else:
                        pe.wait_ge(inter_ready[f], t)
                    for c in range(KC):
                        last = mm(b[:, :], xT[v][:, c, :], wall[:, bass.ds(at + (part * KC + c) * MLP, MLP)],
                                  start=(c == 0), stop=(c == KC - 1))
                    last.then_inc(signal[f], 1)

                def inner_transpose(t):
                    pe.wait_ge(inter_ready[f], t + 1)
                    pe.wait_ge(it_sb[f], t)
                    for c in range(MC):
                        last = tr(bank[6][:, c * P:(c + 1) * P], inter[:, c * P:(c + 1) * P], ident)
                    last.then_inc(it_psum[f], 1)

                def outer(t, at):
                    pe.wait_ge(it_sb[f], t + 1)
                    pe.wait_ge(y_sb[f], t)
                    for c in range(MC):
                        last = mm(bank[7][:, 0:D], interT[:, c, :], wall[:, bass.ds(at + 2 * KC * MLP + c * D, D)],
                                  start=(c == 0), stop=(c == MC - 1))
                    last.then_inc(y_psum[f], 1)

                pe.wait_ge(tables_ready[f], 1)
                if f == 0:
                    pe.wait_ge(moew_in, 16 * 3 * E)
                xt(0, 1, 0)
                at = weights_of(0)
                hidden(0, 0, at, 0)
                xt(1, 1, 1)
                hidden(0, 0, at, 1)

                def turn(i):
                    for v in range(3):
                        t = i * 3 + 1 + v
                        before, at = weights_of(t - 1), weights_of(t)
                        inner_transpose(t - 1)
                        hidden(t, (1 + v) % 3, at, 0)
                        xt(t + 1, i + 1 + (2 + v) // 3, (2 + v) % 3)
                        hidden(t, (1 + v) % 3, at, 1)
                        outer(t - 1, before)

                turn(0)
                with pe.Fori(1, TILES // 3 - 1) as i:
                    turn(i)
                for t in (TILES - 2, TILES - 1):
                    before, at = weights_of(t - 1), weights_of(t)
                    inner_transpose(t - 1)
                    hidden(t, t % 3, at, 0)
                    if t < TILES - 1:
                        xt(t + 1, TILES // 3, (t + 1) % 3)
                    hidden(t, t % 3, at, 1)
                    outer(t - 1, before)
                inner_transpose(TILES - 1)
                outer(TILES - 1, at)

            pe.wait_ge(const_in, 48)
            for i in range(NG // 2):
                for u in range(2):
                    route(0, i, u)
            counts(0)

            pe.wait_ge(scaled_w, 1)
            pe.wait_ge(tables_ready[0], 1)
            wq_h = stage_q.rearrange("p (h n) -> p h n", h=NH)
            wkv_h = stage_kv.rearrange("p (h n) -> p h n", h=NH)
            for k, src in enumerate((wq_h, wkv_h, wkv_h)):
                at = HD if k == 2 else 0
                for h in range(NH):
                    last = tr(bank[2 * k + h // 8][0:HD, (h % 8) * HD:(h % 8 + 1) * HD], src[:, h, at:at + HD], ident[0:HD, 0:HD])
                    if h % 8 == 7:
                        last.then_inc(wt_psum, 1)
            pe.wait_ge(wt_sb, 6)
            for h in range(NH):
                last = mm(bank[6 + h // 8][0:HD, (h % 8) * HD:(h % 8 + 1) * HD], qnT[:, h, :], knT[:, h, :], start=True, stop=True)
                if h % 8 == 7:
                    last.then_inc(zw_psum, 1)
            for h in range(NH):
                a = h // 2
                last = mm(bank[a // 2][(h % 2) * HD:(h % 2 + 1) * HD, (a % 2) * D:(a % 2 + 1) * D], vT[:, h, :], stage_o[:, h, :],
                          start=True, stop=True)
                if h % 4 == 3:
                    last.then_inc(vo_psum, 1)
            pe.wait_ge(folded_w, 6)
            pe.wait_ge(wa_ready, 1)

            moe(0)

            for i in range(NG // 2):
                for u in range(2):
                    g = i * 2 + u
                    xn_transpose(1, g, u)
                    pe.wait_ge(proj_sb, g)
                    pe.wait_ge(kO_sb, g)
                    for j in range(GT):
                        for c in range(KC):
                            last = mm(bank[2 + j // 2][:, (j % 2) * 3 * HD:(j % 2 + 1) * 3 * HD],
                                      xnT[:, c, j * P:(j + 1) * P], wproj[:, c, :], start=(c == 0), stop=(c == KC - 1))
                    last.then_inc(proj_psum, 1)
                    pe.wait_ge(keys_ready, g + 1)
                    pe.wait_ge(kE_sb, g * 2)
                    for j in range(GT):
                        tr(bank[4][:, j * P:(j + 1) * P], keys[:, j, 0:P], ident)
                        tr(bank[5][:, j * P:(j + 1) * P], keys[:, j, HD:HD + P], ident)
                        last = tr(bank[6][0:HD, j * P:(j + 1) * P], cqn[:, j, :], ident)
                    last.then_inc(kT_psum, 1)

            def flat(v):
                return v.rearrange("p a n -> p (a n)")

            def queries(p, part):
                src = cqT[:, bass.ds(p // PAIRS, 1), :]
                if part == 0:
                    pe.wait_ge(wcur_ready, p + 1)
                    pe.wait_ge(qz_sb, p)
                else:
                    pe.wait_ge((ropeA_sb, ropeB_sb)[part - 1], p + 1)
                mm(bank[7][:, :], wcur[:, part, :], flat(src), start=True, stop=True)\
                    .then_inc((qa_psum, qb_psum, qz_psum)[part], 1)

            def scores(p, par, k):
                hh, qt = k // 4, k % 4
                if k == 0:
                    pe.wait_ge(q_rope, p + 1)
                    pe.wait_ge(qz_sb, p + 1)
                keys_t = (kE, kO)[hh]
                mm(bank[k % 4][:, :], qs[par][hh][:, qt * P:(qt + 1) * P], flat(keys_t[:, bass.ds(p // PAIRS, 1), :]),
                   start=True, stop=True).then_inc(s_psum, 1)

            def transposed(p, k):
                s = p * 8 + k
                pe.wait_ge(exp_ready, s + 1)
                pe.wait_ge((pT_even, pT_odd)[k % 2], p * 4 + k // 2)
                for c in range(GT):
                    last = tr(bank[4 + k % 2][:, c * P:(c + 1) * P], prob[k % 2][:, c * P:(c + 1) * P], ident)
                last.then_inc(pT_psum, 1)

            def attend(p, k):
                hh, qt = k // 4, k % 4
                pe.wait_ge((pT_even, pT_odd)[k % 2], p * 4 + k // 2 + 1)
                if qt == 0:
                    pe.wait_ge(att_ready, p * 2 + hh)
                for c in range(GT):
                    v = vals[:, bass.ds(p // PAIRS, 1), c, :].rearrange("p a n -> p (a n)")
                    last = mm(bank[6][:, qt * VW:(qt + 1) * VW], probT[k % 2][:, c * P:(c + 1) * P], v,
                              start=(c == 0), stop=(c == GT - 1))
                last.then_inc(o_psum, 1)

            def pair(p, par, first, last):
                for k in range(8):
                    transposed(p, k)
                    if k < 6:
                        scores(p, par, k + 2)
                    elif not last:
                        scores(p + 1, 1 - par, k - 6)
                    if k > 0:
                        attend(p, k - 1)
                    elif not first:
                        attend(p - 1, 7)
                    if k in (0, 2, 3) and not last:
                        queries(p + 1, {0: 0, 2: 1, 3: 2}[k])

            pe.wait_ge(kE_sb, 2 * B)
            pe.wait_ge(kO_sb, B)
            for part in range(3):
                queries(0, part)
            scores(0, 0, 0)
            scores(0, 0, 1)
            pair(0, 0, True, False)
            with pe.Fori(0, NPAIR // 2 - 1) as i:
                for v in range(2):
                    pair(i * 2 + 1 + v, 1 - v, False, False)
            pair(NPAIR - 1, 1, False, True)
            attend(NPAIR - 1, 7)

            def att_transpose(g, i, j):
                t = g * GT + j
                pe.wait_ge(attl_in[j % 2], (g * 2 + j // 2 + 1) * 16)
                for half, freed in ((0, aT_sb0), (1, aT_sb1)):
                    pe.wait_ge(freed, t)
                    for c in range(4):
                        last = tr(bank[4 + half][:, c * P:(c + 1) * P], attl[j % 2][:, half * 4 + c, :], ident)
                    last.then_inc(aT_psum, 1)

            for i in range(NG // 2):
                for u in range(2):
                    g = i * 2 + u
                    for j in range(GT):
                        t = g * GT + j
                        att_transpose(g, i, j)
                        pe.wait_ge(aT_sb0, t + 1)
                        pe.wait_ge(aT_sb1, t + 1)
                        pe.wait_ge(x2_ready, t)
                        for a in range(PAIRS):
                            last = mm(bank[6][:, 0:D], attT[j % 2][:, a, :], wvo[:, a, :], start=(a == 0), stop=(a == PAIRS - 1))
                        last.then_inc(wo_psum, 1)
                    route(1, i, u)
            counts(1)
            moe(1)


_INS = ["L0_attn_hidden_states", "L0_attn_wq_a", "L0_attn_q_a_norm_w", "L0_attn_wq_b", "L0_attn_wkv_a",
        "L0_attn_kv_a_norm_w", "L0_attn_wkv_b", "L0_attn_wo", "L0_ffn_gate_kernel", "L0_ffn_w0_kernel",
        "L0_ffn_w1_kernel", "L0_ffn_wo_kernel"]


def kernel(**inputs):
    import concourse.bacc as bacc
    from concourse.bass_utils import run_bass_kernel_spmd

    nc = bacc.Bacc("TRN2", target_bir_lowering=False, num_devices=1)
    const, ids = constants()
    arrays = {name: np.ascontiguousarray(inputs[name]) for name in _INS}
    arrays["const_tables"], arrays["token_ids_in"] = const, ids
    args = [nc.dram_tensor(n, a.shape, mybir.dt.from_np(a.dtype), kind="ExternalInput").ap() for n, a in arrays.items()]
    out = nc.dram_tensor("out", (B, S, D), F32, kind="ExternalOutput").ap()
    build(nc, *args, out)
    r = run_bass_kernel_spmd(nc, [arrays], core_ids=[0])
    return r.results[0]["out"]
```

```python
import math
from contextlib import ExitStack, contextmanager

import numpy as np
import concourse.bass as bass
from concourse import mybir

F32 = mybir.dt.float32
F32R = mybir.dt.float32r
I32 = mybir.dt.int32
U32 = mybir.dt.uint32
ALU = mybir.AluOpType
ACT = mybir.ActivationFunctionType
AX = mybir.AxisListType

P = 128
B, S, D = 4, 512, 256
T = B * S
NT = T // P
GT = S // P
NG = NT // GT
KC = D // P

E, TOPK, MLP = 8, 2, 512
MC = MLP // P
REGION = T + P
TILES = (T * TOPK + E * (P - 1)) // P
SPARE = TILES - T * TOPK // P
ROW = D + 2
SKIP = 1 << 20
WEXP = 2 * KC * MLP + MC * D
WPIECE = WEXP // 3

NH, HD, ROPE = 16, 64, 64
HALF = ROPE // 2
PAIRS = NH // 2
SCALE = (HD + ROPE) ** -0.5
NPAIR = B * PAIRS
LN_EPS, RMS_EPS = 1e-5, 1e-6

F32_SHARED = 13 * S + P
F32R_SHARED = 4 * GT * 3 * HD + 8 * S + 2 * GT * 2 * P + 2 * 3 * P


def rope_tables():
    base, factor, fast, slow, orig, mscale = 10000.0, 40.0, 32.0, 1.0, 512, 0.707
    ex = np.arange(0, ROPE, 2, dtype=np.float64) / ROPE
    extra, inter = 1.0 / base ** ex, 1.0 / (factor * base ** ex)
    corr = lambda rot: ROPE * math.log(orig / (rot * 2 * math.pi)) / (2 * math.log(base))
    low, high = max(math.floor(corr(fast)), 0), min(math.ceil(corr(slow)), ROPE - 1)
    if low == high:
        high = high + 0.001
    ramp = np.clip((np.arange(HALF, dtype=np.float64) - low) / (high - low), 0.0, 1.0)
    freq = inter * ramp + extra * (1.0 - ramp)
    ang = np.outer(np.arange(S, dtype=np.float64), freq)
    m = (0.1 * mscale * math.log(factor) + 1.0) / 1.0
    return (np.cos(ang) * m).astype(np.float32), (np.sin(ang) * m).astype(np.float32)


C_ID, C_UP, C_ONE = 0, P, 2 * P
C_IOTA = 3 * P
C_BASE = C_IOTA + E
C_J = C_BASE + E
C_STEP = C_J + TILES
C_HALF = C_STEP + NT
C_KCOS = C_HALF + NT
C_KSIN = C_KCOS + GT * HALF
C_COS = C_KSIN + GT * HALF
C_SIN = C_COS + S
C_ALL = C_SIN + S


def constants():
    c = np.zeros((P, C_ALL), np.float32)
    c[:, C_ID:C_ID + P] = np.eye(P)
    c[:, C_UP:C_UP + P] = np.triu(np.ones((P, P)), 1)
    c[:, C_ONE:C_ONE + P] = 1.0
    c[:, C_IOTA:C_IOTA + E] = np.arange(E)
    c[:, C_BASE:C_BASE + E] = np.arange(E) * REGION
    c[:, C_J:C_J + TILES] = np.arange(TILES)
    c[:, C_STEP:C_STEP + NT] = np.arange(NT) * P
    c[:, C_HALF:C_HALF + NT] = -0.5
    cos, sin = rope_tables()
    c[:, C_KCOS:C_KSIN] = cos.reshape(GT, P, HALF).transpose(1, 0, 2).reshape(P, -1)
    c[:, C_KSIN:C_COS] = sin.reshape(GT, P, HALF).transpose(1, 0, 2).reshape(P, -1)
    c[:, C_COS:C_SIN] = np.tile(cos.T, (4, 1))
    c[:, C_SIN:C_ALL] = np.tile(sin.T, (4, 1))
    ids = (np.arange(NT)[None, :] * P + np.arange(P)[:, None]).astype(np.int32)
    return c, ids


class Steps:

    def __init__(self, eng, sem):
        self.eng, self.sem, self.done, self.it = eng, sem, 0, 0
        self.per = 0

    @contextmanager
    def loop(self, i, times, per):
        start = self.done
        self.it, self.per = i, per
        yield
        assert self.done - start == per, (self.done - start, per)
        self.it, self.per, self.done = 0, 0, start + times * per

    def step(self, ins):
        ins.then_inc(self.sem, 1)
        self.done += 1

    def settle(self):
        self.eng.wait_ge(self.sem, self.it * self.per + self.done)


def build(nc, x_in, wq_a, qn_w, wq_b, wkv_a, kvn_w, wkv_b, wo, gate, w0, w1, wout, const, ids_in, out):
    xs = nc.dram_tensor("rows_by_expert", [E * REGION + SPARE * P, ROW], F32, kind="Internal").ap()
    xd = nc.dram_tensor("x_after_moe", [T, D], F32, kind="Internal").ap()
    invd = nc.dram_tensor("inverse_sums", [NPAIR, 2 * S], F32, kind="Internal").ap()
    atd = nc.dram_tensor("attended_transposed", [B * PAIRS * P, S], F32, kind="Internal").ap()

    ctx = ExitStack()
    with ctx:
        def sb(name, shape, dt=F32):
            return ctx.enter_context(nc.sbuf_tensor(name, shape, dt))

        def sem(name):
            return ctx.enter_context(nc.semaphore(name))

        def sems(name, n):
            return [sem(f"{name}{k}") for k in range(n)]

        bank = [ctx.enter_context(nc.psum_tensor(f"bank{k}", [P, 512], F32)) for k in range(8)]

        wraw = sb("expert_weights", [P, 2, WEXP])
        whi = sb("expert_weights_high", [P, 2 * WEXP], F32R)
        wlo = sb("expert_weights_low", [P, 2 * WEXP], F32R)
        parts = sb("split_rows_and_inner", [P, 2 * (3 * D + MLP)], F32R)
        cst = sb("constants", [P, C_ALL])
        ids = sb("token_ids", [P, NT], I32)
        gate_sb = sb("gate_weights", [P, KC, E])
        wproj = sb("attention_in_weights", [P, KC, 3 * HD])
        norm_w = sb("latent_norm_weights", [P, 2])
        rows = [sb(f"rows{u}", [P, GT, TOPK, ROW]) for u in range(2)]
        wpair = sb("query_weights", [P, PAIRS, 3, P])
        wvo = sb("value_out_weights", [P, PAIRS, D])
        zrow = sb("empty_rows", [P, ROW])
        small = sb("small", [P, 1056])
        shared_at = -(-nc.sbuf_base // 32) * 32
        shared = sb("shared", [P, F32_SHARED + F32R_SHARED])
        split = nc.alloc_sbuf_tensor_at("shared_split", [P, F32R_SHARED], F32R, offset=shared_at + 4 * F32_SHARED)

        used = [0]

        def tiny(shape, dt=F32):
            n = int(np.prod(shape))
            v = small[:, used[0]:used[0] + n]
            used[0] += n
            assert used[0] <= 1056
            if dt != F32:
                v = v.bitcast(dt)
            names = "abcd"[:len(shape)]
            return v.rearrange(f"p ({' '.join(names)}) -> p {' '.join(names)}", **dict(zip(names, shape)))

        def area(at, shape, parts=P):
            n = int(np.prod(shape))
            v = shared[0:parts, at:at + n]
            names = "abcd"[:len(shape)]
            return v.rearrange(f"p ({' '.join(names)}) -> p {' '.join(names)}", **dict(zip(names, shape)))

        def split_area(t, at, shape):
            n = int(np.prod(shape))
            names = "abcd"[:len(shape)]
            return t[:, at:at + n].rearrange(f"p ({' '.join(names)}) -> p {' '.join(names)}", **dict(zip(names, shape)))

        ident, upper, ones = (cst[:, c:c + P] for c in (C_ID, C_UP, C_ONE))
        iota_e = cst[:, C_IOTA:C_IOTA + E]
        region_at = cst[:, C_BASE:C_BASE + E]
        minus_half = cst[:, C_HALF:C_HALF + NT]
        kcos = cst[:, C_KCOS:C_KSIN].rearrange("p (t c) -> p t c", t=GT)
        ksin = cst[:, C_KSIN:C_COS].rearrange("p (t c) -> p t c", t=GT)
        qcos, qsin = cst[:, C_COS:C_SIN], cst[:, C_SIN:C_ALL]

        stats = tiny([GT, 6])
        mv = tiny([NT, 2])
        veps = tiny([NT])
        rstd = tiny([NT])
        logit = tiny([GT, E])
        top = tiny([GT, 8])
        topi = tiny([GT, 8], U32)
        topf = tiny([GT, TOPK])
        diff = tiny([GT])
        e2 = tiny([GT])
        den = tiny([GT])
        rden = tiny([GT])
        hot1, hot2 = tiny([GT, E]), tiny([GT, E])
        mask = tiny([GT, E])
        msum = tiny([E])
        carry = tiny([E])
        place = tiny([GT, E])
        pl1, pl2 = tiny([GT, E]), tiny([GT, E])
        slotf = tiny([TOPK, GT])
        slot = [tiny([TOPK, GT], U32) for _ in range(2)]
        cnt = tiny([E])
        over = tiny([E, NT])
        ntile = tiny([E])
        tend = tiny([E])
        zero8 = tiny([E])
        cnt_i = tiny([E], I32)
        texp = tiny([TILES])
        tfirst = tiny([TILES])
        trow = tiny([TILES])
        row_tab = tiny([TILES], I32)
        exp_tab = tiny([TILES], I32)
        fresh = tiny([TILES])
        event = tiny([TILES])
        split_tab = tiny([TILES], I32)
        load_tab = tiny([TILES], I32)
        tag = [tiny([2]) for _ in range(3)]
        ssq = tiny([GT, 3])
        rvar = tiny([GT, 3])
        rrms = tiny([GT, 3])
        negmax = tiny([8])
        psum = [tiny([8]) for _ in range(2)]
        pinv = [tiny([8]) for _ in range(2)]

        xgroup = [area(u * GT * D, [GT, D]) for u in range(2)]
        xall = area(0, [NT, D])
        o = NT * D
        stage_q = area(o, [NH * 2 * HD])
        stage_kv = area(o + 2048, [NH * 2 * HD], HD)
        stage_o = area(o + 4096, [NH, D], HD)
        qnT = area(o + 8192, [NH, HD], HD)
        knT = area(o + 9216, [NH, HD], HD)
        vT = area(o + 10240, [NH, HD], HD)
        o = 2 * GT * D
        ge_tab = area(o, [TILES, E])
        o = 2 * GT * D
        xslot = [area(o + k * ROW, [ROW]) for k in range(3)]
        o += 3 * ROW + 2
        gated = area(o, [MLP])
        inter = area(o + MLP, [MLP])
        ysb = [area(o + 2 * MLP + k * D, [D]) for k in range(3)]
        o = 2 * GT * D
        kEh, kOh, cq = (split_area(whi, k * B * S, [B, S]) for k in range(3))
        kEl, kOl = (split_area(wlo, k * B * S, [B, S]) for k in range(2))
        vh, vl = (split_area(wlo, 2 * B * S + k * B * GT * HD, [B, GT, HD]) for k in range(2))
        m = F32_SHARED
        xnT = area(m, [KC, S])
        proj = area(m + 1024, [GT, 3 * HD])
        psq = area(m + 1792, [GT, 3 * HD])
        keys = area(m + 2560, [GT, 3 * HD])
        cqn = area(m + 3328, [GT, P])
        rt = [area(m + 3840 + k * GT * HALF, [GT, HALF]) for k in range(4)]
        prob = [area(k * S, [S]) for k in range(2)]
        ropeA, ropeB, rope = (area((2 + k) * S, [S]) for k in range(3))
        raw, rawl, inv, att = ([area((5 + 2 * n + k) * S, [S]) for k in range(2)] for n in range(4))
        invT = area(13 * S, [P], 8)
        vcur = [split_area(split, par * 2 * GT * 3 * HD, [2, GT, 3 * HD]) for par in range(2)]
        o = 4 * GT * 3 * HD
        qh, ql = ([[split_area(split, o + (4 * k + 2 * par + hh) * S, [S]) for hh in range(2)] for par in range(2)]
                  for k in range(2))
        o += 8 * S
        pTh = [split_area(split, o + k * GT * 2 * P, [GT, 2 * P]) for k in range(2)]
        pTl = [split_area(parts, k * GT * 2 * P, [GT, 2 * P]) for k in range(2)]
        o += 2 * GT * 2 * P
        wch, wcl = (split_area(split, o + k * 3 * P, [3, P]) for k in range(2))
        xTh, xTl = (split_area(parts, k * 3 * D, [3, KC, P]) for k in range(2))
        interTh, interTl = (split_area(parts, 6 * D + k * MLP, [MC, P]) for k in range(2))
        o = 2 * GT * D
        xTr = [wvo[:, 0:KC * S // D, :].rearrange("p a n -> p (a n)").rearrange("p (c n) -> p c n", c=KC),
               area(o, [KC, S])]
        attl = [area(o + 1024 + k * PAIRS * S, [PAIRS, S]) for k in range(2)]

        const_in, x_in_sem = sem("const_in"), sems("x_group_in", NG)
        attw_in, xd_copied = sem("attw_in"), sem("xd_copied")
        zrow_ready = sem("zrow_ready")
        own_v, own_a, own_p = sem("own_v"), sem("own_a"), sem("own_p")
        veps_ready, rstd_ready = sems("veps_ready", 3), sems("rstd_ready", 3)
        xn_ready, xn_psum = sems("xn_ready", 3), sems("xn_psum", 3)
        xn_sb0, xn_sb1 = sems("xn_sb_a", 3), sems("xn_sb_b", 3)
        xn_copied = sems("xn_copied", 2)
        logits_psum, diff_ready, e2_ready = sems("logits_psum", 2), sems("diff_ready", 2), sems("e2_ready", 2)
        mask_ready, ranks_psum = sems("mask_ready", 2), sems("ranks_psum", 2)
        slots_ready = sems("slots_ready", 2)
        scattered = [sems(f"scattered{f}_", 2) for f in range(2)]
        carry_ready, counts_psum, tables_ready, tails_zeroed = sems("carry_ready", 2), sems("counts_psum", 2), sems("tables_ready", 2), sems("tails_zeroed", 2)
        slots_in = [sems(f"slots_in{f}_", 3) for f in range(2)]
        w_in, whi_ready, wlo_ready = sems("expert_in", 2), sems("expert_high", 2), sems("expert_low", 2)
        xth_sb, ith_sb = sems("xt_high_sb", 2), sems("it_high_sb", 2)
        xt_psum, xt_sb = sems("xt_psum", 2), sems("xt_sb", 2)
        h0_psum, h1_psum = sems("h0_psum", 2), sems("h1_psum", 2)
        silu_ready, inter_ready = sems("silu_ready", 2), sems("inter_ready", 2)
        it_psum, it_sb = sems("it_psum", 2), sems("it_sb", 2)
        y_psum, y_sb = sems("y_psum", 2), sems("y_sb", 2)
        tag_sb = sems("tag_sb", 2)
        add_due = sems("add_due", 2)
        added = [sems(f"added{f}_", 3) for f in range(2)]
        scaled_w, fold_psum, wt_sb = sem("scaled_w"), sem("fold_psum"), sem("wt_sb")
        folded_w, wa_ready = sem("folded_w"), sem("wa_ready")
        proj_psum, proj_sb, var2_ready, rms_ready = sem("proj_psum"), sem("proj_sb"), sem("var2_ready"), sem("rms_ready")
        keys_ready, kT_psum = sem("keys_ready"), sem("kT_psum")
        k_high, k_low, v_high, v_low = sem("keys_high"), sem("keys_low"), sem("v_high"), sem("v_low")
        wc_high, wc_low_due, wcur_ready = (sem(f"query_weights_{k}") for k in ("high", "low_due", "ready"))
        qa_psum, qb_psum, qz_psum = sem("qa_psum"), sem("qb_psum"), sem("qz_psum")
        ropeA_sb, ropeB_sb, rope_ready = sem("ropeA_sb"), sem("ropeB_sb"), sem("rope_ready")
        qz_high, qz_low, rope_high, rope_low = sem("qz_high"), sem("qz_low"), sem("rope_high"), sem("rope_low")
        v_filled, vcur_ready = sem("v_filled"), sem("values_ready")
        s_psum, max_ready, exp_ready = sem("s_psum"), sem("max_ready"), sem("exp_ready")
        pT_psum, pT_high, pT_low = sem("pT_psum"), sem("pT_high"), sem("pT_low")
        o_psum, raw_sb, rawl_sb, raw_added = sem("o_psum"), sem("raw_sb"), sem("raw_low_sb"), sem("raw_added")
        pinv_ready, invT_psum, invT_sb, inv_stored = sem("pinv_ready"), sem("invT_psum"), sem("invT_sb"), sem("inv_stored")
        inv_in = sems("inv_in", 2)
        att_ready, att_stored = sem("att_ready"), sems("att_stored", 2)
        attl_in = sems("attl_in", 2)
        wo_psum, x2_ready, out_stored = sem("wo_psum"), sem("x2_ready"), sems("out_stored", 2)

        block = ctx.enter_context(nc.Block())

        def expert_steps(eng, step):
            step(0, 0)
            for k in (1, 2, 3):
                step(0, k)
            with eng.Fori(1, TILES // 3 - 1) as i:
                for k in (1, 2, 3):
                    step(i, k)
            for k in (1, 2):
                step(TILES // 3 - 1, k)

        def head_pairs(eng, pair):
            for p in range(4):
                pair(p, p % 2)
            with eng.Fori(0, (NPAIR - 6) // 2) as i:
                for v in range(2):
                    pair(i * 2 + 4 + v, v)
            for p in (NPAIR - 2, NPAIR - 1):
                pair(p, p % 2)

        def among(p, *these):
            return isinstance(p, int) and p in these

        def is_first(i, k):
            return isinstance(i, int) and (i, k) == (0, 0)

        def is_last(i, k):
            return isinstance(i, int) and 3 * i + k == TILES - 1

        @block.sync
        def _(sp):
            sp.dma_start(cst[:, :], const).then_inc(const_in, 16)
            sp.dma_start(ids[:, :], ids_in).then_inc(const_in, 16)
            sp.dma_start(gate_sb[:, :, :], gate.rearrange("(c p) e -> p c e", p=P)).then_inc(const_in, 16)
            for g in range(NG):
                sp.dma_start(xall[:, g * GT:(g + 1) * GT, :],
                             x_in[g].rearrange("(t p) d -> p t d", p=P)).then_inc(x_in_sem[g], 16)
            sp.dma_start(wproj[:, :, 0:2 * HD], wkv_a.rearrange("(c p) n -> p c n", p=P)).then_inc(attw_in, 16)
            sp.dma_start(wproj[:, :, 2 * HD:3 * HD], wq_a.rearrange("(c p) n -> p c n", p=P)).then_inc(attw_in, 16)
            sp.dma_start(norm_w[0:HD, 1:2], kvn_w.rearrange("(p a) -> p a", a=1)).then_inc(attw_in, 16)
            for k in range(2):
                sp.dma_start(norm_w[k * HD:(k + 1) * HD, 0:1], qn_w.rearrange("(p a) -> p a", a=1)).then_inc(attw_in, 16)
                sp.dma_start(stage_q[k * HD:(k + 1) * HD], wq_b).then_inc(attw_in, 16)
            sp.dma_start(stage_kv, wkv_b).then_inc(attw_in, 16)
            sp.dma_start(stage_o, wo.rearrange("(h v) n -> v h n", v=HD)).then_inc(attw_in, 16)

            def load_expert(f, e):
                to = wraw[:, bass.ds(e % 2, 1), :].rearrange("p a n -> p (a n)")
                for at, w, chunks, n in ((0, w0, KC, MLP), (KC * MLP, w1, KC, MLP), (2 * KC * MLP, wout, MC, D)):
                    sp.dma_start(to[:, at:at + chunks * n].rearrange("p (c n) -> p c n", c=chunks),
                                 w[bass.ds(e, 1)].rearrange("a (c p) n -> p (a c) n", p=P)).then_inc(w_in[f], 16)

            load_expert(0, 0)
            load_expert(0, 1)
            sp.dma_start(xd, x_in.rearrange("b s d -> (b s) d")).then_inc(xd_copied, 16)
            sp.wait_ge(zrow_ready, 2)
            for k in range(SPARE):
                at = E * REGION + k * P
                sp.dma_start(xs[at:at + P, :], zrow[:, :]).then_inc(tails_zeroed[0], 16)

            def moe(f):
                sp.wait_ge(tables_ready[f], 1)
                for e in range(E):
                    n = sp.value_load(cnt_i[0:1, e:e + 1], min_val=0, max_val=T)
                    sp.dma_start(xs[bass.ds(n + e * REGION, P), :], zrow[:, :]).then_inc(tails_zeroed[f], 16)
                sp.wait_ge(tails_zeroed[f], 16 * (E if f else E + SPARE))
                for u in range(2):
                    sp.wait_ge(scattered[f][u], 16 * GT * TOPK * NG // 2)
                sp.wait_ge(wlo_ready[f], 3)
                sp.wait_ge(w_in[f], 2 * 48)
                load_expert(f, 2)

                def load_rows(t, v, again):
                    at = sp.value_load(row_tab[0:1, bass.ds(t, 1)], min_val=0, max_val=E * REGION + (SPARE - 1) * P)
                    if again:
                        sp.wait_ge(tag_sb[f], t - 2)
                    sp.dma_start(xslot[v], xs[bass.ds(at, P), :]).then_inc(slots_in[f][v], 16)

                load_rows(0, 0, False)
                load_rows(1, 1, False)

                def step(i, k):
                    t = i * 3 + k
                    if not isinstance(i, int) or t < TILES - 2:
                        load_rows(t + 2, (k + 2) % 3, not isinstance(i, int) or t > 0)
                    if is_first(i, k):
                        return
                    e = sp.value_load(load_tab[0:1, bass.ds(t, 1)], min_val=0, max_val=E - 2)
                    with sp.If(e > 0):
                        sp.wait_ge(wlo_ready[f], e * 3)
                        sp.wait_ge(w_in[f], e * 48 + 48)
                        load_expert(f, e + 1)

                expert_steps(sp, step)
                for v in range(3):
                    sp.wait_ge(added[f][v], 16 * TILES // 3)

            moe(0)
            for i in range(NG // 2):
                for u in range(2):
                    sp.wait_ge(xn_ready[1], i * 2)
                    sp.dma_start(xgroup[u], xd[bass.ds((i * 2 + u) * S, S), :]
                                 .rearrange("(t p) d -> p t d", p=P)).then_inc(x_in_sem[u], 16)
            def store(p, par, ready):
                at = sp.snap(p * P) if not isinstance(p, int) else p * P
                sp.wait_ge(att_ready, ready)
                sp.dma_start(atd[bass.ds(at, P), :], att[par]).then_inc(att_stored[par], 16)

            def spread(p, par):
                at = p if isinstance(p, int) else sp.snap(p)
                sp.wait_ge(invT_sb, p + 1)
                sp.dma_start(invd[bass.ds(at, 1), :].rearrange("a (k q) -> (a k) q", k=8), invT).then_inc(inv_stored, 16)
                sp.wait_ge(inv_stored, (p + 1) * 16)
                for hh in range(2):
                    sp.dma_start(inv[par][hh * HD:(hh + 1) * HD], invd[bass.ds(at, 1), hh * S:(hh + 1) * S].to_broadcast([HD, S])).then_inc(inv_in[par], 16)

            spread(0, 0)
            spread(1, 1)
            with sp.Fori(0, NPAIR // 2 - 1) as i:
                for v in range(2):
                    store(i * 2 + v, v, i * 2 + v + 1)
                    spread(i * 2 + v + 2, v)
            for v in range(2):
                store(NPAIR - 2 + v, v, NPAIR - 1 + v)
            for v in range(2):
                sp.wait_ge(att_stored[v], 16 * NPAIR // 2)
            sp.wait_ge(wlo_ready[0], 3 * E)
            load_expert(1, 0)
            load_expert(1, 1)
            for i in range(NG // 2):
                for u in range(2):
                    g = i * 2 + u
                    sp.wait_ge(out_stored[u], i * 16)
                    sp.wait_ge(xn_ready[2], i * 2)
                    sp.dma_start(xgroup[u], xd[bass.ds(g * S, S), :]
                                 .rearrange("(t p) d -> p t d", p=P)).then_inc(x_in_sem[u], 16)
                    sp.wait_ge(wo_psum, i * 2 * GT)
                    sp.dma_start(attl[u], atd[bass.ds(g * PAIRS * P, PAIRS * P), :]
                                 .rearrange("(a p) s -> p a s", p=P)).then_inc(attl_in[u], 16)
                    sp.wait_ge(x2_ready, g * GT + GT)
                    sp.dma_start(out.rearrange("b s d -> (b s) d")[bass.ds(g * S, S), :]
                                 .rearrange("(t p) d -> p t d", p=P), xgroup[u]).then_inc(out_stored[u], 16)
            moe(1)

        @block.gpsimd
        def _(pool):
            own = Steps(pool, own_p)
            nc.gpsimd.memset(zrow[:, 0:D + 1], 0.0).then_inc(zrow_ready, 1)
            nc.gpsimd.memset(zrow[:, D + 1:ROW].bitcast(I32), SKIP).then_inc(zrow_ready, 1)

            def root(n, at, count):
                nc.gpsimd.tensor_tensor(rstd[:, bass.ds(at, count)], veps[:, bass.ds(at, count)],
                                        minus_half[:, 0:count], ALU.pow).then_inc(rstd_ready[n], 1)

            def scatter(f, i, u):
                pool.wait_ge(slots_ready[f], i * 2 + u + 1)
                pool.wait_ge(xn_copied[f], i * 2 + u + 1)
                for k in range(TOPK):
                    for j in range(GT):
                        nc.gpsimd.indirect_dma_start(
                            out=xs, out_offset=bass.IndirectOffsetOnAxis(ap=slot[u][:, k, j:j + 1], axis=0),
                            in_=rows[u][:, j, k, :], in_offset=None).then_inc(scattered[f][u], 16)

            def add_results(f, dst):

                def turn(i):
                    for v in range(3):
                        pool.wait_ge(y_sb[f], i * 3 + v + 1)
                        prev = (v - 1) % 3
                        pool.wait_ge(added[f][prev], (i + (v > 0)) * 16)
                        pool.sem_inc(add_due[f], 1)
                        nc.gpsimd.indirect_dma_start(
                            out=dst, out_offset=bass.IndirectOffsetOnAxis(
                                ap=tag[v][:, 1:2].bitcast(U32), axis=0),
                            in_=ysb[v], in_offset=None, bounds_check=T - 1, oob_is_err=False,
                            compute_op=ALU.add).then_inc(added[f][v], 16)

                turn(0)
                with pool.Fori(1, TILES // 3) as i:
                    turn(i)

            pool.wait_ge(const_in, 48)
            pool.wait_ge(veps_ready[0], 1)
            root(0, 0, NT)
            for i in range(NG // 2):
                for u in range(2):
                    scatter(0, i, u)
            pool.wait_ge(xd_copied, 16)
            add_results(0, xd)

            for g in range(NG):
                pool.wait_ge(veps_ready[1], g + 1)
                root(1, 0, GT)
                pool.wait_ge(var2_ready, g + 1)
                nc.gpsimd.tensor_tensor(rrms, rvar, minus_half[:, 0:GT * 3].rearrange("p (a b) -> p a b", a=GT),
                                        ALU.pow).then_inc(rms_ready, 1)
                pool.wait_ge(keys_ready, g + 1)
                nc.gpsimd.tensor_copy(vh[:, g, :, :], keys[:, :, HD:2 * HD]).then_inc(v_high, 1)
                pool.wait_ge(v_high, g + 1)
                nc.gpsimd.tensor_tensor(vl[:, g, :, :], keys[:, :, HD:2 * HD], vh[:, g, :, :].bitcast(F32),
                                        ALU.subtract).then_inc(v_low, 1)

            def load_weights(p, used):
                a = p % PAIRS if isinstance(p, int) else pool.snap(p % PAIRS)
                src = wpair[:, bass.ds(a, 1), :, :].rearrange("p a s n -> p (a s) n")
                if used is not None:
                    pool.wait_ge(qz_psum, used)
                nc.gpsimd.tensor_copy(wch, src).then_inc(wc_high, 1)
                pool.wait_ge(wc_high, p + 1)
                pool.sem_inc(wc_low_due, 1)
                nc.gpsimd.tensor_tensor(wcl, src, wch.bitcast(F32), ALU.subtract).then_inc(wcur_ready, 1)

            def load_values(p, par, used):
                if used is not None:
                    pool.wait_ge(o_psum, used)
                high, low = (src[:, bass.ds(p // PAIRS, 1), :, :] for src in (vh, vl))
                nc.gpsimd.tensor_copy(vcur[par][:, :, :, HD:2 * HD], high.to_broadcast([P, 2, GT, HD]))
                nc.gpsimd.tensor_copy(vcur[par][:, 0, :, :].rearrange("p t (n c) -> p t n c", n=3)[:, :, 0:3:2, :],
                                      low.rearrange("p a t n -> p t a n").to_broadcast([P, GT, 2, HD])).then_inc(vcur_ready, 1)

            def rope_sum(p, last_used):
                if last_used:
                    pool.wait_ge(rope_low, p * 2)
                pool.wait_ge(ropeB_sb, p + 1)
                nc.gpsimd.tensor_tensor(rope, ropeA, ropeB, ALU.add).then_inc(rope_ready, 1)


            def rope_lower(p, par):
                for hh in range(2):
                    rows_ = slice(hh * HD, (hh + 1) * HD)
                    pool.wait_ge(rope_high, p * 2 + hh + 1)
                    if hh == 1:
                        pool.wait_ge(rope_low, p * 2 + 1)
                    nc.gpsimd.tensor_tensor(ql[par][hh][rows_], rope[rows_], qh[par][hh][rows_].bitcast(F32),
                                            ALU.subtract).then_inc(rope_low, 1)
                pool.wait_ge(rope_low, p * 2 + 2)

            def add_lower(p, par):
                pool.wait_ge(raw_sb, p * 2 + 2)
                pool.wait_ge(rawl_sb, p * 2 + 2)
                nc.gpsimd.tensor_tensor(raw[par], raw[par], rawl[par], ALU.add).then_inc(raw_added, 1)

            def multiply(p, par, fills, stored):
                if stored is not None:
                    pool.wait_ge(att_stored[par], stored)
                pool.wait_ge(inv_in[par], fills * 32)
                pool.wait_ge(raw_added, p + 1)
                nc.gpsimd.tensor_tensor(att[par], raw[par], inv[par], ALU.mult).then_inc(att_ready, 1)

            pool.wait_ge(folded_w, 2)
            pool.wait_ge(wa_ready, 1)
            pool.wait_ge(k_low, B)
            pool.wait_ge(v_low, B)
            for par in range(2):
                for at in (0, 2 * HD):
                    last = nc.gpsimd.tensor_copy(vcur[par][:, 1, :, at:at + HD],
                                                 zrow[:, 0:HD].unsqueeze(1).to_broadcast([P, GT, HD]))
            last.then_inc(v_filled, 1)
            load_weights(0, None)
            load_values(0, 0, None)
            load_weights(1, 1)
            rope_sum(0, False)
            rope_lower(0, 0)

            def pair(p, par, half):
                last = among(p, NPAIR - 1)
                if not last:
                    rope_sum(p + 1, True)
                if not among(p, 0, 1):
                    multiply(p - 2, par, half, None if among(p, 2, 3) else (half - 1) * 16)
                if not among(p, NPAIR - 2, NPAIR - 1):
                    load_weights(p + 2, p + 2)
                if not last:
                    rope_lower(p + 1, 1 - par)
                if not among(p, 0):
                    add_lower(p - 1, 1 - par)
                if not last:
                    load_values(p + 1, 1 - par, None if among(p, 0) else p * 4)

            for p in range(4):
                pair(p, p % 2, p // 2)
            with pool.Fori(0, (NPAIR - 6) // 2) as i:
                for v in range(2):
                    pair(i * 2 + 4 + v, v, i + 2)
            for p in (NPAIR - 2, NPAIR - 1):
                pair(p, p % 2, p // 2)
            multiply(NPAIR - 2, 0, NPAIR // 2, (NPAIR // 2 - 1) * 16)
            add_lower(NPAIR - 1, 1)
            multiply(NPAIR - 1, 1, NPAIR // 2, (NPAIR // 2 - 1) * 16)

            for i in range(NG // 2):
                for u in range(2):
                    g = i * 2 + u
                    pool.wait_ge(veps_ready[2], g + 1)
                    root(2, 0, GT)
                    scatter(1, i, u)
            for u in range(2):
                pool.wait_ge(out_stored[u], 16 * NG // 2)
            add_results(1, out.rearrange("b s d -> (b s) d"))
            for v in range(3):
                pool.wait_ge(added[1][v], 16 * TILES // 3)

        @block.scalar
        def _(act):
            own = Steps(act, own_a)

            def xn_out(n, g, u, dst, freed, copies):
                if copies:
                    act.wait_ge(xn_ready[n], g + 1)
                    nc.scalar.copy(rows[u][:, :, 1, 0:D], rows[u][:, :, 0, 0:D]).then_inc(xn_copied[n // 2], 1)
                act.wait_ge(xn_psum[n], g * 2 + 1)
                act.wait_ge(freed, g)
                nc.scalar.copy(dst[:, 0, :], bank[0][:, :]).then_inc(xn_sb0[n], 1)

            def route(f, i, u):
                g = i * 2 + u
                xn_out(2 * f, g, u, xTr[f], logits_psum[f], True)
                act.wait_ge(diff_ready[f], g + 1)
                nc.scalar.activation(e2, diff, ACT.Exp).then_inc(e2_ready[f], 1)

            for i in range(NG // 2):
                for u in range(2):
                    route(0, i, u)

            act.wait_ge(attw_in, 16 * 9)
            own.step(nc.scalar.activation(stage_q, stage_q, ACT.Copy, scale=norm_w[:, 0:1]))
            own.step(nc.scalar.activation(stage_kv, stage_kv, ACT.Copy, scale=norm_w[0:HD, 1:2]))
            own.settle()
            nc.scalar.mul(stage_q, stage_q, SCALE).then_inc(scaled_w, 1)
            for k, dst in enumerate((qnT, qnT, knT, knT, vT, vT)):
                act.wait_ge(fold_psum, k + 1)
                nc.scalar.copy(dst[:, (k % 2) * 8:(k % 2) * 8 + 8, :].rearrange("p h n -> p (h n)"),
                               bank[k][0:HD, :]).then_inc(wt_sb, 1)
            for k in range(2):
                act.wait_ge(fold_psum, 6 + k + 1)
                src = bank[6 + k][:, :].rearrange("p (a h n) -> p a h n", a=4, h=2)
                for hh in range(2):
                    last = nc.scalar.copy(wpair[:, 4 * k:4 * k + 4, 2, (1 - hh) * HD:(2 - hh) * HD], src[:, :, hh, :])
                last.then_inc(folded_w, 1)
            for k in range(4):
                act.wait_ge(fold_psum, 8 + k + 1)
                nc.scalar.copy(wvo[:, 2 * k:2 * k + 2, :].rearrange("p a n -> p (a n)"), bank[k][:, :]).then_inc(folded_w, 1)

            def split_high(f, e, piece):
                par = e % 2
                nc.scalar.copy(whi[:, bass.ds(par * WEXP + piece * WPIECE, WPIECE)],
                               wraw[:, bass.ds(par, 1), piece * WPIECE:(piece + 1) * WPIECE]
                               .rearrange("p a n -> p (a n)")).then_inc(whi_ready[f], 1)

            def moe(f):
                def xt_high(t, v):
                    act.wait_ge(xt_psum[f], t + 1)
                    nc.scalar.copy(xTh[:, v, :, :].rearrange("p c n -> p (c n)"), bank[0][:, 0:D]).then_inc(xth_sb[f], 1)

                def it_high(t):
                    act.wait_ge(it_psum[f], t + 1)
                    nc.scalar.copy(interTh[:, :, :].rearrange("p c n -> p (c n)"), bank[6][:, :]).then_inc(ith_sb[f], 1)

                def step(i, k):
                    t = i * 3 + k
                    if is_first(i, k):
                        xt_high(0, 0)
                    else:
                        e = act.value_load(split_tab[0:1, bass.ds(t, 1)], min_val=0, max_val=E - 1)
                        it_high(t - 1)
                        with act.If(e > 0):
                            act.wait_ge(w_in[f], e * 48 + 48)
                            split_high(f, e, 0)
                    act.wait_ge(h0_psum[f], t + 1)
                    nc.scalar.activation(gated, bank[4][:, :], ACT.Silu).then_inc(silu_ready[f], 1)
                    if not is_last(i, k):
                        xt_high(t + 1, (k + 1) % 3)
                    if not is_first(i, k):
                        with act.If(e > 0):
                            split_high(f, e, 1)
                            act.wait_ge(y_psum[f], t)
                            split_high(f, e, 2)

                for e in range(2):
                    act.wait_ge(w_in[f], 48 * 2)
                    for piece in range(3):
                        split_high(f, e, piece)
                act.wait_ge(tables_ready[f], 1)
                expert_steps(act, step)
                it_high(TILES - 1)

            moe(0)

            for i in range(NG // 2):
                for u in range(2):
                    g = i * 2 + u
                    xn_out(1, g, u, xnT, proj_psum, False)
                    act.wait_ge(proj_psum, g + 1)
                    act.wait_ge(keys_ready, g)
                    nc.scalar.copy(proj[:, 0:2, :].rearrange("p t n -> p (t n)"), bank[2][:, 0:6 * HD]).then_inc(proj_sb, 1)
                    act.wait_ge(kT_psum, g + 1)
                    nc.scalar.copy(kEh[:, g, :], bank[4][:, :]).then_inc(k_high, 1)
                    nc.scalar.copy(kOh[:, g, :], bank[5][:, :]).then_inc(k_high, 1)
                    nc.scalar.copy(cq[:, g, :], bank[6][:, :]).then_inc(k_high, 1)

            def exp(s, k, par, first):
                act.wait_ge(max_ready, s + 1)
                if not first:
                    act.wait_ge(pT_psum, s - 1)
                nc.scalar.activation(prob[k % 2], bank[k % 4][:, :], ACT.Exp,
                                     bias=negmax[:, k % 8:k % 8 + 1],
                                     accum_out=psum[par][:, k % 8:k % 8 + 1]).then_inc(exp_ready, 1)

            def high_probs(p, k, first):
                act.wait_ge(pT_psum, p * 8 + k + 1)
                if k % 2 == 0 and not (first and k < 4):
                    act.wait_ge(o_psum, p * 4 + k // 2 - 1)
                nc.scalar.copy(pTh[k // 2 % 2][:, :, (k % 2) * P:(k % 2 + 1) * P],
                               bank[4 + k % 2][:, :].rearrange("p (c n) -> p c n", c=GT)).then_inc(pT_high, 1)

            def queries_latent(p, par, hh):
                act.wait_ge(qz_psum, p + 1)
                rows_ = (slice(HD, P), slice(0, HD))[hh]
                nc.scalar.copy(qh[par][hh][rows_], bank[7][rows_, :]).then_inc(qz_high, 1)

            def queries_rope(p, par, hh):
                act.wait_ge(rope_ready, p + 1)
                rows_ = (slice(0, HD), slice(HD, P))[hh]
                nc.scalar.copy(qh[par][hh][rows_], rope[rows_]).then_inc(rope_high, 1)

            def take_output(p, par, hh):
                rows_ = slice(hh * HD, (hh + 1) * HD)
                act.wait_ge(o_psum, p * 4 + hh * 2 + 2)
                if hh == 0 and not among(p, 0, 1):
                    act.wait_ge(att_ready, p - 1)
                nc.scalar.copy(raw[par][rows_], bank[6][rows_, :]).then_inc(raw_sb, 1)

            def take_inverse(p):
                act.wait_ge(invT_psum, p + 1)
                act.wait_ge(inv_stored, p * 16)
                nc.scalar.copy(invT, bank[7][0:8, 0:P]).then_inc(invT_sb, 1)

            def pair(p, par):
                first, last = among(p, 0), among(p, NPAIR - 1)
                for k in range(8):
                    s = p * 8 + k
                    if k == 2 and not first:
                        take_output(p - 1, 1 - par, 1)
                    if k == 6:
                        take_output(p, par, 0)
                    if not (last and k == 7):
                        exp(s + 1, k + 1, par if k < 7 else 1 - par, first and k < 1)
                    high_probs(p, k, first)
                    if k in ((3, 4) if first else (2, 3)) and not last:
                        queries_latent(p + 1, 1 - par, k - (3 if first else 2))
                    if k in (3, 4) and not last:
                        queries_rope(p + 1, 1 - par, k - 3)
                    if k == 6 and not first:
                        take_inverse(p - 1)

            for hh in range(2):
                queries_latent(0, 0, hh)
            for hh in range(2):
                queries_rope(0, 0, hh)
            exp(0, 0, 0, True)
            head_pairs(act, pair)
            take_output(NPAIR - 1, 1, 1)
            take_inverse(NPAIR - 1)

            for i in range(NG // 2):
                for u in range(2):
                    g = i * 2 + u
                    route(1, i, u)
            moe(1)

        @block.vector
        def _(dve):
            own = Steps(dve, own_v)
            V = nc.vector

            def ln_stats(x, at, tiles, signal):
                for j in range(tiles):
                    own.step(V.bn_stats(stats[:, j, :], x[:, j, :]))
                own.settle()
                for j in range(tiles):
                    own.step(V.bn_aggr(mv[:, bass.ds(at + j, 1), :].rearrange("p a b -> p (a b)"), stats[:, j, :]))
                own.settle()
                ins = V.tensor_scalar(veps[:, bass.ds(at, tiles)],
                                      mv[:, bass.ds(at, tiles), 1:2].rearrange("p a b -> p (a b)"),
                                      LN_EPS, None, ALU.add)
                if signal is None:
                    own.step(ins)
                else:
                    ins.then_inc(signal, 1)

            def ln_rows(n, x, at, g, u):
                for j in range(GT):
                    ins = V.tensor_scalar(rows[u][:, j, 0, 0:D], x[:, j, :],
                                          mv[:, bass.ds(at + j, 1), 0:1].rearrange("p a b -> p (a b)"),
                                          rstd[:, bass.ds(at + j, 1)], ALU.subtract, ALU.mult)
                ins.then_inc(xn_ready[n], 1)

            def route(f, x, i, u):
                g = i * 2 + u
                dve.wait_ge(slots_ready[f], g)
                dve.wait_ge(scattered[f][u], i * (16 * GT * TOPK))
                ln_rows(2 * f, x, g * GT if f == 0 else 0, g, u)
                dve.wait_ge(xn_psum[2 * f], g * 2 + 2)
                V.tensor_copy(xTr[f][:, 1, :], bank[1][:, :]).then_inc(xn_sb1[2 * f], 1)
                dve.wait_ge(logits_psum[f], g + 1)
                own.step(V.tensor_copy(logit.rearrange("p t e -> p (t e)"), bank[2][:, 0:GT * E]))
                own.settle()
                for j in range(GT):
                    own.step(V.max(top[:, j, :], logit[:, j, :]))
                own.settle()
                for j in range(GT):
                    own.step(V.max_index(topi[:, j, :], top[:, j, :], logit[:, j, :]))
                own.settle()
                own.step(V.tensor_copy(topf, topi[:, :, 0:TOPK]))
                V.tensor_tensor(diff.unsqueeze(2), top[:, :, 1:2], top[:, :, 0:1], ALU.subtract).then_inc(diff_ready[f], 1)
                own.settle()
                iota_b = iota_e.unsqueeze(1).to_broadcast([P, GT, E])
                own.step(V.tensor_tensor(hot1, iota_b, topf[:, :, 0:1].to_broadcast([P, GT, E]), ALU.is_equal))
                own.step(V.tensor_tensor(hot2, iota_b, topf[:, :, 1:2].to_broadcast([P, GT, E]), ALU.is_equal))
                own.settle()
                V.tensor_tensor(mask, hot1, hot2, ALU.add).then_inc(mask_ready[f], 1)
                dve.wait_ge(e2_ready[f], g + 1)
                own.step(V.tensor_scalar(den, e2, 1.0, None, ALU.add))
                own.settle()
                own.step(V.reciprocal(rden, den))
                own.settle()
                V.tensor_scalar(rows[u][:, :, 0, D:D + 1], rden.unsqueeze(2), 0.5, None, ALU.mult)
                V.scalar_tensor_tensor(rows[u][:, :, 1, D:D + 1], e2.unsqueeze(2), 0.5, rden.unsqueeze(2),
                                       ALU.mult, ALU.mult)
                for k in range(TOPK):
                    own.step(V.tensor_copy(rows[u][:, :, k, D + 1:ROW].bitcast(I32),
                                           ids[:, bass.ds(g * GT, GT)].unsqueeze(2)))
                dve.wait_ge(ranks_psum[f], g + 1)
                own.step(V.tensor_reduce(msum, mask.rearrange("p t e -> p e t"), AX.X, ALU.add))
                own.step(V.tensor_tensor(place, bank[3][:, 0:GT * E].rearrange("p (t e) -> p t e", e=E),
                                         region_at.unsqueeze(1).to_broadcast([P, GT, E]), ALU.add))
                own.settle()
                V.tensor_tensor(carry, carry, msum, ALU.add).then_inc(carry_ready[f], 1)
                own.step(V.tensor_tensor(pl1, place, hot1, ALU.mult))
                own.step(V.tensor_tensor(pl2, place, hot2, ALU.mult))
                own.settle()
                own.step(V.tensor_reduce(slotf[:, 0, :], pl1, AX.X, ALU.add))
                own.step(V.tensor_reduce(slotf[:, 1, :], pl2, AX.X, ALU.add))
                own.settle()
                V.tensor_copy(slot[u], slotf).then_inc(slots_ready[f], 1)

            def tables(f):
                dve.wait_ge(counts_psum[f], 1)
                own.step(V.tensor_copy(cnt, bank[3][:, 0:E]))
                own.settle()
                own.step(V.tensor_copy(cnt_i, cnt))
                own.step(V.tensor_tensor(over, cnt.unsqueeze(2).to_broadcast([P, E, NT]),
                                         cst[:, C_STEP:C_STEP + NT].unsqueeze(1).to_broadcast([P, E, NT]), ALU.is_gt))
                own.settle()
                own.step(V.tensor_reduce(ntile, over, AX.X, ALU.add))
                own.settle()
                own.step(V.tensor_scalar(ntile, ntile, 1.0, None, ALU.max))
                own.settle()
                own.step(V.tensor_tensor_scan(tend, ntile, zero8, 0.0, ALU.add, ALU.add))
                own.settle()
                own.step(V.tensor_tensor(ge_tab, cst[:, C_J:C_J + TILES].unsqueeze(2).to_broadcast([P, TILES, E]),
                                         tend.unsqueeze(1).to_broadcast([P, TILES, E]), ALU.is_ge))
                own.settle()
                own.step(V.tensor_reduce(texp, ge_tab, AX.X, ALU.add))
                own.settle()
                own.step(V.tensor_tensor(ge_tab, ge_tab, ntile.unsqueeze(1).to_broadcast([P, TILES, E]), ALU.mult))
                own.settle()
                own.step(V.tensor_reduce(tfirst, ge_tab, AX.X, ALU.add))
                own.settle()
                own.step(V.tensor_tensor(tfirst, cst[:, C_J:C_J + TILES], tfirst, ALU.subtract))
                own.step(V.tensor_scalar(trow, texp, float(REGION), None, ALU.mult))
                own.settle()
                own.step(V.scalar_tensor_tensor(trow, tfirst, float(P), trow, ALU.mult, ALU.add))
                own.step(V.tensor_scalar(texp, texp, float(E - 1), None, ALU.min))
                own.settle()
                own.step(V.tensor_copy(row_tab, trow))
                own.step(V.tensor_copy(exp_tab, texp))
                own.step(V.memset(fresh[:, 0:1], 0.0))
                own.step(V.tensor_tensor(fresh[:, 1:TILES], texp[:, 1:TILES], texp[:, 0:TILES - 1], ALU.subtract))
                for ahead, tab in ((1, split_tab), (2, load_tab)):
                    own.settle()
                    own.step(V.tensor_scalar(event, texp, float(E - 1 - ahead), None, ALU.is_le))
                    own.settle()
                    own.step(V.tensor_tensor(event, event, fresh, ALU.mult))
                    own.step(V.tensor_scalar(trow, texp, 1.0, None, ALU.add))
                    own.settle()
                    ins = V.tensor_tensor(tab, trow, event, ALU.mult)
                    if ahead == 1:
                        own.step(ins)
                    else:
                        ins.then_inc(tables_ready[f], 1)

            def split_low(f, e, piece):
                par = e % 2
                dve.wait_ge(whi_ready[f], e * 3 + piece + 1)
                V.tensor_tensor(wlo[:, bass.ds(par * WEXP + piece * WPIECE, WPIECE)],
                                wraw[:, bass.ds(par, 1), piece * WPIECE:(piece + 1) * WPIECE].rearrange("p a n -> p (a n)"),
                                whi[:, bass.ds(par * WEXP + piece * WPIECE, WPIECE)].bitcast(F32),
                                ALU.subtract).then_inc(wlo_ready[f], 1)

            def moe(f):
                def xt_low(t, v):
                    dve.wait_ge(xth_sb[f], t + 1)
                    V.tensor_tensor(xTl[:, v, :, :].rearrange("p c n -> p (c n)"), bank[0][:, 0:D],
                                    xTh[:, v, :, :].rearrange("p c n -> p (c n)").bitcast(F32), ALU.subtract).then_inc(xt_sb[f], 1)

                def it_low(t):
                    dve.wait_ge(ith_sb[f], t + 1)
                    V.tensor_tensor(interTl[:, :, :].rearrange("p c n -> p (c n)"), bank[6][:, :],
                                    interTh[:, :, :].rearrange("p c n -> p (c n)").bitcast(F32), ALU.subtract).then_inc(it_sb[f], 1)

                def multiply(t):
                    dve.wait_ge(h1_psum[f], t + 1)
                    dve.wait_ge(silu_ready[f], t + 1)
                    V.tensor_tensor(inter, gated, bank[5][:, :], ALU.mult).then_inc(inter_ready[f], 1)

                def keep_tag(t, i, k):
                    dve.wait_ge(added[f][k % 3], (i + k // 3) * 16)
                    V.tensor_copy(tag[k % 3].bitcast(I32), xslot[k % 3][:, D:ROW].bitcast(I32)).then_inc(tag_sb[f], 1)

                def scale(t, v):
                    dve.wait_ge(y_psum[f], t + 1)
                    dve.wait_ge(tag_sb[f], t + 1)
                    V.tensor_scalar(ysb[v], bank[7][:, 0:D], tag[v][:, 0:1], None, ALU.mult).then_inc(y_sb[f], 1)

                def step(i, k):
                    t = i * 3 + k
                    if is_first(i, k):
                        xt_low(0, 0)
                    else:
                        e = dve.value_load(split_tab[0:1, bass.ds(t, 1)], min_val=0, max_val=E - 1)
                        it_low(t - 1)
                    if not is_last(i, k):
                        xt_low(t + 1, (k + 1) % 3)
                    if not is_first(i, k):
                        with dve.If(e > 0):
                            split_low(f, e, 0)
                    multiply(t)
                    keep_tag(t, i, k)
                    if not is_first(i, k):
                        scale(t - 1, (k - 1) % 3)
                        with dve.If(e > 0):
                            split_low(f, e, 1)
                            split_low(f, e, 2)

                for e in range(2):
                    for piece in range(3):
                        split_low(f, e, piece)
                dve.wait_ge(tables_ready[f], 1)
                expert_steps(dve, step)
                it_low(TILES - 1)
                scale(TILES - 1, (TILES - 1) % 3)

            own.step(V.memset(carry, 0.0))
            own.step(V.memset(zero8, 0.0))
            dve.wait_ge(const_in, 48)
            for g in range(NG):
                dve.wait_ge(x_in_sem[g], 16)
                ln_stats(xall[:, g * GT:(g + 1) * GT, :], g * GT, GT, veps_ready[0] if g == NG - 1 else None)
            dve.wait_ge(rstd_ready[0], 1)
            for i in range(NG // 2):
                for u in range(2):
                    route(0, xall[:, (i * 2 + u) * GT:(i * 2 + u + 1) * GT, :], i, u)
            tables(0)
            dve.wait_ge(scaled_w, 1)
            q_rope_w = stage_q.rearrange("p (a h n) -> p a h n", a=PAIRS, h=2)
            for two in range(2):
                src = q_rope_w[:, :, :, HD + two:2 * HD:2]
                for hh in range(2):
                    at = hh * HD
                    V.tensor_copy(wpair[:, :, 0, at + two * HALF:at + (two + 1) * HALF], src[:, :, hh, :])
                    last = V.tensor_scalar(wpair[:, :, 1, at + (1 - two) * HALF:at + (2 - two) * HALF], src[:, :, hh, :],
                                           -1.0 if two else 1.0, None, ALU.mult)
            last.then_inc(wa_ready, 1)
            moe(0)

            for i in range(NG // 2):
                if True:
                    for u in range(2):
                        g = i * 2 + u
                        dve.wait_ge(x_in_sem[u], (i + 2) * 16)
                        ln_stats(xgroup[u], 0, GT, veps_ready[1])
                        dve.wait_ge(rstd_ready[1], g + 1)
                        ln_rows(1, xgroup[u], 0, g, u)
                        dve.wait_ge(xn_psum[1], g * 2 + 2)
                        V.tensor_copy(xnT[:, 1, :], bank[1][:, :]).then_inc(xn_sb1[1], 1)
                        dve.wait_ge(proj_psum, g + 1)
                        own.step(V.tensor_copy(proj[:, 2:4, :].rearrange("p t n -> p (t n)"), bank[3][:, 0:6 * HD]))
                        own.settle()
                        dve.wait_ge(proj_sb, g + 1)
                        own.step(V.tensor_tensor(psq, proj, proj, ALU.mult))
                        own.settle()
                        own.step(V.tensor_reduce(ssq, psq.rearrange("p t (a n) -> p t a n", a=3), AX.X, ALU.add))
                        own.settle()
                        V.tensor_scalar(rvar, ssq, 1.0 / HD, RMS_EPS, ALU.mult, ALU.add).then_inc(var2_ready, 1)
                        x1, x2 = proj[:, :, HD:2 * HD:2], proj[:, :, HD + 1:2 * HD:2]
                        own.step(V.tensor_tensor(rt[0], x1, kcos, ALU.mult))
                        own.step(V.tensor_tensor(rt[1], x2, ksin, ALU.mult))
                        own.step(V.tensor_tensor(rt[2], x2, kcos, ALU.mult))
                        own.step(V.tensor_tensor(rt[3], x1, ksin, ALU.mult))
                        own.settle()
                        dve.wait_ge(v_low, g)
                        for at in (0, 2 * HD):
                            own.step(V.tensor_tensor(keys[:, :, at:at + HALF], rt[0], rt[1], ALU.subtract))
                            own.step(V.tensor_tensor(keys[:, :, at + HALF:at + HD], rt[2], rt[3], ALU.add))
                        dve.wait_ge(rms_ready, g + 1)
                        r_kv = rrms[:, :, 0:1].to_broadcast([P, GT, HD])
                        for k in range(2):
                            own.step(V.tensor_tensor(cqn[:, :, k * HD:(k + 1) * HD], proj[:, :, 2 * HD:3 * HD],
                                                     rrms[:, :, 2:3].to_broadcast([P, GT, HD]), ALU.mult))
                        V.tensor_tensor(keys[:, :, HD:2 * HD], proj[:, :, 0:HD], r_kv, ALU.mult).then_inc(keys_ready, 1)
                        for high, low, b in ((kEh, kEl, 4), (kOh, kOl, 5)):
                            dve.wait_ge(k_high, g * 3 + b - 3)
                            V.tensor_tensor(low[:, g, :], bank[b][:, :], high[:, g, :].bitcast(F32), ALU.subtract)
                        dve.wait_ge(k_high, g * 3 + 3)
                        V.tensor_tensor(cq[HD:P, g, :], bank[6][HD:P, :], cq[HD:P, g, :].bitcast(F32),
                                        ALU.subtract).then_inc(k_low, 1)

            def row_max(s, k):
                dve.wait_ge(s_psum, s + 1)
                V.tensor_reduce(negmax[:, k % 8:k % 8 + 1], bank[k % 4][:, :], AX.X, ALU.max, negate=True).then_inc(max_ready, 1)

            def ropes(p, which, first):
                if which == 0:
                    dve.wait_ge(qa_psum, p + 1)
                    if not first:
                        dve.wait_ge(rope_ready, p)
                    V.tensor_tensor(ropeA, bank[7][:, :], qcos, ALU.mult).then_inc(ropeA_sb, 1)
                else:
                    dve.wait_ge(qb_psum, p + 1)
                    V.tensor_tensor(ropeB, bank[7][:, :], qsin, ALU.mult).then_inc(ropeB_sb, 1)

            def latent_lower(p, par, hh):
                rows_ = (slice(HD, P), slice(0, HD))[hh]
                dve.wait_ge(qz_high, p * 2 + 1 + hh)
                V.tensor_tensor(ql[par][hh][rows_], bank[7][rows_, :], qh[par][hh][rows_].bitcast(F32),
                                ALU.subtract).then_inc(qz_low, 1)

            def take_output(p, par, hh):
                rows_, low_rows = slice(hh * HD, (hh + 1) * HD), slice((1 - hh) * HD, (2 - hh) * HD)
                dve.wait_ge(o_psum, p * 4 + hh * 2 + 2)
                if hh == 0 and not among(p, 0, 1):
                    dve.wait_ge(att_ready, p - 1)
                V.tensor_copy(rawl[par][rows_], bank[6][low_rows, :]).then_inc(rawl_sb, 1)

            def low_probs(p, k):
                dve.wait_ge(pT_high, p * 8 + k + 1)
                at = slice((k % 2) * P, (k % 2 + 1) * P)
                V.tensor_tensor(pTl[k // 2 % 2][:, :, at], bank[4 + k % 2][:, :].rearrange("p (c n) -> p c n", c=GT),
                                pTh[k // 2 % 2][:, :, at].bitcast(F32), ALU.subtract).then_inc(pT_low, 1)

            def invert_sums(p, par):
                dve.wait_ge(exp_ready, p * 8 + 8)
                V.reciprocal(pinv[par], psum[par]).then_inc(pinv_ready, 1)

            def pair(p, par):
                first, last = among(p, 0), among(p, NPAIR - 1)
                for k in range(8):
                    if k == 2 and not first:
                        take_output(p - 1, 1 - par, 1)
                    if k == 6:
                        take_output(p, par, 0)
                    if k in ((1, 2) if first else (0, 1)) and not last:
                        ropes(p + 1, k - (1 if first else 0), False)
                    if k in (3, 4) and not last and not first:
                        latent_lower(p + 1, 1 - par, k - 3)
                    if k == 5 and not first:
                        invert_sums(p - 1, 1 - par)
                    if not (last and k >= 6):
                        row_max(p * 8 + k + 2, k + 2)
                    low_probs(p, k)
                    if k in (3, 4) and first:
                        latent_lower(p + 1, 1 - par, k - 3)

            ropes(0, 0, True)
            ropes(0, 1, True)
            latent_lower(0, 0, 0)
            latent_lower(0, 0, 1)
            row_max(0, 0)
            row_max(1, 1)
            head_pairs(dve, pair)
            invert_sums(NPAIR - 1, 1)
            take_output(NPAIR - 1, 1, 1)

            own.step(V.memset(carry, 0.0))
            own.settle()
            for i in range(NG // 2):
                if True:
                    for u in range(2):
                        g = i * 2 + u
                        dve.wait_ge(x_in_sem[u], (i + 4) * 16)
                        for j in range(GT):
                            t = g * GT + j
                            dve.wait_ge(wo_psum, t + 1)
                            V.tensor_tensor(xgroup[u][:, j, :], xgroup[u][:, j, :], bank[6][:, 0:D], ALU.add).then_inc(x2_ready, 1)
                        dve.wait_ge(x2_ready, g * GT + GT)
                        ln_stats(xgroup[u], 0, GT, veps_ready[2])
                        dve.wait_ge(rstd_ready[2], g + 1)
                        route(1, xgroup[u], i, u)
            tables(1)
            moe(1)

        @block.tensor
        def _(pe):
            mm, tr = nc.tensor.matmul, nc.tensor.transpose

            def xn_transpose(n, g, u):
                pe.wait_ge(xn_ready[n], g + 1)
                for c, freed in ((0, xn_sb0[n]), (1, xn_sb1[n])):
                    pe.wait_ge(freed, g)
                    for j in range(GT):
                        last = tr(bank[c][:, j * P:(j + 1) * P], rows[u][:, j, 0, c * P:(c + 1) * P], ident)
                    last.then_inc(xn_psum[n], 1)
                pe.wait_ge(xn_sb0[n], g + 1)
                pe.wait_ge(xn_sb1[n], g + 1)

            def route(f, i, u):
                g = i * 2 + u
                xn_transpose(2 * f, g, u)
                for j in range(GT):
                    for c in range(KC):
                        last = mm(bank[2][:, j * E:(j + 1) * E], xTr[f][:, c, j * P:(j + 1) * P], gate_sb[:, c, :],
                                  start=(c == 0), stop=(c == KC - 1))
                last.then_inc(logits_psum[f], 1)
                pe.wait_ge(mask_ready[f], g + 1)
                pe.wait_ge(carry_ready[f], g)
                mask2 = mask.rearrange("p t e -> p (t e)")
                mm(bank[3][:, 0:GT * E], upper, mask2, start=True, stop=False)
                for j in range(GT - 1):
                    mm(bank[3][:, (j + 1) * E:GT * E].rearrange("p (t e) -> p t e", e=E), ones,
                       mask[:, j:j + 1, :].to_broadcast([P, GT - 1 - j, E]), start=False, stop=False)
                mm(bank[3][:, 0:GT * E].rearrange("p (t e) -> p t e", e=E), ones,
                   carry.unsqueeze(1).to_broadcast([P, GT, E]), start=False, stop=True).then_inc(ranks_psum[f], 1)

            def counts(f):
                pe.wait_ge(carry_ready[f], NG)
                mm(bank[3][:, 0:E], ones, carry, start=True, stop=True).then_inc(counts_psum[f], 1)

            def moe(f):
                def xt(i, k):
                    t, v = i * 3 + k, k % 3
                    pe.wait_ge(slots_in[f][v], (i + k // 3 + 1) * 16)
                    pe.wait_ge(xt_sb[f], t)
                    for c in range(KC):
                        last = tr(bank[0][:, c * P:(c + 1) * P], xslot[v][:, c * P:(c + 1) * P], ident)
                    last.then_inc(xt_psum[f], 1)

                def product(b, xh, xl, at, first, last):
                    n = b.shape[1]
                    mm(b, xh, whi[:, bass.ds(at, n)], start=first, stop=False)
                    mm(b, xh, wlo[:, bass.ds(at, n)], start=False, stop=False)
                    return mm(b, xl, whi[:, bass.ds(at, n)], start=False, stop=last)

                def hidden(t, v, at, part):
                    b, signal = ((bank[4], h0_psum), (bank[5], h1_psum))[part]
                    if part == 0:
                        pe.wait_ge(xt_sb[f], t + 1)
                        pe.wait_ge(silu_ready[f], t)
                    else:
                        pe.wait_ge(inter_ready[f], t)
                    for c in range(KC):
                        last = product(b[:, :], xTh[:, v, c, :], xTl[:, v, c, :], at + (part * KC + c) * MLP,
                                       c == 0, c == KC - 1)
                    last.then_inc(signal[f], 1)

                def inner_transpose(t):
                    pe.wait_ge(inter_ready[f], t + 1)
                    pe.wait_ge(it_sb[f], t)
                    for c in range(MC):
                        last = tr(bank[6][:, c * P:(c + 1) * P], inter[:, c * P:(c + 1) * P], ident)
                    last.then_inc(it_psum[f], 1)

                def outer(t, at):
                    pe.wait_ge(it_sb[f], t + 1)
                    pe.wait_ge(y_sb[f], t)
                    for c in range(MC):
                        last = product(bank[7][:, 0:D], interTh[:, c, :], interTl[:, c, :],
                                       at + 2 * KC * MLP + c * D, c == 0, c == MC - 1)
                    last.then_inc(y_psum[f], 1)

                def expert_of(t):
                    return pe.value_load(exp_tab[0:1, bass.ds(t, 1)], min_val=0, max_val=E - 1)

                def step(i, k):
                    t = i * 3 + k
                    e = expert_of(t)
                    at = pe.snap((e % 2) * WEXP)
                    if not is_first(i, k):
                        before = pe.snap((expert_of(t - 1) % 2) * WEXP)
                        inner_transpose(t - 1)
                    pe.wait_ge(wlo_ready[f], e * 3 + 3)
                    hidden(t, k % 3, at, 0)
                    if not is_last(i, k):
                        xt(i, k + 1)
                    hidden(t, k % 3, at, 1)
                    if not is_first(i, k):
                        outer(t - 1, before)

                pe.wait_ge(tables_ready[f], 1)
                xt(0, 0)
                expert_steps(pe, step)
                inner_transpose(TILES - 1)
                outer(TILES - 1, pe.snap((expert_of(TILES - 1) % 2) * WEXP))

            pe.wait_ge(const_in, 48)
            for i in range(NG // 2):
                for u in range(2):
                    route(0, i, u)
            counts(0)

            pe.wait_ge(scaled_w, 1)
            pe.wait_ge(tables_ready[0], 1)
            wq_h = stage_q.rearrange("p (h n) -> p h n", h=NH)
            wkv_h = stage_kv.rearrange("p (h n) -> p h n", h=NH)
            for k, src in enumerate((wq_h[0:HD], wkv_h, wkv_h)):
                at = HD if k == 2 else 0
                for h in range(NH):
                    last = tr(bank[2 * k + h // 8][0:HD, (h % 8) * HD:(h % 8 + 1) * HD], src[:, h, at:at + HD], ident[0:HD, 0:HD])
                    if h % 8 == 7:
                        last.then_inc(fold_psum, 1)
            pe.wait_ge(wt_sb, 6)
            for h in range(NH):
                for k in range(2):
                    last = mm(bank[6 + h // 8][k * HD:(k + 1) * HD, (h % 8) * HD:(h % 8 + 1) * HD], qnT[:, h, :], knT[:, h, :],
                              start=True, stop=True)
                if h % 8 == 7:
                    last.then_inc(fold_psum, 1)
            for h in range(NH):
                a = h // 2
                last = mm(bank[a // 2][(h % 2) * HD:(h % 2 + 1) * HD, (a % 2) * D:(a % 2 + 1) * D], vT[:, h, :], stage_o[:, h, :],
                          start=True, stop=True)
                if h % 4 == 3:
                    last.then_inc(fold_psum, 1)
            pe.wait_ge(folded_w, 6)
            pe.wait_ge(wa_ready, 1)

            moe(0)

            for i in range(NG // 2):
                for u in range(2):
                    g = i * 2 + u
                    xn_transpose(1, g, u)
                    pe.wait_ge(proj_sb, g)
                    pe.wait_ge(k_low, g)
                    for j in range(GT):
                        for c in range(KC):
                            last = mm(bank[2 + j // 2][:, (j % 2) * 3 * HD:(j % 2 + 1) * 3 * HD],
                                      xnT[:, c, j * P:(j + 1) * P], wproj[:, c, :], start=(c == 0), stop=(c == KC - 1))
                    last.then_inc(proj_psum, 1)
                    pe.wait_ge(keys_ready, g + 1)
                    for j in range(GT):
                        tr(bank[4][:, j * P:(j + 1) * P], keys[:, j, 0:P], ident)
                        tr(bank[5][:, j * P:(j + 1) * P], keys[:, j, HD:HD + P], ident)
                        last = tr(bank[6][:, j * P:(j + 1) * P], cqn[:, j, :], ident)
                    last.then_inc(kT_psum, 1)

            def flat(v):
                return v.rearrange("p a n -> p (a n)")

            def queries(p, part):
                src = flat(cq[:, bass.ds(p // PAIRS, 1), :])
                if part == 0:
                    pe.wait_ge(wcur_ready, p + 1)
                    if not among(p, 0):
                        pe.wait_ge(qz_low, p * 2)
                    if not among(p, 0, 1, 2):
                        pe.wait_ge(invT_sb, p - 2)
                else:
                    pe.wait_ge((ropeA_sb, ropeB_sb)[part - 1], p + 1)
                mm(bank[7][:, :], wch[:, part, :], src, start=True, stop=False)
                mm(bank[7][:, :], wcl[:, part, :], src, start=False, stop=True)\
                    .then_inc((qa_psum, qb_psum, qz_psum)[part], 1)

            def scores(p, par, k):
                hh, qt = k // 4, k % 4
                if k == 0:
                    pe.wait_ge(rope_low, p * 2 + 2)
                    pe.wait_ge(qz_low, p * 2 + 2)
                high, low = (flat(t[:, bass.ds(p // PAIRS, 1), :]) for t in ((kEh, kOh)[hh], (kEl, kOl)[hh]))
                q_high, q_low = (t[par][hh][:, qt * P:(qt + 1) * P] for t in (qh, ql))
                mm(bank[k % 4][:, :], q_high, high, start=True, stop=False)
                mm(bank[k % 4][:, :], q_high, low, start=False, stop=False)
                mm(bank[k % 4][:, :], q_low, high, start=False, stop=True).then_inc(s_psum, 1)

            def transposed(p, k, first):
                s = p * 8 + k
                pe.wait_ge(exp_ready, s + 1)
                if not (first and k < 2):
                    pe.wait_ge(pT_low, s - 1)
                for c in range(GT):
                    last = tr(bank[4 + k % 2][:, c * P:(c + 1) * P], prob[k % 2][:, c * P:(c + 1) * P], ident)
                last.then_inc(pT_psum, 1)

            def attend(p, par, half, piece, first=False):
                hh, at = half // 2, slice((half % 2) * 2 * P, (half % 2 + 1) * 2 * P)
                if piece == 0:
                    if half == 0:
                        pe.wait_ge(vcur_ready, p + 1)
                    pe.wait_ge(pT_low, p * 8 + half * 2 + 2)
                    if half % 2 == 0 and not (first and half == 0):
                        pe.wait_ge(raw_sb, p * 2 + hh)
                        pe.wait_ge(rawl_sb, p * 2 + hh)
                cols = slice((1 - hh) * HD, (1 - hh) * HD + P)
                for c in (2 * piece, 2 * piece + 1):
                    mm(bank[6][:, at], vcur[par][:, 0, c, cols], pTh[half % 2][:, c, :], start=(c == 0), stop=False)
                    last = mm(bank[6][:, at], vcur[par][:, 1, c, cols], pTl[half % 2][:, c, :], start=False, stop=(c == GT - 1))
                if piece == 1:
                    last.then_inc(o_psum, 1)

            def inverse_transpose(p, par):
                pe.wait_ge(pinv_ready, p + 1)
                tr(bank[7][0:8, 0:P], pinv[par], ident).then_inc(invT_psum, 1)

            def pair(p, par):
                first, last = among(p, 0), among(p, NPAIR - 1)
                for k in range(8):
                    transposed(p, k, first)
                    if k < 6:
                        scores(p, par, k + 2)
                    elif not last:
                        scores(p + 1, 1 - par, k - 6)
                    if k > 1:
                        attend(p, par, k // 2 - 1, k % 2, first)
                    elif not first:
                        attend(p - 1, 1 - par, 3, k)
                    if first and k < 2:
                        queries(1, k)
                    if k in ((2,) if first else (0, 1)) and not last:
                        queries(p + 1, 2 if first else k + 1)
                    if k == 5 and not first:
                        if not last:
                            pe.wait_ge(qz_low, p * 2 + 4)
                        inverse_transpose(p - 1, 1 - par)
                    if k == 7 and not among(p, NPAIR - 2, NPAIR - 1):
                        queries(p + 2, 0)

            pe.wait_ge(k_low, B)
            pe.wait_ge(v_filled, 1)
            for part in range(3):
                queries(0, part)
            scores(0, 0, 0)
            scores(0, 0, 1)
            head_pairs(pe, pair)
            pe.wait_ge(invT_sb, NPAIR - 1)
            inverse_transpose(NPAIR - 1, 1)
            for piece in range(2):
                attend(NPAIR - 1, 1, 3, piece)

            for i in range(NG // 2):
                for u in range(2):
                    g = i * 2 + u
                    pe.wait_ge(attl_in[u], i * 16 + 16)
                    for j in range(GT):
                        t = g * GT + j
                        pe.wait_ge(x2_ready, t)
                        for a in range(PAIRS):
                            last = mm(bank[6][:, 0:D], attl[u][:, a, j * P:(j + 1) * P], wvo[:, a, :],
                                      start=(a == 0), stop=(a == PAIRS - 1))
                        last.then_inc(wo_psum, 1)
                    route(1, i, u)
            counts(1)
            moe(1)


_INS = ["L0_attn_hidden_states", "L0_attn_wq_a", "L0_attn_q_a_norm_w", "L0_attn_wq_b", "L0_attn_wkv_a",
        "L0_attn_kv_a_norm_w", "L0_attn_wkv_b", "L0_attn_wo", "L0_ffn_gate_kernel", "L0_ffn_w0_kernel",
        "L0_ffn_w1_kernel", "L0_ffn_wo_kernel"]


def kernel(**inputs):
    import concourse.bacc as bacc
    from concourse.bass_utils import run_bass_kernel_spmd

    nc = bacc.Bacc("TRN2", target_bir_lowering=False, num_devices=1)
    const, ids = constants()
    arrays = {name: np.ascontiguousarray(inputs[name]) for name in _INS}
    arrays["const_tables"], arrays["token_ids_in"] = const, ids
    args = [nc.dram_tensor(n, a.shape, mybir.dt.from_np(a.dtype), kind="ExternalInput").ap() for n, a in arrays.items()]
    out = nc.dram_tensor("out", (B, S, D), F32, kind="ExternalOutput").ap()
    build(nc, *args, out)
    r = run_bass_kernel_spmd(nc, [arrays], core_ids=[0])
    return r.results[0]["out"]
```

```python
import math
from contextlib import ExitStack

import numpy as np
import concourse.bass as bass
from concourse import mybir

F32 = mybir.dt.float32
F32R = mybir.dt.float32r
I32 = mybir.dt.int32
U32 = mybir.dt.uint32
ALU = mybir.AluOpType
ACT = mybir.ActivationFunctionType
AX = mybir.AxisListType

P = 128
B, S, D = 4, 512, 256
T = B * S
NT = T // P
GT = S // P
NG = NT // GT
KC = D // P

E, TOPK, MLP = 8, 2, 512
MC = MLP // P
REGION = T + P
TILES = (T * TOPK + E * (P - 1)) // P
SPARE = TILES - T * TOPK // P
ROW = D + 2
SKIP = 1 << 20
WEXP = 2 * KC * MLP + MC * D
WPIECE = WEXP // 3

NH, HD, ROPE = 16, 64, 64
HALF = ROPE // 2
PAIRS = NH // 2
SCALE = (HD + ROPE) ** -0.5
NPAIR = B * PAIRS
LN_EPS, RMS_EPS = 1e-5, 1e-6

F32_SHARED = 13 * S + P
F32R_SHARED = 4 * GT * 3 * HD + 8 * S + 2 * GT * 2 * P + 2 * 3 * P


def rope_tables():
    base, factor, fast, slow, orig, mscale = 10000.0, 40.0, 32.0, 1.0, 512, 0.707
    ex = np.arange(0, ROPE, 2, dtype=np.float64) / ROPE
    extra, inter = 1.0 / base ** ex, 1.0 / (factor * base ** ex)
    corr = lambda rot: ROPE * math.log(orig / (rot * 2 * math.pi)) / (2 * math.log(base))
    low, high = max(math.floor(corr(fast)), 0), min(math.ceil(corr(slow)), ROPE - 1)
    if low == high:
        high = high + 0.001
    ramp = np.clip((np.arange(HALF, dtype=np.float64) - low) / (high - low), 0.0, 1.0)
    freq = inter * ramp + extra * (1.0 - ramp)
    ang = np.outer(np.arange(S, dtype=np.float64), freq)
    m = (0.1 * mscale * math.log(factor) + 1.0) / 1.0
    return (np.cos(ang) * m).astype(np.float32), (np.sin(ang) * m).astype(np.float32)


C_ID, C_UP, C_ONE = 0, P, 2 * P
C_IOTA = 3 * P
C_BASE = C_IOTA + E
C_J = C_BASE + E
C_STEP = C_J + TILES
C_HALF = C_STEP + NT
C_KCOS = C_HALF + NT
C_KSIN = C_KCOS + GT * HALF
C_COS = C_KSIN + GT * HALF
C_SIN = C_COS + S
C_ALL = C_SIN + S


def constants():
    c = np.zeros((P, C_ALL), np.float32)
    c[:, C_ID:C_ID + P] = np.eye(P)
    c[:, C_UP:C_UP + P] = np.triu(np.ones((P, P)), 1)
    c[:, C_ONE:C_ONE + P] = 1.0
    c[:, C_IOTA:C_IOTA + E] = np.arange(E)
    c[:, C_BASE:C_BASE + E] = np.arange(E) * REGION
    c[:, C_J:C_J + TILES] = np.arange(TILES)
    c[:, C_STEP:C_STEP + NT] = np.arange(NT) * P
    c[:, C_HALF:C_HALF + NT] = -0.5
    cos, sin = rope_tables()
    c[:, C_KCOS:C_KSIN] = cos.reshape(GT, P, HALF).transpose(1, 0, 2).reshape(P, -1)
    c[:, C_KSIN:C_COS] = sin.reshape(GT, P, HALF).transpose(1, 0, 2).reshape(P, -1)
    c[:, C_COS:C_SIN] = np.tile(cos.T, (4, 1))
    c[:, C_SIN:C_ALL] = np.tile(sin.T, (4, 1))
    ids = (np.arange(NT)[None, :] * P + np.arange(P)[:, None]).astype(np.int32)
    return c, ids


class Steps:

    def __init__(self, eng, sem):
        self.eng, self.sem, self.done = eng, sem, 0

    def step(self, ins):
        ins.then_inc(self.sem, 1)
        self.done += 1

    def settle(self):
        self.eng.wait_ge(self.sem, self.done)


def build(nc, x_in, wq_a, qn_w, wq_b, wkv_a, kvn_w, wkv_b, wo, gate, w0, w1, wout, const, ids_in, out):
    xs = nc.dram_tensor("rows_by_expert", [E * REGION + SPARE * P, ROW], F32, kind="Internal").ap()
    xd = nc.dram_tensor("x_after_moe", [T, D], F32, kind="Internal").ap()
    invd = nc.dram_tensor("inverse_sums", [NPAIR, 2 * S], F32, kind="Internal").ap()
    atd = nc.dram_tensor("attended_transposed", [B * PAIRS * P, S], F32, kind="Internal").ap()

    ctx = ExitStack()
    with ctx:
        def sb(name, shape, dt=F32):
            return ctx.enter_context(nc.sbuf_tensor(name, shape, dt))

        def sem(name):
            return ctx.enter_context(nc.semaphore(name))

        def sems(name, n):
            return [sem(f"{name}{k}") for k in range(n)]

        bank = [ctx.enter_context(nc.psum_tensor(f"bank{k}", [P, 512], F32)) for k in range(8)]

        wraw = sb("expert_weights", [P, 2, WEXP])
        whi = sb("expert_weights_high", [P, 2 * WEXP], F32R)
        wlo = sb("expert_weights_low", [P, 2 * WEXP], F32R)
        parts = sb("split_rows_and_inner", [P, 2 * (3 * D + MLP)], F32R)
        cst = sb("constants", [P, C_ALL])
        ids = sb("token_ids", [P, NT], I32)
        gate_sb = sb("gate_weights", [P, KC, E])
        wproj = sb("attention_in_weights", [P, KC, 3 * HD])
        norm_w = sb("latent_norm_weights", [P, 2])
        rows = [sb(f"rows{u}", [P, GT, TOPK, ROW]) for u in range(2)]
        wpair = sb("query_weights", [P, PAIRS, 3, P])
        rows.append(wpair[:, :, :, :].rearrange("p a s n -> p (a s n)")[:, 0:GT * TOPK * ROW]
                    .rearrange("p (t k n) -> p t k n", t=GT, k=TOPK))
        wvo = sb("value_out_weights", [P, PAIRS, D])
        zrow = sb("empty_rows", [P, ROW])
        small = sb("small", [P, 1088])
        shared_at = -(-nc.sbuf_base // 32) * 32
        shared = sb("shared", [P, F32_SHARED + F32R_SHARED])
        split = nc.alloc_sbuf_tensor_at("shared_split", [P, F32R_SHARED], F32R, offset=shared_at + 4 * F32_SHARED)

        used = [0]

        def tiny(shape, dt=F32):
            n = int(np.prod(shape))
            v = small[:, used[0]:used[0] + n]
            used[0] += n
            assert used[0] <= 1088
            if dt != F32:
                v = v.bitcast(dt)
            names = "abcd"[:len(shape)]
            return v.rearrange(f"p ({' '.join(names)}) -> p {' '.join(names)}", **dict(zip(names, shape)))

        def area(at, shape, parts=P):
            n = int(np.prod(shape))
            v = shared[0:parts, at:at + n]
            names = "abcd"[:len(shape)]
            return v.rearrange(f"p ({' '.join(names)}) -> p {' '.join(names)}", **dict(zip(names, shape)))

        def split_area(t, at, shape):
            n = int(np.prod(shape))
            names = "abcd"[:len(shape)]
            return t[:, at:at + n].rearrange(f"p ({' '.join(names)}) -> p {' '.join(names)}", **dict(zip(names, shape)))

        ident, upper, ones = (cst[:, c:c + P] for c in (C_ID, C_UP, C_ONE))
        iota_e = cst[:, C_IOTA:C_IOTA + E]
        region_at = cst[:, C_BASE:C_BASE + E]
        minus_half = cst[:, C_HALF:C_HALF + NT]
        kcos = cst[:, C_KCOS:C_KSIN].rearrange("p (t c) -> p t c", t=GT)
        ksin = cst[:, C_KSIN:C_COS].rearrange("p (t c) -> p t c", t=GT)
        qcos, qsin = cst[:, C_COS:C_SIN], cst[:, C_SIN:C_ALL]

        stats = tiny([GT, 6])
        mv = tiny([NT, 2])
        veps = tiny([NT])
        rstd = tiny([NT])
        logit = tiny([GT, E])
        top = tiny([GT, 8])
        topi = tiny([GT, 8], U32)
        topf = tiny([GT, TOPK])
        diff = tiny([GT])
        e2 = tiny([GT])
        den = tiny([GT])
        rden = tiny([GT])
        hot1, hot2 = tiny([GT, E]), tiny([GT, E])
        mask = tiny([GT, E])
        msum = tiny([E])
        carry = tiny([E])
        place = tiny([GT, E])
        pl1, pl2 = tiny([GT, E]), tiny([GT, E])
        slotf = tiny([TOPK, GT])
        slot = [tiny([TOPK, GT], U32) for _ in range(3)]
        cnt = tiny([E])
        over = tiny([E, NT])
        ntile = tiny([E])
        tend = tiny([E])
        zero8 = tiny([E])
        cnt_i = tiny([E], I32)
        texp = tiny([TILES])
        tfirst = tiny([TILES])
        trow = tiny([TILES])
        row_tab = tiny([TILES], I32)
        exp_tab = tiny([TILES], I32)
        fresh = tiny([TILES])
        event = tiny([TILES])
        split_tab = tiny([TILES], I32)
        load_tab = tiny([TILES], I32)
        tag = [tiny([2]) for _ in range(3)]
        ssq = tiny([GT, 3])
        rvar = tiny([GT, 3])
        rrms = tiny([GT, 3])
        negmax = tiny([8])
        psum = [tiny([8]) for _ in range(2)]
        pinv = [tiny([8]) for _ in range(2)]

        xgroup = [area(u * GT * D, [GT, D]) for u in range(2)]
        xall = area(0, [NT, D])
        o = NT * D
        stage_q = area(o, [NH * 2 * HD])
        stage_kv = area(o + 2048, [NH * 2 * HD], HD)
        stage_o = area(o + 4096, [NH, D], HD)
        qnT = area(o + 8192, [NH, HD], HD)
        knT = area(o + 9216, [NH, HD], HD)
        vT = area(o + 10240, [NH, HD], HD)
        o = 2 * GT * D
        ge_tab = area(o, [TILES, E])
        o = 2 * GT * D
        xslot = [area(o + k * ROW, [ROW]) for k in range(3)]
        o += 3 * ROW + 2
        gated = area(o, [MLP])
        inter = area(o + MLP, [MLP])
        ysb = [area(o + 2 * MLP + k * D, [D]) for k in range(3)]
        kEh, kOh, cq = (split_area(whi, k * B * S, [B, S]) for k in range(3))
        kEl, kOl = (split_area(wlo, k * B * S, [B, S]) for k in range(2))
        vh, vl = (split_area(wlo, 2 * B * S + k * B * GT * HD, [B, GT, HD]) for k in range(2))
        m = F32_SHARED
        xnT = area(m, [KC, S])
        proj = area(m + 1024, [GT, 3 * HD])
        psq = area(m + 1792, [GT, 3 * HD])
        keys = area(m + 2560, [GT, 3 * HD])
        cqn = area(m + 3328, [GT, P])
        rt = [area(m + 3840 + k * GT * HALF, [GT, HALF]) for k in range(4)]
        prob = [area(k * S, [S]) for k in range(2)]
        ropeA, ropeB, rope = (area((2 + k) * S, [S]) for k in range(3))
        raw, rawl, inv, att = ([area((5 + 2 * n + k) * S, [S]) for k in range(2)] for n in range(4))
        invT = area(13 * S, [P], 8)
        o = 0
        qh, ql = ([[split_area(split, o + (4 * k + 2 * par + hh) * S, [S]) for hh in range(2)] for par in range(2)]
                  for k in range(2))
        o += 8 * S
        pTh = [split_area(split, o + k * GT * 2 * P, [GT, 2 * P]) for k in range(2)]
        pTl = [split_area(parts, k * GT * 2 * P, [GT, 2 * P]) for k in range(2)]
        o += 2 * GT * 2 * P
        vcur = [split_area(split, o + par * 2 * GT * 3 * HD, [2, GT, 3 * HD]) for par in range(2)]
        o += 4 * GT * 3 * HD
        wch, wcl = (split_area(split, o + k * 3 * P, [3, P]) for k in range(2))
        xTh, xTl = (split_area(parts, k * 3 * D, [3, KC, P]) for k in range(2))
        interTh, interTl = (split_area(parts, 6 * D + k * MLP, [MC, P]) for k in range(2))
        late = wraw[:, :, :].rearrange("p a n -> p (a n)")
        attl = [late[:, 0:PAIRS * S].rearrange("p (a n) -> p a n", a=PAIRS), area(F32_SHARED, [PAIRS, S])]
        x2group = [late[:, PAIRS * S + k * GT * D:PAIRS * S + (k + 1) * GT * D].rearrange("p (a n) -> p a n", a=GT)
                   for k in range(2)]
        xTr = [wvo[:, 0:KC * S // D, :].rearrange("p a n -> p (a n)").rearrange("p (c n) -> p c n", c=KC),
               area(F32_SHARED + PAIRS * S, [KC, S])]

        const_in, x_in_sem = sem("const_in"), sems("x_group_in", NG)
        attw_in, xd_copied = sem("attw_in"), sem("xd_copied")
        zrow_ready = sem("zrow_ready")
        own_v, own_a = sem("own_v"), sem("own_a")
        veps_ready, rstd_ready = sems("veps_ready", 3), sems("rstd_ready", 3)
        xn_ready, xn_psum = sems("xn_ready", 3), sems("xn_psum", 3)
        xn_sb0, xn_sb1 = sems("xn_sb_a", 3), sems("xn_sb_b", 3)
        xn_copied = sems("xn_copied", 2)
        logits_psum, diff_ready, e2_ready = sems("logits_psum", 2), sems("diff_ready", 2), sems("e2_ready", 2)
        mask_ready, ranks_psum = sems("mask_ready", 2), sems("ranks_psum", 2)
        slots_ready = sems("slots_ready", 2)
        scattered = [sems(f"scattered{f}_", 3) for f in range(2)]
        carry_ready, counts_psum, tables_ready, tails_zeroed = sems("carry_ready", 2), sems("counts_psum", 2), sems("tables_ready", 2), sems("tails_zeroed", 2)
        slots_in = [sems(f"slots_in{f}_", 3) for f in range(2)]
        w_in, whi_ready, wlo_ready = sems("expert_in", 2), sems("expert_high", 2), sems("expert_low", 2)
        xth_sb, ith_sb = sems("xt_high_sb", 2), sems("it_high_sb", 2)
        xt_psum, xt_sb = sems("xt_psum", 2), sems("xt_sb", 2)
        h0_psum, h1_psum = sems("h0_psum", 2), sems("h1_psum", 2)
        silu_ready, inter_ready = sems("silu_ready", 2), sems("inter_ready", 2)
        it_psum, it_sb = sems("it_psum", 2), sems("it_sb", 2)
        y_psum, y_sb = sems("y_psum", 2), sems("y_sb", 2)
        tag_sb = sems("tag_sb", 2)
        add_due = sems("add_due", 2)
        added = [sems(f"added{f}_", 3) for f in range(2)]
        scaled_w, fold_psum, wt_sb = sem("scaled_w"), sem("fold_psum"), sem("wt_sb")
        folded_w, wa_ready = sem("folded_w"), sem("wa_ready")
        proj_psum, proj_sb, var2_ready, rms_ready = sem("proj_psum"), sem("proj_sb"), sem("var2_ready"), sem("rms_ready")
        keys_ready, kT_psum = sem("keys_ready"), sem("kT_psum")
        k_high, k_low, v_split = sem("keys_high"), sem("keys_low"), sem("values_split")
        wc_high, wc_low_due, wcur_ready = (sem(f"query_weights_{k}") for k in ("high", "low_due", "ready"))
        qa_psum, qb_psum, qz_psum = sem("qa_psum"), sem("qb_psum"), sem("qz_psum")
        ropeA_sb, ropeB_sb, rope_ready = sem("ropeA_sb"), sem("ropeB_sb"), sem("rope_ready")
        qz_high, qz_low, rope_high, rope_low = sem("qz_high"), sem("qz_low"), sem("rope_high"), sem("rope_low")
        vcur_ready = sem("values_ready")
        s_psum, max_ready, exp_ready = sem("s_psum"), sem("max_ready"), sem("exp_ready")
        pT_psum, pT_high, pT_low = sem("pT_psum"), sem("pT_high"), sem("pT_low")
        o_psum, raw_sb, rawl_sb, raw_added = sem("o_psum"), sem("raw_sb"), sem("raw_low_sb"), sem("raw_added")
        pinv_ready, invT_psum, invT_sb, inv_stored = sem("pinv_ready"), sem("invT_psum"), sem("invT_sb"), sem("inv_stored")
        inv_in = sems("inv_in", 2)
        att_ready, att_stored = sem("att_ready"), sems("att_stored", 2)
        attl_in = sems("attl_in", 2)
        wo_psum, x2_ready, out_stored = sem("wo_psum"), sem("x2_ready"), sems("out_stored", 2)

        block = ctx.enter_context(nc.Block())

        def expert_steps(eng, step):
            step(0, 0)
            for k in (1, 2, 3):
                step(0, k)
            with eng.Fori(1, TILES // 3 - 1) as i:
                for k in (1, 2, 3):
                    step(i, k)
            for k in (1, 2):
                step(TILES // 3 - 1, k)

        def head_pairs(eng, pair):
            for p in range(4):
                pair(p, p % 2)
            with eng.Fori(0, (NPAIR - 6) // 2) as i:
                for v in range(2):
                    pair(i * 2 + 4 + v, v)
            for p in (NPAIR - 2, NPAIR - 1):
                pair(p, p % 2)

        def among(p, *these):
            return isinstance(p, int) and p in these

        def is_first(i, k):
            return isinstance(i, int) and (i, k) == (0, 0)

        def is_last(i, k):
            return isinstance(i, int) and 3 * i + k == TILES - 1

        @block.sync
        def _(sp):
            sp.dma_start(cst[:, :], const).then_inc(const_in, 16)
            sp.dma_start(ids[:, :], ids_in).then_inc(const_in, 16)
            sp.dma_start(gate_sb[:, :, :], gate.rearrange("(c p) e -> p c e", p=P)).then_inc(const_in, 16)
            for g in range(NG):
                sp.dma_start(xall[:, g * GT:(g + 1) * GT, :],
                             x_in[g].rearrange("(t p) d -> p t d", p=P)).then_inc(x_in_sem[g], 16)
            sp.dma_start(wproj[:, :, 0:2 * HD], wkv_a.rearrange("(c p) n -> p c n", p=P)).then_inc(attw_in, 16)
            sp.dma_start(wproj[:, :, 2 * HD:3 * HD], wq_a.rearrange("(c p) n -> p c n", p=P)).then_inc(attw_in, 16)
            sp.dma_start(norm_w[0:HD, 1:2], kvn_w.rearrange("(p a) -> p a", a=1)).then_inc(attw_in, 16)
            for k in range(2):
                sp.dma_start(norm_w[k * HD:(k + 1) * HD, 0:1], qn_w.rearrange("(p a) -> p a", a=1)).then_inc(attw_in, 16)
                sp.dma_start(stage_q[k * HD:(k + 1) * HD], wq_b).then_inc(attw_in, 16)
            sp.dma_start(stage_kv, wkv_b).then_inc(attw_in, 16)
            sp.dma_start(stage_o, wo.rearrange("(h v) n -> v h n", v=HD)).then_inc(attw_in, 16)

            def load_expert(f, e):
                to = wraw[:, bass.ds(e % 2, 1), :].rearrange("p a n -> p (a n)")
                for at, w, chunks, n in ((0, w0, KC, MLP), (KC * MLP, w1, KC, MLP), (2 * KC * MLP, wout, MC, D)):
                    sp.dma_start(to[:, at:at + chunks * n].rearrange("p (c n) -> p c n", c=chunks),
                                 w[bass.ds(e, 1)].rearrange("a (c p) n -> p (a c) n", p=P)).then_inc(w_in[f], 16)

            load_expert(0, 0)
            load_expert(0, 1)
            sp.dma_start(xd, x_in.rearrange("b s d -> (b s) d")).then_inc(xd_copied, 16)
            sp.wait_ge(zrow_ready, 2)
            for k in range(SPARE):
                at = E * REGION + k * P
                sp.dma_start(xs[at:at + P, :], zrow[:, :]).then_inc(tails_zeroed[0], 16)

            def moe(f):
                sp.wait_ge(tables_ready[f], 1)
                for e in range(E):
                    n = sp.value_load(cnt_i[0:1, e:e + 1], min_val=0, max_val=T)
                    sp.dma_start(xs[bass.ds(n + e * REGION, P), :], zrow[:, :]).then_inc(tails_zeroed[f], 16)
                sp.wait_ge(tails_zeroed[f], 16 * (E if f else E + SPARE))
                for u in range(3):
                    sp.wait_ge(scattered[f][u], 16 * GT * TOPK * ((NG + 2 - u) // 3))
                sp.wait_ge(tables_ready[f], 2)

                def load_rows(t, v, again):
                    at = sp.value_load(row_tab[0:1, bass.ds(t, 1)], min_val=0, max_val=E * REGION + (SPARE - 1) * P)
                    if again:
                        sp.wait_ge(tag_sb[f], t - 2)
                    sp.dma_start(xslot[v], xs[bass.ds(at, P), :]).then_inc(slots_in[f][v], 16)

                load_rows(0, 0, False)
                load_rows(1, 1, False)
                sp.wait_ge(wlo_ready[f], 3)
                sp.wait_ge(w_in[f], 2 * 48)
                load_expert(f, 2)

                def step(i, k):
                    t = i * 3 + k
                    if not isinstance(i, int) or t < TILES - 2:
                        load_rows(t + 2, (k + 2) % 3, not isinstance(i, int) or t > 0)
                    if is_first(i, k):
                        return
                    e = sp.value_load(load_tab[0:1, bass.ds(t, 1)], min_val=0, max_val=E - 2)
                    with sp.If(e > 0):
                        sp.wait_ge(wlo_ready[f], e * 3)
                        sp.wait_ge(w_in[f], e * 48 + 48)
                        load_expert(f, e + 1)

                expert_steps(sp, step)
                for v in range(3):
                    sp.wait_ge(added[f][v], 16 * TILES // 3)

            moe(0)
            for i in range(NG // 2):
                for u in range(2):
                    sp.wait_ge(xn_ready[1], i * 2)
                    sp.dma_start(xgroup[u], xd[bass.ds((i * 2 + u) * S, S), :]
                                 .rearrange("(t p) d -> p t d", p=P)).then_inc(x_in_sem[u], 16)
            def store(p, par, ready):
                at = sp.snap(p * P) if not isinstance(p, int) else p * P
                sp.wait_ge(att_ready, ready)
                sp.dma_start(atd[bass.ds(at, P), :], att[par]).then_inc(att_stored[par], 16)

            def spread(p, par):
                at = p if isinstance(p, int) else sp.snap(p)
                sp.wait_ge(invT_sb, p + 1)
                sp.dma_start(invd[bass.ds(at, 1), :].rearrange("a (k q) -> (a k) q", k=8), invT).then_inc(inv_stored, 16)
                sp.wait_ge(inv_stored, (p + 1) * 16)
                for hh in range(2):
                    sp.dma_start(inv[par][hh * HD:(hh + 1) * HD], invd[bass.ds(at, 1), hh * S:(hh + 1) * S].to_broadcast([HD, S])).then_inc(inv_in[par], 16)

            spread(0, 0)
            spread(1, 1)
            def turn(i):
                for v in range(2):
                    store(i * 2 + v, v, i * 2 + v + 1)
                    spread(i * 2 + v + 2, v)

            with sp.Fori(0, NPAIR // 2 - 2) as i:
                turn(i)

            def load_x(g):
                if g > 1:
                    sp.wait_ge(out_stored[g % 2], 16)
                    sp.wait_ge(xn_ready[2], g - 1)
                sp.dma_start(x2group[g % 2], xd[g * S:(g + 1) * S, :]
                             .rearrange("(t p) d -> p t d", p=P)).then_inc(x_in_sem[g % 2], 16)

            def load_attended(g):
                if g > 1:
                    sp.wait_ge(wo_psum, (g - 1) * GT)
                for v in range(2):
                    sp.wait_ge(att_stored[v], 16 * (g + 1) * PAIRS // 2)
                sp.dma_start(attl[g % 2], atd[g * PAIRS * P:(g + 1) * PAIRS * P, :]
                             .rearrange("(a p) s -> p a s", p=P)).then_inc(attl_in[g % 2], 16)

            load_x(0)
            load_attended(0)
            load_x(1)
            turn(NPAIR // 2 - 2)
            sp.wait_ge(o_psum, NPAIR * 4)
            load_attended(1)
            for v in range(2):
                store(NPAIR - 2 + v, v, NPAIR - 1 + v)
            for g in range(NG):
                sp.wait_ge(x2_ready, g * GT + GT)
                sp.dma_start(out[g].rearrange("(t p) d -> p t d", p=P), x2group[g % 2]).then_inc(out_stored[g % 2], 16)
                if g + 2 < NG:
                    load_attended(g + 2)
                    load_x(g + 2)
            for u in range(2):
                sp.wait_ge(out_stored[u], 16 * NG // 2)
            sp.wait_ge(xn_ready[2], NG)
            load_expert(1, 0)
            load_expert(1, 1)
            moe(1)

        @block.gpsimd
        def _(pool):
            nc.gpsimd.memset(zrow[:, 0:D + 1], 0.0).then_inc(zrow_ready, 1)
            nc.gpsimd.memset(zrow[:, D + 1:ROW].bitcast(I32), SKIP).then_inc(zrow_ready, 1)

            def root(n, at, count):
                nc.gpsimd.tensor_tensor(rstd[:, bass.ds(at, count)], veps[:, bass.ds(at, count)],
                                        minus_half[:, 0:count], ALU.pow).then_inc(rstd_ready[n], 1)

            def scatter(f, g):
                u = g % 3
                pool.wait_ge(slots_ready[f], g + 1)
                pool.wait_ge(xn_copied[f], g + 1)
                for k in range(TOPK):
                    for j in range(GT):
                        nc.gpsimd.indirect_dma_start(
                            out=xs, out_offset=bass.IndirectOffsetOnAxis(ap=slot[u][:, k, j:j + 1], axis=0),
                            in_=rows[u][:, j, k, :], in_offset=None).then_inc(scattered[f][u], 16)

            def add_results(f, dst):

                def turn(i):
                    for v in range(3):
                        pool.wait_ge(y_sb[f], i * 3 + v + 1)
                        prev = (v - 1) % 3
                        pool.wait_ge(added[f][prev], (i + (v > 0)) * 16)
                        pool.sem_inc(add_due[f], 1)
                        nc.gpsimd.indirect_dma_start(
                            out=dst, out_offset=bass.IndirectOffsetOnAxis(
                                ap=tag[v][:, 1:2].bitcast(U32), axis=0),
                            in_=ysb[v], in_offset=None, bounds_check=T - 1, oob_is_err=False,
                            compute_op=ALU.add).then_inc(added[f][v], 16)

                turn(0)
                with pool.Fori(1, TILES // 3) as i:
                    turn(i)

            pool.wait_ge(const_in, 48)
            for g in range(NG):
                pool.wait_ge(veps_ready[0], g + 1)
                root(0, g * GT, GT)
            for g in range(NG):
                scatter(0, g)
            pool.wait_ge(xd_copied, 16)
            add_results(0, xd)

            def load_weights(p, used):
                a = p % PAIRS if isinstance(p, int) else pool.snap(p % PAIRS)
                src = wpair[:, bass.ds(a, 1), :, :].rearrange("p a s n -> p (a s) n")
                if used is not None:
                    pool.wait_ge(qz_psum, used)
                nc.gpsimd.tensor_copy(wch, src).then_inc(wc_high, 1)
                pool.wait_ge(wc_high, p + 1)
                pool.sem_inc(wc_low_due, 1)
                nc.gpsimd.tensor_tensor(wcl, src, wch.bitcast(F32), ALU.subtract).then_inc(wcur_ready, 1)

            def load_values(p, par, used):
                if used is not None:
                    pool.wait_ge(o_psum, used)
                high, low = (src[:, bass.ds(p // PAIRS, 1), :, :] for src in (vh, vl))
                nc.gpsimd.tensor_copy(vcur[par][:, :, :, HD:2 * HD], high.to_broadcast([P, 2, GT, HD]))
                nc.gpsimd.tensor_copy(vcur[par][:, 0, :, :].rearrange("p t (n c) -> p t n c", n=3)[:, :, 0:3:2, :],
                                      low.rearrange("p a t n -> p t a n").to_broadcast([P, GT, 2, HD])).then_inc(vcur_ready, 1)

            def rope_sum(p):
                if not among(p, 0):
                    pool.wait_ge(rope_low, p * 2)
                pool.wait_ge(ropeB_sb, p + 1)
                nc.gpsimd.tensor_tensor(rope, ropeA, ropeB, ALU.add).then_inc(rope_ready, 1)

            def rope_lower(p, par):
                for hh in range(2):
                    rows_ = slice(hh * HD, (hh + 1) * HD)
                    pool.wait_ge(rope_high, p * 2 + hh + 1)
                    if hh == 1:
                        pool.wait_ge(rope_low, p * 2 + 1)
                    nc.gpsimd.tensor_tensor(ql[par][hh][rows_], rope[rows_], qh[par][hh][rows_].bitcast(F32),
                                            ALU.subtract).then_inc(rope_low, 1)
                pool.wait_ge(rope_low, p * 2 + 2)

            def add_lower(p, par):
                pool.wait_ge(raw_sb, p * 2 + 2)
                pool.wait_ge(rawl_sb, p * 2 + 2)
                nc.gpsimd.tensor_tensor(raw[par], raw[par], rawl[par], ALU.add).then_inc(raw_added, 1)

            def multiply(p, par, fills, stored):
                if stored is not None:
                    pool.wait_ge(att_stored[par], stored)
                pool.wait_ge(inv_in[par], fills * 32)
                pool.wait_ge(raw_added, p + 1)
                nc.gpsimd.tensor_tensor(att[par], raw[par], inv[par], ALU.mult).then_inc(att_ready, 1)

            pool.wait_ge(folded_w, 2)
            pool.wait_ge(wa_ready, 1)
            for par in range(2):
                for at in (0, 2 * HD):
                    last = nc.gpsimd.tensor_copy(vcur[par][:, 1, :, at:at + HD],
                                                 zrow[:, 0:HD].unsqueeze(1).to_broadcast([P, GT, HD]))
            last.then_inc(v_split, 1)
            load_weights(0, None)

            for g in range(2):
                pool.wait_ge(veps_ready[1], g + 1)
                root(1, 0, GT)
            for g in range(NG):
                pool.wait_ge(var2_ready, g + 1)
                nc.gpsimd.tensor_tensor(rrms, rvar, minus_half[:, 0:GT * 3].rearrange("p (a b) -> p a b", a=GT),
                                        ALU.pow).then_inc(rms_ready, 1)
                if g + 2 < NG:
                    pool.wait_ge(veps_ready[1], g + 3)
                    root(1, 0, GT)
                pool.wait_ge(keys_ready, g + 1)
                nc.gpsimd.tensor_copy(vh[:, g, :, :], keys[:, :, HD:2 * HD]).then_inc(v_split, 1)
                pool.wait_ge(v_split, g * 2 + 2)
                nc.gpsimd.tensor_tensor(vl[:, g, :, :], keys[:, :, HD:2 * HD], vh[:, g, :, :].bitcast(F32),
                                        ALU.subtract).then_inc(v_split, 1)
                if g == 0:
                    pool.wait_ge(v_split, 3)
                    load_values(0, 0, None)

            load_weights(1, 1)
            rope_sum(0)
            rope_lower(0, 0)

            def pair(p, par, half):
                last = among(p, NPAIR - 1)
                if not last:
                    rope_sum(p + 1)
                if not among(p, 0, 1):
                    multiply(p - 2, par, half, None if among(p, 2, 3) else (half - 1) * 16)
                if not among(p, NPAIR - 2, NPAIR - 1):
                    load_weights(p + 2, p + 2)
                if not last:
                    rope_lower(p + 1, 1 - par)
                if not among(p, 0):
                    add_lower(p - 1, 1 - par)
                if not last:
                    load_values(p + 1, 1 - par, None if among(p, 0) else p * 4)

            for p in range(4):
                pair(p, p % 2, p // 2)
            with pool.Fori(0, (NPAIR - 6) // 2) as i:
                for v in range(2):
                    pair(i * 2 + 4 + v, v, i + 2)
            for p in (NPAIR - 2, NPAIR - 1):
                pair(p, p % 2, p // 2)
            multiply(NPAIR - 2, 0, NPAIR // 2, (NPAIR // 2 - 1) * 16)
            add_lower(NPAIR - 1, 1)
            multiply(NPAIR - 1, 1, NPAIR // 2, (NPAIR // 2 - 1) * 16)

            pool.wait_ge(veps_ready[2], 1)
            root(2, 0, GT)
            for g in range(NG):
                if g + 1 < NG:
                    pool.wait_ge(veps_ready[2], g + 2)
                    root(2, 0, GT)
                scatter(1, g)
            for u in range(2):
                pool.wait_ge(out_stored[u], 16 * NG // 2)
            add_results(1, out.rearrange("b s d -> (b s) d"))
            for v in range(3):
                pool.wait_ge(added[1][v], 16 * TILES // 3)

        @block.scalar
        def _(act):
            own = Steps(act, own_a)

            def copy_rows(f, g):
                act.wait_ge(xn_ready[2 * f], g + 1)
                nc.scalar.copy(rows[g % 3][:, :, 1, 0:D], rows[g % 3][:, :, 0, 0:D]).then_inc(xn_copied[f], 1)

            def xt_out(n, g, dst, freed):
                act.wait_ge(xn_psum[n], g * 2 + 1)
                act.wait_ge(freed, g)
                nc.scalar.copy(dst[:, 0, :], bank[0][:, :]).then_inc(xn_sb0[n], 1)

            def choice_exp(f, g):
                act.wait_ge(diff_ready[f], g + 1)
                nc.scalar.activation(e2, diff, ACT.Exp).then_inc(e2_ready[f], 1)

            def fold_out(k, b, dst):
                for half in range(2):
                    act.wait_ge(fold_psum, 2 * k + half + 1)
                    nc.scalar.copy(dst[:, half * 8:half * 8 + 8, :].rearrange("p h n -> p (h n)"),
                                   bank[b + half][0:HD, :]).then_inc(wt_sb, 1)

            copy_rows(0, 0)
            xt_out(0, 0, xTr[0], logits_psum[0])
            for g in range(NG):
                if g + 1 < NG:
                    copy_rows(0, g + 1)
                choice_exp(0, g)
                if g + 1 < NG:
                    xt_out(0, g + 1, xTr[0], logits_psum[0])
                if g == 0:
                    act.wait_ge(attw_in, 16 * 9)
                    nc.scalar.activation(stage_kv, stage_kv, ACT.Copy, scale=norm_w[0:HD, 1:2]).then_inc(scaled_w, 1)
                    own.step(nc.scalar.mul(norm_w[:, 0:1], norm_w[:, 0:1], SCALE))
                    own.settle()
                elif g == 1:
                    nc.scalar.activation(stage_q, stage_q, ACT.Copy, scale=norm_w[:, 0:1]).then_inc(scaled_w, 1)
                elif g == 2:
                    fold_out(0, 6, knT)
            fold_out(1, 4, vT)
            fold_out(2, 6, qnT)
            act.wait_ge(scattered[0][2], 16 * GT * TOPK)

            def split_high(f, e, piece):
                par = e % 2
                nc.scalar.copy(whi[:, bass.ds(par * WEXP + piece * WPIECE, WPIECE)],
                               wraw[:, bass.ds(par, 1), piece * WPIECE:(piece + 1) * WPIECE]
                               .rearrange("p a n -> p (a n)")).then_inc(whi_ready[f], 1)

            act.wait_ge(w_in[0], 48 * 2)
            for k in range(2):
                act.wait_ge(fold_psum, 6 + k + 1)
                src = bank[6 + k][:, :].rearrange("p (a h n) -> p a h n", a=4, h=2)
                for hh in range(2):
                    last = nc.scalar.copy(wpair[:, 4 * k:4 * k + 4, 2, (1 - hh) * HD:(2 - hh) * HD], src[:, :, hh, :])
                last.then_inc(folded_w, 1)
                split_high(0, 0, k)
            for k in range(4):
                act.wait_ge(fold_psum, 8 + k + 1)
                nc.scalar.copy(wvo[:, 2 * k:2 * k + 2, :].rearrange("p a n -> p (a n)"), bank[k][:, :]).then_inc(folded_w, 1)
                split_high(0, (2 + k) // 3, (2 + k) % 3)

            def moe(f):
                def xt_high(t, v):
                    act.wait_ge(xt_psum[f], t + 1)
                    nc.scalar.copy(xTh[:, v, :, :].rearrange("p c n -> p (c n)"), bank[0][:, 0:D]).then_inc(xth_sb[f], 1)

                def it_high(t):
                    act.wait_ge(it_psum[f], t + 1)
                    nc.scalar.copy(interTh[:, :, :].rearrange("p c n -> p (c n)"), bank[6][:, :]).then_inc(ith_sb[f], 1)

                def step(i, k):
                    t = i * 3 + k
                    if is_first(i, k):
                        xt_high(0, 0)
                    else:
                        e = act.value_load(split_tab[0:1, bass.ds(t, 1)], min_val=0, max_val=E - 1)
                        it_high(t - 1)
                        with act.If(e > 0):
                            act.wait_ge(w_in[f], e * 48 + 48)
                            split_high(f, e, 0)
                    act.wait_ge(h0_psum[f], t + 1)
                    nc.scalar.activation(gated, bank[4][:, :], ACT.Silu).then_inc(silu_ready[f], 1)
                    if not is_last(i, k):
                        xt_high(t + 1, (k + 1) % 3)
                    if not is_first(i, k):
                        with act.If(e > 0):
                            split_high(f, e, 1)
                            act.wait_ge(y_psum[f], t)
                            split_high(f, e, 2)

                for e in range(0 if f == 0 else 2):
                    act.wait_ge(w_in[f], 48 * 2)
                    for piece in range(3):
                        split_high(f, e, piece)
                act.wait_ge(tables_ready[f], 2)
                expert_steps(act, step)
                it_high(TILES - 1)

            moe(0)

            xt_out(1, 0, xnT, proj_psum)
            for g in range(NG):
                act.wait_ge(proj_psum, g + 1)
                act.wait_ge(keys_ready, g)
                nc.scalar.copy(proj[:, 0:2, :].rearrange("p t n -> p (t n)"), bank[2][:, 0:6 * HD]).then_inc(proj_sb, 1)
                if g + 1 < NG:
                    xt_out(1, g + 1, xnT, proj_psum)
                act.wait_ge(kT_psum, g + 1)
                nc.scalar.copy(kEh[:, g, :], bank[4][:, :]).then_inc(k_high, 1)
                nc.scalar.copy(kOh[:, g, :], bank[5][:, :]).then_inc(k_high, 1)
                nc.scalar.copy(cq[:, g, :], bank[6][:, :]).then_inc(k_high, 1)

            def exp(s, k, par, first):
                act.wait_ge(max_ready, s + 1)
                if not first:
                    act.wait_ge(pT_psum, s - 1)
                nc.scalar.activation(prob[k % 2], bank[k % 4][:, :], ACT.Exp,
                                     bias=negmax[:, k % 8:k % 8 + 1],
                                     accum_out=psum[par][:, k % 8:k % 8 + 1]).then_inc(exp_ready, 1)

            def high_probs(p, k, first):
                act.wait_ge(pT_psum, p * 8 + k + 1)
                if k % 2 == 0 and not (first and k < 4):
                    act.wait_ge(o_psum, p * 4 + k // 2 - 1)
                nc.scalar.copy(pTh[k // 2 % 2][:, :, (k % 2) * P:(k % 2 + 1) * P],
                               bank[4 + k % 2][:, :].rearrange("p (c n) -> p c n", c=GT)).then_inc(pT_high, 1)

            def queries_latent(p, par, hh):
                act.wait_ge(qz_psum, p + 1)
                rows_ = (slice(HD, P), slice(0, HD))[hh]
                nc.scalar.copy(qh[par][hh][rows_], bank[7][rows_, :]).then_inc(qz_high, 1)

            def queries_rope(p, par, hh):
                act.wait_ge(rope_ready, p + 1)
                rows_ = (slice(0, HD), slice(HD, P))[hh]
                nc.scalar.copy(qh[par][hh][rows_], rope[rows_]).then_inc(rope_high, 1)

            def take_output(p, par, hh):
                rows_ = slice(hh * HD, (hh + 1) * HD)
                act.wait_ge(o_psum, p * 4 + hh * 2 + 2)
                if hh == 0 and not among(p, 0, 1):
                    act.wait_ge(att_ready, p - 1)
                nc.scalar.copy(raw[par][rows_], bank[6][rows_, :]).then_inc(raw_sb, 1)

            def take_inverse(p):
                act.wait_ge(invT_psum, p + 1)
                act.wait_ge(inv_stored, p * 16)
                nc.scalar.copy(invT, bank[7][0:8, 0:P]).then_inc(invT_sb, 1)

            def pair(p, par):
                first, last = among(p, 0), among(p, NPAIR - 1)
                for k in range(8):
                    s = p * 8 + k
                    if k == 2 and not first:
                        take_output(p - 1, 1 - par, 1)
                    if k == 6:
                        take_output(p, par, 0)
                    if not (last and k == 7):
                        exp(s + 1, k + 1, par if k < 7 else 1 - par, first and k < 1)
                    high_probs(p, k, first)
                    if k in ((3, 4) if first else (2, 3)) and not last:
                        queries_latent(p + 1, 1 - par, k - (3 if first else 2))
                    if k in (3, 4) and not last:
                        queries_rope(p + 1, 1 - par, k - 3)
                    if k == 5 and not first:
                        take_inverse(p - 1)

            for hh in range(2):
                queries_latent(0, 0, hh)
            for hh in range(2):
                queries_rope(0, 0, hh)
            exp(0, 0, 0, True)
            head_pairs(act, pair)
            take_output(NPAIR - 1, 1, 1)
            take_inverse(NPAIR - 1)

            for g in range(NG):
                copy_rows(1, g)
                xt_out(2, g, xTr[1], logits_psum[1])
                choice_exp(1, g)
            moe(1)

        @block.vector
        def _(dve):
            own = Steps(dve, own_v)
            V = nc.vector

            def ln_stats(x, at, tiles, signal):
                for j in range(tiles):
                    own.step(V.bn_stats(stats[:, j, :], x[:, j, :]))
                own.settle()
                for j in range(tiles):
                    own.step(V.bn_aggr(mv[:, bass.ds(at + j, 1), :].rearrange("p a b -> p (a b)"), stats[:, j, :]))
                own.settle()
                ins = V.tensor_scalar(veps[:, bass.ds(at, tiles)],
                                      mv[:, bass.ds(at, tiles), 1:2].rearrange("p a b -> p (a b)"),
                                      LN_EPS, None, ALU.add)
                if signal is None:
                    own.step(ins)
                else:
                    ins.then_inc(signal, 1)

            def ln_rows(n, x, at, g, u):
                for j in range(GT):
                    ins = V.tensor_scalar(rows[u][:, j, 0, 0:D], x[:, j, :],
                                          mv[:, bass.ds(at + j, 1), 0:1].rearrange("p a b -> p (a b)"),
                                          rstd[:, bass.ds(at + j, 1)], ALU.subtract, ALU.mult)
                ins.then_inc(xn_ready[n], 1)

            def norm_rows(f, g, x):
                dve.wait_ge(scattered[f][g % 3], g // 3 * (16 * GT * TOPK))
                ln_rows(2 * f, x, g * GT if f == 0 else 0, g, g % 3)

            def xt_out(n, g, dst):
                dve.wait_ge(xn_psum[n], g * 2 + 2)
                V.tensor_copy(dst[:, 1, :], bank[1][:, :]).then_inc(xn_sb1[n], 1)

            def choose(f, g):
                u = g % 3
                dve.wait_ge(slots_ready[f], g)
                dve.wait_ge(logits_psum[f], g + 1)
                own.step(V.tensor_copy(logit.rearrange("p t e -> p (t e)"), bank[2][:, 0:GT * E]))
                own.settle()
                for j in range(GT):
                    own.step(V.max(top[:, j, :], logit[:, j, :]))
                own.settle()
                for j in range(GT):
                    own.step(V.max_index(topi[:, j, :], top[:, j, :], logit[:, j, :]))
                own.settle()
                own.step(V.tensor_copy(topf, topi[:, :, 0:TOPK]))
                V.tensor_tensor(diff.unsqueeze(2), top[:, :, 1:2], top[:, :, 0:1], ALU.subtract).then_inc(diff_ready[f], 1)
                own.settle()
                iota_b = iota_e.unsqueeze(1).to_broadcast([P, GT, E])
                own.step(V.tensor_tensor(hot1, iota_b, topf[:, :, 0:1].to_broadcast([P, GT, E]), ALU.is_equal))
                own.step(V.tensor_tensor(hot2, iota_b, topf[:, :, 1:2].to_broadcast([P, GT, E]), ALU.is_equal))
                own.settle()
                V.tensor_tensor(mask, hot1, hot2, ALU.add).then_inc(mask_ready[f], 1)
                dve.wait_ge(e2_ready[f], g + 1)
                own.step(V.tensor_scalar(den, e2, 1.0, None, ALU.add))
                own.settle()
                own.step(V.reciprocal(rden, den))
                own.settle()
                V.tensor_scalar(rows[u][:, :, 0, D:D + 1], rden.unsqueeze(2), 0.5, None, ALU.mult)
                V.scalar_tensor_tensor(rows[u][:, :, 1, D:D + 1], e2.unsqueeze(2), 0.5, rden.unsqueeze(2),
                                       ALU.mult, ALU.mult)
                for k in range(TOPK):
                    own.step(V.tensor_copy(rows[u][:, :, k, D + 1:ROW].bitcast(I32),
                                           ids[:, bass.ds(g * GT, GT)].unsqueeze(2)))

            def find_slots(f, g):
                u = g % 3
                dve.wait_ge(ranks_psum[f], g + 1)
                own.step(V.tensor_reduce(msum, mask.rearrange("p t e -> p e t"), AX.X, ALU.add))
                own.step(V.tensor_tensor(place, bank[3][:, 0:GT * E].rearrange("p (t e) -> p t e", e=E),
                                         region_at.unsqueeze(1).to_broadcast([P, GT, E]), ALU.add))
                own.settle()
                V.tensor_tensor(carry, carry, msum, ALU.add).then_inc(carry_ready[f], 1)
                own.step(V.tensor_tensor(pl1, place, hot1, ALU.mult))
                own.step(V.tensor_tensor(pl2, place, hot2, ALU.mult))
                own.settle()
                own.step(V.tensor_reduce(slotf[:, 0, :], pl1, AX.X, ALU.add))
                own.step(V.tensor_reduce(slotf[:, 1, :], pl2, AX.X, ALU.add))
                own.settle()
                V.tensor_copy(slot[u], slotf).then_inc(slots_ready[f], 1)

            def tables(f):
                dve.wait_ge(counts_psum[f], 1)
                own.step(V.tensor_copy(cnt, bank[3][:, 0:E]))
                own.settle()
                V.tensor_copy(cnt_i, cnt).then_inc(tables_ready[f], 1)
                own.step(V.tensor_tensor(over, cnt.unsqueeze(2).to_broadcast([P, E, NT]),
                                         cst[:, C_STEP:C_STEP + NT].unsqueeze(1).to_broadcast([P, E, NT]), ALU.is_gt))
                own.settle()
                own.step(V.tensor_reduce(ntile, over, AX.X, ALU.add))
                own.settle()
                own.step(V.tensor_scalar(ntile, ntile, 1.0, None, ALU.max))
                own.settle()
                own.step(V.tensor_tensor_scan(tend, ntile, zero8, 0.0, ALU.add, ALU.add))
                own.settle()
                own.step(V.tensor_tensor(ge_tab, cst[:, C_J:C_J + TILES].unsqueeze(2).to_broadcast([P, TILES, E]),
                                         tend.unsqueeze(1).to_broadcast([P, TILES, E]), ALU.is_ge))
                own.settle()
                own.step(V.tensor_reduce(texp, ge_tab, AX.X, ALU.add))
                own.settle()
                own.step(V.tensor_tensor(ge_tab, ge_tab, ntile.unsqueeze(1).to_broadcast([P, TILES, E]), ALU.mult))
                own.settle()
                own.step(V.tensor_reduce(tfirst, ge_tab, AX.X, ALU.add))
                own.settle()
                own.step(V.tensor_tensor(tfirst, cst[:, C_J:C_J + TILES], tfirst, ALU.subtract))
                own.step(V.tensor_scalar(trow, texp, float(REGION), None, ALU.mult))
                own.settle()
                own.step(V.scalar_tensor_tensor(trow, tfirst, float(P), trow, ALU.mult, ALU.add))
                own.step(V.tensor_scalar(texp, texp, float(E - 1), None, ALU.min))
                own.settle()
                own.step(V.tensor_copy(row_tab, trow))
                own.step(V.tensor_copy(exp_tab, texp))
                own.step(V.memset(fresh[:, 0:1], 0.0))
                own.step(V.tensor_tensor(fresh[:, 1:TILES], texp[:, 1:TILES], texp[:, 0:TILES - 1], ALU.subtract))
                for ahead, tab in ((1, split_tab), (2, load_tab)):
                    own.settle()
                    own.step(V.tensor_scalar(event, texp, float(E - 1 - ahead), None, ALU.is_le))
                    own.settle()
                    own.step(V.tensor_tensor(event, event, fresh, ALU.mult))
                    own.step(V.tensor_scalar(trow, texp, 1.0, None, ALU.add))
                    own.settle()
                    ins = V.tensor_tensor(tab, trow, event, ALU.mult)
                    if ahead == 1:
                        own.step(ins)
                    else:
                        ins.then_inc(tables_ready[f], 1)

            def split_low(f, e, piece):
                par = e % 2
                dve.wait_ge(whi_ready[f], e * 3 + piece + 1)
                V.tensor_tensor(wlo[:, bass.ds(par * WEXP + piece * WPIECE, WPIECE)],
                                wraw[:, bass.ds(par, 1), piece * WPIECE:(piece + 1) * WPIECE].rearrange("p a n -> p (a n)"),
                                whi[:, bass.ds(par * WEXP + piece * WPIECE, WPIECE)].bitcast(F32),
                                ALU.subtract).then_inc(wlo_ready[f], 1)

            def moe(f):
                def xt_low(t, v):
                    dve.wait_ge(xth_sb[f], t + 1)
                    V.tensor_tensor(xTl[:, v, :, :].rearrange("p c n -> p (c n)"), bank[0][:, 0:D],
                                    xTh[:, v, :, :].rearrange("p c n -> p (c n)").bitcast(F32), ALU.subtract).then_inc(xt_sb[f], 1)

                def it_low(t):
                    dve.wait_ge(ith_sb[f], t + 1)
                    V.tensor_tensor(interTl[:, :, :].rearrange("p c n -> p (c n)"), bank[6][:, :],
                                    interTh[:, :, :].rearrange("p c n -> p (c n)").bitcast(F32), ALU.subtract).then_inc(it_sb[f], 1)

                def multiply(t):
                    dve.wait_ge(h1_psum[f], t + 1)
                    dve.wait_ge(silu_ready[f], t + 1)
                    V.tensor_tensor(inter, gated, bank[5][:, :], ALU.mult).then_inc(inter_ready[f], 1)

                def keep_tag(t, i, k):
                    dve.wait_ge(added[f][k % 3], (i + k // 3) * 16)
                    V.tensor_copy(tag[k % 3].bitcast(I32), xslot[k % 3][:, D:ROW].bitcast(I32)).then_inc(tag_sb[f], 1)

                def scale(t, v):
                    dve.wait_ge(y_psum[f], t + 1)
                    dve.wait_ge(tag_sb[f], t + 1)
                    V.tensor_scalar(ysb[v], bank[7][:, 0:D], tag[v][:, 0:1], None, ALU.mult).then_inc(y_sb[f], 1)

                def step(i, k):
                    t = i * 3 + k
                    if is_first(i, k):
                        xt_low(0, 0)
                    else:
                        e = dve.value_load(split_tab[0:1, bass.ds(t, 1)], min_val=0, max_val=E - 1)
                        it_low(t - 1)
                    if not is_last(i, k):
                        xt_low(t + 1, (k + 1) % 3)
                    if not is_first(i, k):
                        with dve.If(e > 0):
                            split_low(f, e, 0)
                    multiply(t)
                    keep_tag(t, i, k)
                    if not is_first(i, k):
                        scale(t - 1, (k - 1) % 3)
                        with dve.If(e > 0):
                            split_low(f, e, 1)
                            split_low(f, e, 2)

                for e in range(2):
                    for piece in range(3):
                        split_low(f, e, piece)
                dve.wait_ge(tables_ready[f], 2)
                expert_steps(dve, step)
                it_low(TILES - 1)
                scale(TILES - 1, (TILES - 1) % 3)

            own.step(V.memset(carry, 0.0))
            own.step(V.memset(zero8, 0.0))
            dve.wait_ge(const_in, 48)
            def first_stats(g):
                dve.wait_ge(x_in_sem[g], 16)
                ln_stats(xall[:, g * GT:(g + 1) * GT, :], g * GT, GT, veps_ready[0])

            def norm_first(g):
                dve.wait_ge(rstd_ready[0], g + 1)
                norm_rows(0, g, xall[:, g * GT:(g + 1) * GT, :])

            first_stats(0)
            first_stats(1)
            norm_first(0)
            first_stats(2)
            xt_out(0, 0, xTr[0])
            for g in range(NG):
                if g + 1 < NG:
                    norm_first(g + 1)
                if g == 0:
                    first_stats(3)
                choose(0, g)
                if g + 1 < NG:
                    xt_out(0, g + 1, xTr[0])
                find_slots(0, g)
            tables(0)
            dve.wait_ge(scattered[0][2], 16 * GT * TOPK)
            dve.wait_ge(scaled_w, 2)
            q_rope_w = stage_q.rearrange("p (a h n) -> p a h n", a=PAIRS, h=2)
            for two in range(2):
                src = q_rope_w[:, :, :, HD + two:2 * HD:2]
                for hh in range(2):
                    at = hh * HD
                    V.tensor_copy(wpair[:, :, 0, at + two * HALF:at + (two + 1) * HALF], src[:, :, hh, :])
                    last = V.tensor_scalar(wpair[:, :, 1, at + (1 - two) * HALF:at + (2 - two) * HALF], src[:, :, hh, :],
                                           -1.0 if two else 1.0, None, ALU.mult)
            last.then_inc(wa_ready, 1)
            moe(0)

            def norm_batch(g):
                dve.wait_ge(x_in_sem[g % 2], (g // 2 + 2) * 16)
                dve.wait_ge(xn_ready[1], g)
                ln_stats(xgroup[g % 2], 0, GT, veps_ready[1])
                dve.wait_ge(rstd_ready[1], g + 1)
                ln_rows(1, xgroup[g % 2], 0, g, g % 2)

            def squares(g):
                dve.wait_ge(proj_psum, g + 1)
                own.step(V.tensor_copy(proj[:, 2:4, :].rearrange("p t n -> p (t n)"), bank[3][:, 0:6 * HD]))
                own.settle()
                dve.wait_ge(proj_sb, g + 1)
                own.step(V.tensor_tensor(psq, proj, proj, ALU.mult))
                own.settle()
                own.step(V.tensor_reduce(ssq, psq.rearrange("p t (a n) -> p t a n", a=3), AX.X, ALU.add))
                own.settle()
                V.tensor_scalar(rvar, ssq, 1.0 / HD, RMS_EPS, ALU.mult, ALU.add).then_inc(var2_ready, 1)

            def make_keys(g):
                x1, x2 = proj[:, :, HD:2 * HD:2], proj[:, :, HD + 1:2 * HD:2]
                own.step(V.tensor_tensor(rt[0], x1, kcos, ALU.mult))
                own.step(V.tensor_tensor(rt[1], x2, ksin, ALU.mult))
                own.step(V.tensor_tensor(rt[2], x2, kcos, ALU.mult))
                own.step(V.tensor_tensor(rt[3], x1, ksin, ALU.mult))
                own.settle()
                dve.wait_ge(v_split, g * 2 + 1)
                for at in (0, 2 * HD):
                    own.step(V.tensor_tensor(keys[:, :, at:at + HALF], rt[0], rt[1], ALU.subtract))
                    own.step(V.tensor_tensor(keys[:, :, at + HALF:at + HD], rt[2], rt[3], ALU.add))
                dve.wait_ge(rms_ready, g + 1)
                r_kv = rrms[:, :, 0:1].to_broadcast([P, GT, HD])
                for k in range(2):
                    own.step(V.tensor_tensor(cqn[:, :, k * HD:(k + 1) * HD], proj[:, :, 2 * HD:3 * HD],
                                             rrms[:, :, 2:3].to_broadcast([P, GT, HD]), ALU.mult))
                V.tensor_tensor(keys[:, :, HD:2 * HD], proj[:, :, 0:HD], r_kv, ALU.mult).then_inc(keys_ready, 1)

            def lower_keys(g):
                for high, low, b in ((kEh, kEl, 4), (kOh, kOl, 5)):
                    dve.wait_ge(k_high, g * 3 + b - 3)
                    V.tensor_tensor(low[:, g, :], bank[b][:, :], high[:, g, :].bitcast(F32), ALU.subtract)
                dve.wait_ge(k_high, g * 3 + 3)
                V.tensor_tensor(cq[HD:P, g, :], bank[6][HD:P, :], cq[HD:P, g, :].bitcast(F32),
                                ALU.subtract).then_inc(k_low, 1)

            norm_batch(0)
            xt_out(1, 0, xnT)
            norm_batch(1)
            for g in range(NG):
                squares(g)
                if g + 1 < NG:
                    xt_out(1, g + 1, xnT)
                make_keys(g)
                if g + 2 < NG:
                    norm_batch(g + 2)
                lower_keys(g)

            def row_max(s, k):
                dve.wait_ge(s_psum, s + 1)
                V.tensor_reduce(negmax[:, k % 8:k % 8 + 1], bank[k % 4][:, :], AX.X, ALU.max, negate=True).then_inc(max_ready, 1)

            def ropes(p, which):
                if which == 0:
                    dve.wait_ge(qa_psum, p + 1)
                    if not among(p, 0):
                        dve.wait_ge(rope_ready, p)
                    V.tensor_tensor(ropeA, bank[7][:, :], qcos, ALU.mult).then_inc(ropeA_sb, 1)
                else:
                    dve.wait_ge(qb_psum, p + 1)
                    V.tensor_tensor(ropeB, bank[7][:, :], qsin, ALU.mult).then_inc(ropeB_sb, 1)

            def latent_lower(p, par, hh):
                rows_ = (slice(HD, P), slice(0, HD))[hh]
                dve.wait_ge(qz_high, p * 2 + 1 + hh)
                V.tensor_tensor(ql[par][hh][rows_], bank[7][rows_, :], qh[par][hh][rows_].bitcast(F32),
                                ALU.subtract).then_inc(qz_low, 1)

            def take_output(p, par, hh):
                rows_, low_rows = slice(hh * HD, (hh + 1) * HD), slice((1 - hh) * HD, (2 - hh) * HD)
                dve.wait_ge(o_psum, p * 4 + hh * 2 + 2)
                if hh == 0 and not among(p, 0, 1):
                    dve.wait_ge(att_ready, p - 1)
                V.tensor_copy(rawl[par][rows_], bank[6][low_rows, :]).then_inc(rawl_sb, 1)

            def low_probs(p, k):
                dve.wait_ge(pT_high, p * 8 + k + 1)
                at = slice((k % 2) * P, (k % 2 + 1) * P)
                V.tensor_tensor(pTl[k // 2 % 2][:, :, at], bank[4 + k % 2][:, :].rearrange("p (c n) -> p c n", c=GT),
                                pTh[k // 2 % 2][:, :, at].bitcast(F32), ALU.subtract).then_inc(pT_low, 1)

            def invert_sums(p, par):
                dve.wait_ge(exp_ready, p * 8 + 8)
                V.reciprocal(pinv[par], psum[par]).then_inc(pinv_ready, 1)

            def pair(p, par):
                first, last = among(p, 0), among(p, NPAIR - 1)
                for k in range(8):
                    if k == 2 and not first:
                        take_output(p - 1, 1 - par, 1)
                    if k == 6:
                        take_output(p, par, 0)
                    if k == 7 and not among(p, NPAIR - 2, NPAIR - 1):
                        ropes(p + 2, 0)
                    if k in ((1, 2) if first else (1,)) and not last:
                        ropes(p + 1, k - 1 if first else 1)
                    if k in (3, 4) and not last and not first:
                        latent_lower(p + 1, 1 - par, k - 3)
                    if k == 4 and not first:
                        invert_sums(p - 1, 1 - par)
                    if not (last and k >= 6):
                        row_max(p * 8 + k + 2, k + 2)
                    low_probs(p, k)
                    if k in (3, 4) and first:
                        latent_lower(p + 1, 1 - par, k - 3)

            ropes(0, 0)
            ropes(0, 1)
            dve.wait_ge(v_split, B * 2 + 1)
            latent_lower(0, 0, 0)
            latent_lower(0, 0, 1)
            row_max(0, 0)
            row_max(1, 1)
            head_pairs(dve, pair)
            invert_sums(NPAIR - 1, 1)
            take_output(NPAIR - 1, 1, 1)

            own.step(V.memset(carry, 0.0))
            own.settle()
            def second_route(g, part):
                if g >= 0:
                    if part == 0:
                        xt_out(2, g, xTr[1])
                    elif part == 1:
                        choose(1, g)
                    elif part == 2:
                        find_slots(1, g)

            for g in range(NG):
                x = x2group[g % 2]
                dve.wait_ge(x_in_sem[g % 2], (g // 2 + 4) * 16)
                for j in range(GT):
                    t = g * GT + j
                    dve.wait_ge(wo_psum, t + 1)
                    V.tensor_tensor(x[:, j, :], x[:, j, :], bank[5 + j % 2][:, 0:D], ALU.add).then_inc(x2_ready, 1)
                    second_route(g - 1, j)
                dve.wait_ge(x2_ready, g * GT + GT)
                dve.wait_ge(xn_ready[2], g)
                ln_stats(x, 0, GT, veps_ready[2])
                dve.wait_ge(rstd_ready[2], g + 1)
                norm_rows(1, g, x)
            for part in range(3):
                second_route(NG - 1, part)
            tables(1)
            moe(1)

        @block.tensor
        def _(pe):
            mm, tr = nc.tensor.matmul, nc.tensor.transpose

            def xn_transpose(n, g):
                pe.wait_ge(xn_ready[n], g + 1)
                for c, freed in ((0, xn_sb0[n]), (1, xn_sb1[n])):
                    pe.wait_ge(freed, g)
                    for j in range(GT):
                        last = tr(bank[c][:, j * P:(j + 1) * P], rows[g % (2 if n == 1 else 3)][:, j, 0, c * P:(c + 1) * P], ident)
                    last.then_inc(xn_psum[n], 1)

            def logits(f, g):
                pe.wait_ge(xn_sb0[2 * f], g + 1)
                pe.wait_ge(xn_sb1[2 * f], g + 1)
                for j in range(GT):
                    for c in range(KC):
                        last = mm(bank[2][:, j * E:(j + 1) * E], xTr[f][:, c, j * P:(j + 1) * P], gate_sb[:, c, :],
                                  start=(c == 0), stop=(c == KC - 1))
                last.then_inc(logits_psum[f], 1)

            def ranks(f, g):
                pe.wait_ge(mask_ready[f], g + 1)
                pe.wait_ge(carry_ready[f], g)
                mask2 = mask.rearrange("p t e -> p (t e)")
                mm(bank[3][:, 0:GT * E], upper, mask2, start=True, stop=False)
                for j in range(GT - 1):
                    mm(bank[3][:, (j + 1) * E:GT * E].rearrange("p (t e) -> p t e", e=E), ones,
                       mask[:, j:j + 1, :].to_broadcast([P, GT - 1 - j, E]), start=False, stop=False)
                mm(bank[3][:, 0:GT * E].rearrange("p (t e) -> p t e", e=E), ones,
                   carry.unsqueeze(1).to_broadcast([P, GT, E]), start=False, stop=True).then_inc(ranks_psum[f], 1)

            def counts(f):
                pe.wait_ge(carry_ready[f], NG)
                mm(bank[3][:, 0:E], ones, carry, start=True, stop=True).then_inc(counts_psum[f], 1)

            def moe(f):
                def xt(i, k):
                    t, v = i * 3 + k, k % 3
                    pe.wait_ge(slots_in[f][v], (i + k // 3 + 1) * 16)
                    pe.wait_ge(xt_sb[f], t)
                    for c in range(KC):
                        last = tr(bank[0][:, c * P:(c + 1) * P], xslot[v][:, c * P:(c + 1) * P], ident)
                    last.then_inc(xt_psum[f], 1)

                def product(b, xh, xl, at, first, last):
                    n = b.shape[1]
                    mm(b, xh, whi[:, bass.ds(at, n)], start=first, stop=False)
                    mm(b, xh, wlo[:, bass.ds(at, n)], start=False, stop=False)
                    return mm(b, xl, whi[:, bass.ds(at, n)], start=False, stop=last)

                def hidden(t, v, at, part):
                    b, signal = ((bank[4], h0_psum), (bank[5], h1_psum))[part]
                    if part == 0:
                        pe.wait_ge(xt_sb[f], t + 1)
                        pe.wait_ge(silu_ready[f], t)
                    else:
                        pe.wait_ge(inter_ready[f], t)
                    for c in range(KC):
                        last = product(b[:, :], xTh[:, v, c, :], xTl[:, v, c, :], at + (part * KC + c) * MLP,
                                       c == 0, c == KC - 1)
                    last.then_inc(signal[f], 1)

                def inner_transpose(t):
                    pe.wait_ge(inter_ready[f], t + 1)
                    pe.wait_ge(it_sb[f], t)
                    for c in range(MC):
                        last = tr(bank[6][:, c * P:(c + 1) * P], inter[:, c * P:(c + 1) * P], ident)
                    last.then_inc(it_psum[f], 1)

                def outer(t, at):
                    pe.wait_ge(it_sb[f], t + 1)
                    pe.wait_ge(y_sb[f], t)
                    for c in range(MC):
                        last = product(bank[7][:, 0:D], interTh[:, c, :], interTl[:, c, :],
                                       at + 2 * KC * MLP + c * D, c == 0, c == MC - 1)
                    last.then_inc(y_psum[f], 1)

                def expert_of(t):
                    return pe.value_load(exp_tab[0:1, bass.ds(t, 1)], min_val=0, max_val=E - 1)

                def step(i, k):
                    t = i * 3 + k
                    e = expert_of(t)
                    at = pe.snap((e % 2) * WEXP)
                    if not is_first(i, k):
                        before = pe.snap((expert_of(t - 1) % 2) * WEXP)
                        inner_transpose(t - 1)
                    pe.wait_ge(wlo_ready[f], e * 3 + 3)
                    hidden(t, k % 3, at, 0)
                    if not is_last(i, k):
                        xt(i, k + 1)
                    hidden(t, k % 3, at, 1)
                    if not is_first(i, k):
                        outer(t - 1, before)

                pe.wait_ge(tables_ready[f], 2)
                xt(0, 0)
                expert_steps(pe, step)
                inner_transpose(TILES - 1)
                outer(TILES - 1, pe.snap((expert_of(TILES - 1) % 2) * WEXP))

            wq_h = stage_q[0:HD].rearrange("p (h n) -> p h n", h=NH)
            wkv_h = stage_kv.rearrange("p (h n) -> p h n", h=NH)

            def fold_transpose(k, b, src, at):
                pe.wait_ge(scaled_w, 2 if k == 2 else 1)
                pe.wait_ge(wt_sb, 2 if k == 2 else 0)
                for h in range(NH):
                    last = tr(bank[b + h // 8][0:HD, (h % 8) * HD:(h % 8 + 1) * HD], src[:, h, at:at + HD], ident[0:HD, 0:HD])
                    if h % 8 == 7:
                        last.then_inc(fold_psum, 1)

            pe.wait_ge(const_in, 48)
            xn_transpose(0, 0)
            for g in range(NG):
                logits(0, g)
                if g + 1 < NG:
                    xn_transpose(0, g + 1)
                ranks(0, g)
                if g == 1:
                    fold_transpose(0, 6, wkv_h, 0)
                elif g == 2:
                    fold_transpose(1, 4, wkv_h, HD)
            counts(0)
            fold_transpose(2, 6, wq_h, 0)

            pe.wait_ge(wt_sb, 6)
            for h in range(NH):
                for k in range(2):
                    last = mm(bank[6 + h // 8][k * HD:(k + 1) * HD, (h % 8) * HD:(h % 8 + 1) * HD], qnT[:, h, :], knT[:, h, :],
                              start=True, stop=True)
                if h % 8 == 7:
                    last.then_inc(fold_psum, 1)
            pe.wait_ge(tables_ready[0], 1)
            for h in range(NH):
                a = h // 2
                last = mm(bank[a // 2][(h % 2) * HD:(h % 2 + 1) * HD, (a % 2) * D:(a % 2 + 1) * D], vT[:, h, :], stage_o[:, h, :],
                          start=True, stop=True)
                if h % 4 == 3:
                    last.then_inc(fold_psum, 1)
            pe.wait_ge(folded_w, 6)
            pe.wait_ge(wa_ready, 1)

            moe(0)

            def project(g):
                pe.wait_ge(xn_sb0[1], g + 1)
                pe.wait_ge(xn_sb1[1], g + 1)
                pe.wait_ge(proj_sb, g)
                for j in range(GT):
                    for c in range(KC):
                        last = mm(bank[2 + j // 2][:, (j % 2) * 3 * HD:(j % 2 + 1) * 3 * HD],
                                  xnT[:, c, j * P:(j + 1) * P], wproj[:, c, :], start=(c == 0), stop=(c == KC - 1))
                last.then_inc(proj_psum, 1)

            def transpose_keys(g):
                pe.wait_ge(keys_ready, g + 1)
                pe.wait_ge(k_low, g)
                for j in range(GT):
                    tr(bank[4][:, j * P:(j + 1) * P], keys[:, j, 0:P], ident)
                    tr(bank[5][:, j * P:(j + 1) * P], keys[:, j, HD:HD + P], ident)
                    last = tr(bank[6][:, j * P:(j + 1) * P], cqn[:, j, :], ident)
                last.then_inc(kT_psum, 1)

            xn_transpose(1, 0)
            project(0)
            xn_transpose(1, 1)
            for g in range(NG):
                if g + 1 < NG:
                    project(g + 1)
                transpose_keys(g)
                if g + 2 < NG:
                    xn_transpose(1, g + 2)

            def flat(v):
                return v.rearrange("p a n -> p (a n)")

            def queries(p, part):
                src = flat(cq[:, bass.ds(p // PAIRS, 1), :])
                if part == 0:
                    pe.wait_ge(wcur_ready, p + 1)
                    if not among(p, 0):
                        pe.wait_ge(qz_low, p * 2)
                    if not among(p, 0, 1, 2):
                        pe.wait_ge(invT_sb, p - 2)
                else:
                    pe.wait_ge((ropeA_sb, ropeB_sb)[part - 1], p + 1)
                mm(bank[7][:, :], wch[:, part, :], src, start=True, stop=False)
                mm(bank[7][:, :], wcl[:, part, :], src, start=False, stop=True)\
                    .then_inc((qa_psum, qb_psum, qz_psum)[part], 1)

            def scores(p, par, k):
                hh, qt = k // 4, k % 4
                if k == 0:
                    pe.wait_ge(rope_low, p * 2 + 2)
                    pe.wait_ge(qz_low, p * 2 + 2)
                high, low = (flat(t[:, bass.ds(p // PAIRS, 1), :]) for t in ((kEh, kOh)[hh], (kEl, kOl)[hh]))
                q_high, q_low = (t[par][hh][:, qt * P:(qt + 1) * P] for t in (qh, ql))
                mm(bank[k % 4][:, :], q_high, high, start=True, stop=False)
                mm(bank[k % 4][:, :], q_high, low, start=False, stop=False)
                mm(bank[k % 4][:, :], q_low, high, start=False, stop=True).then_inc(s_psum, 1)

            def transposed(p, k, first):
                s = p * 8 + k
                pe.wait_ge(exp_ready, s + 1)
                if not (first and k < 2):
                    pe.wait_ge(pT_low, s - 1)
                for c in range(GT):
                    last = tr(bank[4 + k % 2][:, c * P:(c + 1) * P], prob[k % 2][:, c * P:(c + 1) * P], ident)
                last.then_inc(pT_psum, 1)

            def attend(p, par, half, piece, first=False):
                hh, at = half // 2, slice((half % 2) * 2 * P, (half % 2 + 1) * 2 * P)
                if piece == 0:
                    if half == 0:
                        pe.wait_ge(vcur_ready, p + 1)
                    pe.wait_ge(pT_low, p * 8 + half * 2 + 2)
                    if half % 2 == 0 and not (first and half == 0):
                        pe.wait_ge(raw_sb, p * 2 + hh)
                        pe.wait_ge(rawl_sb, p * 2 + hh)
                cols = slice((1 - hh) * HD, (1 - hh) * HD + P)
                for c in (2 * piece, 2 * piece + 1):
                    mm(bank[6][:, at], vcur[par][:, 0, c, cols], pTh[half % 2][:, c, :], start=(c == 0), stop=False)
                    last = mm(bank[6][:, at], vcur[par][:, 1, c, cols], pTl[half % 2][:, c, :], start=False, stop=(c == GT - 1))
                if piece == 1:
                    last.then_inc(o_psum, 1)

            def inverse_transpose(p, par):
                pe.wait_ge(pinv_ready, p + 1)
                tr(bank[7][0:8, 0:P], pinv[par], ident).then_inc(invT_psum, 1)

            def pair(p, par):
                first, last = among(p, 0), among(p, NPAIR - 1)
                for k in range(8):
                    transposed(p, k, first)
                    if k < 6:
                        scores(p, par, k + 2)
                    elif not last:
                        scores(p + 1, 1 - par, k - 6)
                    if k == 2 and not first and not last:
                        queries(p + 1, 2)
                    if k == 5 and not first:
                        if not last:
                            pe.wait_ge(qz_low, p * 2 + 4)
                        inverse_transpose(p - 1, 1 - par)
                    if k == 6 and not among(p, NPAIR - 2, NPAIR - 1):
                        queries(p + 2, 0)
                    if k > 1:
                        attend(p, par, k // 2 - 1, k % 2, first)
                    elif not first:
                        attend(p - 1, 1 - par, 3, k)
                    if k < 3 and first:
                        queries(1, k)
                    if k == 0 and not first and not last:
                        queries(p + 1, 1)

            pe.wait_ge(k_low, B)
            pe.wait_ge(v_split, 1)
            for part in range(3):
                queries(0, part)
            scores(0, 0, 0)
            scores(0, 0, 1)
            head_pairs(pe, pair)
            pe.wait_ge(invT_sb, NPAIR - 1)
            inverse_transpose(NPAIR - 1, 1)
            for piece in range(2):
                attend(NPAIR - 1, 1, 3, piece)

            def second_route(g, part):
                if g >= 0:
                    if part == 0:
                        xn_transpose(2, g)
                    elif part == 1:
                        logits(1, g)
                    elif part == 2:
                        ranks(1, g)

            for g in range(NG):
                pe.wait_ge(attl_in[g % 2], g // 2 * 16 + 16)
                for j in range(GT):
                    t = g * GT + j
                    if t == 1:
                        pe.wait_ge(raw_sb, 2 * NPAIR)
                        pe.wait_ge(rawl_sb, 2 * NPAIR)
                    pe.wait_ge(x2_ready, max(t - 1, 0))
                    for a in range(PAIRS):
                        last = mm(bank[5 + j % 2][:, 0:D], attl[g % 2][:, a, j * P:(j + 1) * P], wvo[:, a, :],
                                  start=(a == 0), stop=(a == PAIRS - 1))
                    last.then_inc(wo_psum, 1)
                    second_route(g - 1, j)
            for part in range(3):
                second_route(NG - 1, part)
            counts(1)
            moe(1)


_INS = ["L0_attn_hidden_states", "L0_attn_wq_a", "L0_attn_q_a_norm_w", "L0_attn_wq_b", "L0_attn_wkv_a",
        "L0_attn_kv_a_norm_w", "L0_attn_wkv_b", "L0_attn_wo", "L0_ffn_gate_kernel", "L0_ffn_w0_kernel",
        "L0_ffn_w1_kernel", "L0_ffn_wo_kernel"]


def kernel(**inputs):
    import concourse.bacc as bacc
    from concourse.bass_utils import run_bass_kernel_spmd

    nc = bacc.Bacc("TRN2", target_bir_lowering=False, num_devices=1)
    const, ids = constants()
    arrays = {name: np.ascontiguousarray(inputs[name]) for name in _INS}
    arrays["const_tables"], arrays["token_ids_in"] = const, ids
    args = [nc.dram_tensor(n, a.shape, mybir.dt.from_np(a.dtype), kind="ExternalInput").ap() for n, a in arrays.items()]
    out = nc.dram_tensor("out", (B, S, D), F32, kind="ExternalOutput").ap()
    build(nc, *args, out)
    r = run_bass_kernel_spmd(nc, [arrays], core_ids=[0])
    return r.results[0]["out"]
```
